# Optimizing a Trainium2 kernel written in Bass

```python
import numpy as np
import jax
import jax.numpy as jnp

def _softmax(x, axis=-1):
    return jax.nn.softmax(x, axis=axis)

def _gelu(x):
    return jax.nn.gelu(x, approximate=True)

def _silu(x):
    return jax.nn.silu(x)

def _sigmoid(x):
    return jax.nn.sigmoid(x)

def _layernorm(x, axis=-1, eps=1e-05):
    m = jnp.mean(x, axis=axis, keepdims=True)
    v = jnp.var(x, axis=axis, keepdims=True)
    return (x - m) / jnp.sqrt(v + eps)

def _scatter_add(tgt, idx, src, axis=0):
    return tgt.at[idx].add(src)

def _segment_sum(src, seg, n):
    return jax.ops.segment_sum(src, seg, n)
kernel_name = 'mk_adaln_ffn_d2_seqx_r4_18578f'

def setup_inputs(seed: int=0):
    np.random.seed(seed)
    _w = jnp.asarray

    def _rec_inputs():
        import jax
        import jax.numpy as jnp
        _rk = jax.random.key(seed)
        x = -0.000125 + 0.9999 * jax.random.normal(jax.random.fold_in(_rk, 1), (64, 64, 256), jnp.float32)
        _lenS = 64 - jax.random.randint(jax.random.fold_in(_rk, 7), (64,), 0, max(1, 64 // 4) + 1, jnp.int32)
        _lenS2 = 64 - jax.random.randint(jax.random.fold_in(_rk, 8), (64,), 0, max(1, 64 // 4) + 1, jnp.int32)
        cond_1024 = -0.00493535 + 1.00056 * jax.random.normal(jax.random.fold_in(_rk, 11), (64, 256), jnp.float32)
        return (x, cond_1024)
    x, cond_1024 = _rec_inputs()

    def _L0_cond_setup():
        import jax, jax.numpy as jnp
        import numpy as np
        import math
        N, T, D, H = (64, 128, 256, 256)
        key = jax.random.key(seed)
        k1, k2, k3, k4 = jax.random.split(key, 4)
        x = jax.random.normal(k1, (N, T, D), dtype=jnp.float32)
        h0 = jax.random.normal(k2, (N, H), dtype=jnp.float32)
        Wx = jax.random.normal(k3, (D, 4 * H), dtype=jnp.float32) / math.sqrt(D)
        Wh = jax.random.normal(k4, (H, 4 * H), dtype=jnp.float32) / math.sqrt(H)
        b = jnp.zeros((4 * H,), dtype=jnp.float32)
        return {'x': x, 'h0': h0, 'Wx': Wx, 'Wh': Wh, 'b': b}
    _L0_cond_all = _L0_cond_setup()
    _L0_cond_in = {k: v for k, v in _L0_cond_all.items() if k in ('Wx', 'Wh', 'b')}
    del _L0_cond_all

    def _L0_ffn_setup():
        import jax, jax.numpy as jnp
        import numpy as np
        BLOCK = 32
        W_BITS = 4
        ACT_BITS = 16

        def act_qdq(x):
            qmax = 2.0 ** (ACT_BITS - 1) - 1.0
            scale = jnp.maximum(jnp.max(jnp.abs(x)) / qmax, 1e-12)
            return jnp.clip(jnp.round(x / scale), -qmax - 1.0, qmax) * scale

        def fixed_qdq_u16(x):
            scale = 1.0 / 65536.0
            return jnp.clip(jnp.round(x / scale), 0.0, 65535.0) * scale

        def lpbq_dequant(w):
            O, I = w.shape
            qmax = 2.0 ** (W_BITS - 1) - 1.0
            wb = w.reshape(O, I // BLOCK, BLOCK)
            s = jnp.maximum(jnp.max(jnp.abs(wb), axis=-1, keepdims=True) / qmax, 1e-12)
            wq = jnp.clip(jnp.round(wb / s), -qmax - 1.0, qmax) * s
            return wq.reshape(O, I)
        key = jax.random.key(seed)
        k1, k2, k3, k4 = jax.random.split(key, 4)
        B, S, H, I = (2, 1024, 256, 768)
        x = jax.random.normal(k1, (B, S, H), jnp.float32)
        w_gate = jax.random.normal(k2, (I, H), jnp.float32) * 0.02
        w_up = jax.random.normal(k3, (I, H), jnp.float32) * 0.02
        w_down = jax.random.normal(k4, (H, I), jnp.float32) * 0.02
        return {'x': x, 'w_gate': w_gate, 'w_up': w_up, 'w_down': w_down}
    _L0_ffn_all = _L0_ffn_setup()
    _L0_ffn_in = {k: v for k, v in _L0_ffn_all.items() if k in ('w_gate', 'w_up', 'w_down')}
    del _L0_ffn_all

    def _L1_cond_setup():
        import jax, jax.numpy as jnp
        import numpy as np
        import math
        N, T, D, H = (64, 128, 256, 256)
        key = jax.random.key(seed)
        k1, k2, k3, k4 = jax.random.split(key, 4)
        x = jax.random.normal(k1, (N, T, D), dtype=jnp.float32)
        h0 = jax.random.normal(k2, (N, H), dtype=jnp.float32)
        Wx = jax.random.normal(k3, (D, H), dtype=jnp.float32) / math.sqrt(D)
        Wh = jax.random.normal(k4, (H, H), dtype=jnp.float32) / math.sqrt(H)
        b = jnp.zeros((H,), dtype=jnp.float32)
        return {'x': x, 'h0': h0, 'Wx': Wx, 'Wh': Wh, 'b': b}
    _L1_cond_all = _L1_cond_setup()
    _L1_cond_in = {k: v for k, v in _L1_cond_all.items() if k in ('Wx', 'Wh', 'b')}
    del _L1_cond_all

    def _L1_ffn_setup():
        import jax, jax.numpy as jnp
        import numpy as np
        D = 256
        H = 512
        E = 8
        TOP_K = 2
        N_SHARED = 1
        B, S = (2, 256)
        key = jax.random.key(seed)
        ks = jax.random.split(key, 12)
        sc = 0.02
        return {'hidden': jax.random.normal(ks[0], (B, S, D), jnp.float32), 'router_w': jax.random.normal(ks[1], (D, E), jnp.float32) * sc, 'router_b': jnp.zeros((E,), jnp.float32), 'sw1': jax.random.normal(ks[2], (D, H), jnp.float32) * sc, 'sb1': jnp.zeros((H,), jnp.float32), 'sw2': jax.random.normal(ks[3], (H, D), jnp.float32) * sc, 'sb2': jnp.zeros((D,), jnp.float32), 'rw1': jax.random.normal(ks[4], (E, D, H), jnp.float32) * sc, 'rb1': jnp.zeros((E, H), jnp.float32), 'rw2': jax.random.normal(ks[5], (E, H, D), jnp.float32) * sc, 'rb2': jnp.zeros((E, D), jnp.float32)}
    _L1_ffn_all = _L1_ffn_setup()
    _L1_ffn_in = {k: v for k, v in _L1_ffn_all.items() if k in ('router_w', 'router_b', 'sw1', 'sb1', 'sw2', 'sb2', 'rw1', 'rb1', 'rw2', 'rb2')}
    del _L1_ffn_all
    return {'x': x, 'cond_1024': cond_1024, 'L0_cond_Wx': _L0_cond_in['Wx'], 'L0_cond_Wh': _L0_cond_in['Wh'], 'L0_cond_b': _L0_cond_in['b'], 'L0_ffn_w_gate': _L0_ffn_in['w_gate'], 'L0_ffn_w_up': _L0_ffn_in['w_up'], 'L0_ffn_w_down': _L0_ffn_in['w_down'], 'L1_cond_Wx': _L1_cond_in['Wx'], 'L1_cond_Wh': _L1_cond_in['Wh'], 'L1_cond_b': _L1_cond_in['b'], 'L1_ffn_router_w': _L1_ffn_in['router_w'], 'L1_ffn_router_b': _L1_ffn_in['router_b'], 'L1_ffn_sw1': _L1_ffn_in['sw1'], 'L1_ffn_sb1': _L1_ffn_in['sb1'], 'L1_ffn_sw2': _L1_ffn_in['sw2'], 'L1_ffn_sb2': _L1_ffn_in['sb2'], 'L1_ffn_rw1': _L1_ffn_in['rw1'], 'L1_ffn_rb1': _L1_ffn_in['rb1'], 'L1_ffn_rw2': _L1_ffn_in['rw2'], 'L1_ffn_rb2': _L1_ffn_in['rb2']}

def reference(x, cond_1024, L0_cond_Wx, L0_cond_Wh, L0_cond_b, L0_ffn_w_gate, L0_ffn_w_up, L0_ffn_w_down, L1_cond_Wx, L1_cond_Wh, L1_cond_b, L1_ffn_router_w, L1_ffn_router_b, L1_ffn_sw1, L1_ffn_sb1, L1_ffn_sw2, L1_ffn_sb2, L1_ffn_rw1, L1_ffn_rb1, L1_ffn_rw2, L1_ffn_rb2):
    import jax
    import jax.numpy as jnp

    def _L0_cond_ref(x, h0, Wx, Wh, b):
        import jax, jax.numpy as jnp
        import numpy as np
        import math
        N, T, D, H = (64, 128, 256, 256)
        Hdim = h0.shape[1]
        xW = jnp.einsum('ntd,dg->ntg', x, Wx) + b

        def step(carry, xw_t):
            prev_h, prev_c = carry
            a = xw_t + prev_h @ Wh
            i = jax.nn.sigmoid(a[:, :Hdim])
            f = jax.nn.sigmoid(a[:, Hdim:2 * Hdim])
            o = jax.nn.sigmoid(a[:, 2 * Hdim:3 * Hdim])
            g = jnp.tanh(a[:, 3 * Hdim:])
            next_c = f * prev_c + i * g
            next_h = o * jnp.tanh(next_c)
            return ((next_h, next_c), next_h)
        c0 = jnp.zeros_like(h0)
        _, hs = jax.lax.scan(step, (h0, c0), jnp.swapaxes(xW, 0, 1))
        return jnp.swapaxes(hs, 0, 1)

    def _L0_ffn_ref(x, w_gate, w_up, w_down):
        import jax, jax.numpy as jnp
        import numpy as np
        BLOCK = 32
        W_BITS = 4
        ACT_BITS = 16

        def act_qdq(x):
            qmax = 2.0 ** (ACT_BITS - 1) - 1.0
            scale = jnp.maximum(jnp.max(jnp.abs(x)) / qmax, 1e-12)
            return jnp.clip(jnp.round(x / scale), -qmax - 1.0, qmax) * scale

        def fixed_qdq_u16(x):
            scale = 1.0 / 65536.0
            return jnp.clip(jnp.round(x / scale), 0.0, 65535.0) * scale

        def lpbq_dequant(w):
            O, I = w.shape
            qmax = 2.0 ** (W_BITS - 1) - 1.0
            wb = w.reshape(O, I // BLOCK, BLOCK)
            s = jnp.maximum(jnp.max(jnp.abs(wb), axis=-1, keepdims=True) / qmax, 1e-12)
            wq = jnp.clip(jnp.round(wb / s), -qmax - 1.0, qmax) * s
            return wq.reshape(O, I)
        x = act_qdq(x)
        up = act_qdq(x @ lpbq_dequant(w_up).T)
        gate = act_qdq(x @ lpbq_dequant(w_gate).T)
        sig = fixed_qdq_u16(jax.nn.sigmoid(gate))
        gate = act_qdq(gate * sig)
        o = act_qdq(gate * up)
        return o @ lpbq_dequant(w_down).T

    def _L1_cond_ref(x, h0, Wx, Wh, b):
        import jax, jax.numpy as jnp
        import numpy as np
        import math
        N, T, D, H = (64, 128, 256, 256)
        xW = jnp.einsum('ntd,dh->nth', x, Wx) + b

        def step(prev_h, xw_t):
            next_h = jnp.tanh(prev_h @ Wh + xw_t)
            return (next_h, next_h)
        _, hs = jax.lax.scan(step, h0, jnp.swapaxes(xW, 0, 1))
        return jnp.swapaxes(hs, 0, 1)

    def _L1_ffn_ref(hidden, router_w, router_b, sw1, sb1, sw2, sb2, rw1, rb1, rw2, rb2):
        import jax, jax.numpy as jnp
        import numpy as np
        D = 256
        H = 512
        E = 8
        TOP_K = 2
        N_SHARED = 1
        B, S = (2, 256)
        b, s, d = hidden.shape
        T = b * s
        flat = hidden.reshape(T, d)
        router_logits = flat @ router_w + router_b
        router_probs = jax.nn.softmax(router_logits, axis=-1)
        topk_probs, topk_idx = jax.lax.top_k(router_probs, TOP_K)
        weights = jnp.zeros_like(router_probs).at[jnp.arange(T)[:, None], topk_idx].add(topk_probs)
        sh = jax.nn.gelu(flat @ sw1 + sb1, approximate=False)
        shared_out = (sh @ sw2 + sb2) / N_SHARED
        h1 = jax.nn.gelu(jnp.einsum('td,edh->teh', flat, rw1) + rb1[None], approximate=False)
        expert_out = jnp.einsum('teh,ehd->ted', h1, rw2) + rb2[None]
        mixed = jnp.einsum('ted,te->td', expert_out, weights)
        return (shared_out + mixed).reshape(b, s, d)
    x = x + _L0_ffn_ref(_L0_cond_ref(x, cond_1024, L0_cond_Wx, L0_cond_Wh, L0_cond_b), L0_ffn_w_gate, L0_ffn_w_up, L0_ffn_w_down)
    x = x + _L1_ffn_ref(_L1_cond_ref(x, cond_1024, L1_cond_Wx, L1_cond_Wh, L1_cond_b), L1_ffn_router_w, L1_ffn_router_b, L1_ffn_sw1, L1_ffn_sb1, L1_ffn_sw2, L1_ffn_sb2, L1_ffn_rw1, L1_ffn_rb1, L1_ffn_rw2, L1_ffn_rb2)
    return x

_drawn_inputs = setup_inputs


def setup_inputs(seed=0):
    import zlib

    import numpy as np

    out = dict(_drawn_inputs(seed))
    spreads = {'L0_cond_b': (0.0, 0.8),
     'L1_cond_b': (0.0, 0.766),
     'L1_ffn_router_b': (0.0, 0.47),
     'L1_ffn_sb1': (0.0, 0.985),
     'L1_ffn_sb2': (0.0, 0.1),
     'L1_ffn_rb1': (0.0, 0.8),
     'L1_ffn_rb2': (0.0, 0.351)}
    factors = {'cond_1024': 7.628,
     'L0_cond_Wx': 8.0,
     'L0_cond_Wh': 8.0,
     'L0_ffn_w_gate': 8.0,
     'L0_ffn_w_up': 8.0,
     'L0_ffn_w_down': 8.0,
     'L1_ffn_rw1': 4.786,
     'L1_ffn_rw2': 4.313}
    for name, (base, spread) in spreads.items():
        noise = np.random.default_rng([zlib.crc32(name.encode()), seed]).standard_normal(out[name].shape)
        drawn = base * np.exp(spread * noise) if base else spread * noise
        out[name] = jnp.asarray(drawn.astype(out[name].dtype))
    for name, factor in factors.items():
        out[name] = (out[name] * factor).astype(out[name].dtype)
    return out
```

```python
from contextlib import ExitStack

import concourse.bass as bass
from concourse import mybir

ALU = mybir.AluOpType
ACT = mybir.ActivationFunctionType
AX = mybir.AxisListType
F32 = mybir.dt.float32
F16 = mybir.dt.float16
I16 = mybir.dt.int16
U16 = mybir.dt.uint16
ds = bass.ds

P = 128
N = 64
T = 64
D = 256
KD = D // P
SC = KD * N
TILES = T // 2
GATES = 4 * D
I0 = 768
IT = I0 // P
H1 = 512
HT = H1 // P
E = 8
SLOTS = E + 1
SUPERS = 8
SUPER_T = T // SUPERS
GROUP = 3
CH = 4
BLOCK = 1024
BLOCKS = CH * IT
WBLK = 32
PIECES = 3 * I0 // P
QMAX = 32767.0
TINY = 1e-12
WS = 256.0
BIAS_SLOTS0 = GATES // P
BIAS_SLOTS1 = D // P
GATE_ORDER = [0, 1, 2, 3, 6, 7, 4, 5]
EARLY_STEPS = 19
RNN_SUPERS = (T - EARLY_STEPS) // SLOTS


def mixed_layers(nc, a, out):
    with ExitStack() as ctx:
        def sb(name, shape, dt):
            return ctx.enter_context(nc.sbuf_tensor(name, shape, dt))

        def sem(name):
            return ctx.enter_context(nc.semaphore(name))

        ps = ctx.enter_context(nc.psum_tensor("ps", [P, 8, 512], F32))

        big = sb("big", [P, BLOCKS * BLOCK], F32)
        big16 = big[:, :].bitcast(F16)
        xn = sb("xn", [P, TILES, D], F32)
        xh = sb("xh", [P, T * SC], F16)
        xl = sb("xl", [P, T * SC], F16)
        xh_v = xh[:, :].rearrange("p (k t n) -> p k t n", k=KD, n=N)
        xl_v = xl[:, :].rearrange("p (k t n) -> p k t n", k=KD, n=N)
        wt_h = sb("wt_h", [P, PIECES, D], F16)
        wt_l = sb("wt_l", [P, PIECES, D], F16)
        rx_h = sb("rx_h", [P, KD * D], F16)
        rx_l = sb("rx_l", [P, KD * D], F16)
        rh_h = sb("rh_h", [P, KD * D], F16)
        rh_l = sb("rh_l", [P, KD * D], F16)
        tmp = sb("tmp", [P, 4096], F32)
        ident = sb("ident", [P, P], F32)
        ones_row = sb("ones_row", [1, P], F32)
        cstate = sb("cstate", [P, 2 * SC], F32)
        r0 = sb("r0", [P, 2, SC], F16)
        sel1 = sb("sel1", [2 * BIAS_SLOTS1, SC], F16)
        braw1 = sb("braw1", [2 * BIAS_SLOTS1, P], F32)
        bhi1 = sb("bhi1", [2 * BIAS_SLOTS1, P], F16)
        brow1 = sb("brow1", [2 * BIAS_SLOTS1, P], F16)
        nlow0 = sb("nlow0", [2 * BIAS_SLOTS0, 1], F32)
        nlow1 = sb("nlow1", [2 * BIAS_SLOTS1, 1], F32)
        wr_raw = sb("wr_raw", [P, KD * E], F32)
        wr_h = sb("wr_h", [P, KD * E], F16)
        wr_l = sb("wr_l", [P, KD * E], F16)
        rb_all = sb("rb_all", [P, E], F32)
        b1_n = sb("b1_n", [SLOTS * HT, P], F32)
        b1_t = sb("b1_t", [P, SLOTS * HT], F32)
        b2_all = sb("b2_all", [SLOTS, D], F32)
        maxes = sb("maxes", [P, 4, 64], F32)
        colmax = sb("colmax", [P, 8], F32)
        top = sb("top", [1, 8], F32)
        sc = sb("sc", [P, 24], F32)
        blk_s = sb("blk_s", [P, 3, 16], F32)
        lg = sb("lg", [P, 4, E], F32)
        zz = sb("zz", [P, 4, E], F32)
        ee = sb("ee", [P, 4, E], F32)
        mrow = sb("mrow", [P, 16], F32)
        before = sb("before", [P, E, E], F32)
        rank = sb("rank", [P, 4, E], F32)
        w9 = sb("w9", [P, 4, SLOTS], F32)
        hr = sb("hr", [P, SC], F32)

        cond_n = tmp[0:N, 0:D]
        sel0 = tmp[0:2 * BIAS_SLOTS0, 256:512].bitcast(F16)
        braw0 = tmp[0:2 * BIAS_SLOTS0, 512:640]
        bhi0 = tmp[0:2 * BIAS_SLOTS0, 640:704].bitcast(F16)
        brow0 = tmp[0:2 * BIAS_SLOTS0, 704:768].bitcast(F16)
        w9t = tmp[0:SLOTS, 3072:3584]
        cmp_a = tmp[:, 3584:3840].rearrange("p (t e j) -> p t e j", e=E, j=E)
        cmp_b = tmp[:, 3840:4096].rearrange("p (t e j) -> p t e j", e=E, j=E)

        def part(start, cols):
            return big[:, start:start + cols]

        wx_h = part(0, 1024).bitcast(F16)
        wx_l = part(1024, 1024).bitcast(F16)
        wh_h = part(2048, 1024).bitcast(F16)
        wh_l = part(3072, 1024).bitcast(F16)
        wn = part(4096, PIECES * D).rearrange("p (q c) -> p q c", c=D)
        wx_raw = part(8704, 2048)
        wh_raw = part(10752, 2048)
        rx_raw = part(12800, 512)
        rh_raw = part(13312, 512)
        tg = part(13824, 512)
        fc = part(14336, SC)
        ig = part(14464, SC)
        tc = part(14592, SC)
        hb = part(14720, 2 * SC).bitcast(F16).rearrange("p (s h c) -> p s h c", s=2, h=2)
        xt = part(14976, 512).bitcast(F16).rearrange("p (s h c) -> p s h c", s=2, h=2)
        wd = part(15488, 512)
        w16 = part(16000, 256).bitcast(I16)
        hs = part(16384, T * SC)

        tmp_i = tmp[:, :].bitcast(I16)
        tmp_u = tmp[:, :].bitcast(U16)
        qb = [tmp_i[:, i * BLOCK:(i + 1) * BLOCK] for i in range(2)]
        sq = [tmp_u[:, (2 + i) * BLOCK:(3 + i) * BLOCK] for i in range(2)]
        xts = [tmp[:, 2048 + 512 * i:2560 + 512 * i] for i in range(2)]
        x2s = [tmp[:, 3072 + 512 * i:3584 + 512 * i] for i in range(2)]
        xs = tmp[:, 1024:2048].rearrange("p (c d) -> p c d", c=4)
        stage = tmp[:, 0:2048].rearrange("p (m c) -> p m c", m=2)
        hf = [tmp[:, 2048 + 512 * i:2560 + 512 * i] for i in range(2)]
        EXP = 4096
        H1_AT = SLOTS * EXP

        def h1(u, part_, ht):
            at = H1_AT + u * 4096 + part_ * 2048 + ht * 512
            return big16[:, at:at + 512]

        block_v = big[:, :].rearrange("p (b c) -> p b c", c=BLOCK)

        d_x0, d_x1, d_cond, d_w0, d_b, d_ffn, d_rnn, d_moe_small, d_out = (
            sem(s) for s in ("d_x0", "d_x1", "d_cond", "d_w0", "d_b", "d_ffn", "d_rnn", "d_moe_small", "d_out"))
        d_stage = [sem("d_stage1"), sem("d_stage2")]
        const_step = sem("const_step")
        cond_t = sem("cond_t")
        prep_v = sem("prep_v")
        h_hi = sem("h_hi")
        h_lo = sem("h_lo")
        ifg_done, o_done = sem("ifg_done"), sem("o_done")
        ifg_tanh, o_tanh, c_tanh = sem("ifg_tanh"), sem("o_tanh"), sem("c_tanh")
        fc_done, ig_done, c_done, hs_done, hmax_done = (
            sem(s) for s in ("fc_done", "ig_done", "c_done", "hs_done", "hmax_done"))
        x_staged, xs_ready = sem("x_staged"), sem("xs_ready")
        x_tr, xt_hi, xt_lo = sem("x_tr"), sem("xt_hi"), sem("xt_lo")
        wq_step = sem("wq_step")
        w_tr, wt_hi_done, wt_lo_done = sem("w_tr"), sem("wt_hi_done"), sem("wt_lo_done")
        m_col, m_row, m_top, m_all, m_step = (sem(s) for s in ("m_col", "m_row", "m_top", "m_all", "m_step"))
        xq_int, xq_hi, xq_lo = sem("xq_int"), sem("xq_hi"), sem("xq_lo")
        pair_done, pair_free_v, pair_free_a = sem("pair_done"), sem("pair_free_v"), sem("pair_free_a")
        gate_max = sem("gate_max")
        gate_q, gate_t, gate_s, gated, gated_max = (
            sem(s) for s in ("gate_q", "gate_t", "gate_s", "gated", "gated_max"))
        up_q, gated_q, prod, prod_max = sem("up_q"), sem("gated_q"), sem("prod"), sem("prod_max")
        o_int, o_hi, o_lo = sem("o_int"), sem("o_hi"), sem("o_lo")
        xt_ps, xt_sb, down, x2_new, x2_hi, x2_lo, x2_tr, x2_tok = (
            sem(s) for s in ("xt_ps", "xt_sb", "down", "x2_new", "x2_hi", "x2_lo", "x2_tr", "x2_tok"))
        e_hi, e_lo = sem("e_hi"), sem("e_lo")
        b1_tr, b1_ready = sem("b1_tr"), sem("b1_ready")
        r_sum, r_tanh, r_hi, r_lo = sem("r_sum"), sem("r_tanh"), sem("r_hi"), sem("r_lo")
        up1, gelu, split_hi, split_lo, down1, added = (
            sem(s) for s in ("up1", "gelu", "split_hi", "split_lo", "down1", "added"))
        route, route_step, route_z, route_e, w9_done, w9_tr, w9t_done = (
            sem(s) for s in ("route", "route_step", "route_z", "route_e", "w9_done", "w9_tr", "w9t_done"))

        CONSTS = 6 + (2 + BIAS_SLOTS0 - 1 + 2) + (2 + BIAS_SLOTS1 - 1 + 2) + 2
        PREP0 = 15
        PREP1 = PREP0 + 6
        ROUTE_STEPS = 11
        (C_SH, C_IH, C_U, C_SG, C_IG, C_SGH, C_SG16, C_S2, C_F2, C_SU, C_ISU, C_FU, C_S3, C_F3, C_OUT,
         C_T1, C_T2, C_T3, C_T4, C_R) = range(20)

        def col(c):
            return sc[:, c:c + 1]

        x_dram, out_dram = a["x"], out
        block = ctx.enter_context(nc.Block())

        @block.sync
        def _(sp):
            sp.dma_start(cond_n[:, :], a["cond_1024"]).then_inc(d_cond, 16)
            first = TILES // 8
            for j0, j1, s in ((0, first, d_x0), (first, TILES, d_x1)):
                for tt in range(2):
                    sp.dma_start(xn[tt * N:(tt + 1) * N, j0:j1, :],
                                 x_dram.rearrange("n (j tt) d -> tt n j d", tt=2)[tt, :, j0:j1, :]).then_inc(s, 16)
                if j0 == 0:
                    for dst, name in ((wx_raw, "L0_cond_Wx"), (wh_raw, "L0_cond_Wh")):
                        sp.dma_start(dst.rearrange("p (k c) -> p k c", k=KD),
                                     a[name].rearrange("(k p) c -> p k c", p=P)).then_inc(d_w0, 16)
                    b0 = a["L0_cond_b"].rearrange("(g c) -> g c", c=P)
                    b1 = a["L1_cond_b"].rearrange("(g c) -> g c", c=P)
                    for half in range(2):
                        at = half * BIAS_SLOTS0
                        sp.dma_start(braw0[at:at + 4, :], b0[0:4, :]).then_inc(d_b, 16)
                        sp.dma_start(braw0[at + 4:at + 6, :], b0[6:8, :]).then_inc(d_b, 16)
                        sp.dma_start(braw0[at + 6:at + 8, :], b0[4:6, :]).then_inc(d_b, 16)
                        at = half * BIAS_SLOTS1
                        sp.dma_start(braw1[at:at + BIAS_SLOTS1, :], b1).then_inc(d_b, 16)
            sp.dma_start(wn[:, 0:IT, :], a["L0_ffn_w_gate"].rearrange("(q p) c -> p q c", p=P)).then_inc(d_ffn, 16)
            sp.dma_start(wn[:, IT:2 * IT, :], a["L0_ffn_w_up"].rearrange("(q p) c -> p q c", p=P)).then_inc(d_ffn, 16)
            sp.dma_start(wn[:, 2 * IT:3 * IT, :].rearrange("p (o s) c -> p o (s c)", o=KD),
                         a["L0_ffn_w_down"].rearrange("(o p) c -> p o c", p=P)).then_inc(d_ffn, 16)
            for dst, name in ((rx_raw, "L1_cond_Wx"), (rh_raw, "L1_cond_Wh")):
                sp.dma_start(dst.rearrange("p (k c) -> p k c", k=KD),
                             a[name].rearrange("(k p) c -> p k c", p=P)).then_inc(d_rnn, 16)
            sp.dma_start(wr_raw[:, :].rearrange("p (k c) -> p k c", k=KD),
                         a["L1_ffn_router_w"].rearrange("(k p) c -> p k c", p=P)).then_inc(d_rnn, 16)
            sp.dma_start(rb_all[:, :], a["L1_ffn_router_b"].rearrange("(a e) -> a e", a=1).broadcast_to([P, E])).then_inc(d_rnn, 16)
            sp.dma_start(b1_n[0:E * HT, :], a["L1_ffn_rb1"].rearrange("e (h c) -> (e h) c", c=P)).then_inc(d_moe_small, 16)
            sp.dma_start(b1_n[E * HT:SLOTS * HT, :], a["L1_ffn_sb1"].rearrange("(h c) -> h c", c=P)).then_inc(d_moe_small, 16)
            sp.dma_start(b2_all[0:E, :], a["L1_ffn_rb2"]).then_inc(d_moe_small, 16)
            sp.dma_start(b2_all[E:SLOTS, :], a["L1_ffn_sb2"].rearrange("(a c) -> a c", a=1)).then_inc(d_moe_small, 16)

            w1_v = a["L1_ffn_rw1"].rearrange("e (k p) c -> p e k c", p=P)
            w2_v = a["L1_ffn_rw2"].rearrange("e (k p) c -> p e k c", p=P)
            st1 = stage[:, 0, :].rearrange("p (k c) -> p k c", k=KD)
            st2 = stage[:, 1, :].rearrange("p (k c) -> p k c", k=HT)
            sp.wait_ge(down, 4 * CH)
            sp.wait_ge(x2_tok, 4 * CH)
            for e in range(SLOTS):
                s1 = w1_v[:, e] if e < E else a["L1_ffn_sw1"].rearrange("(k p) c -> p k c", p=P)
                s2 = w2_v[:, e] if e < E else a["L1_ffn_sw2"].rearrange("(k p) c -> p k c", p=P)
                for m, (dst, src) in enumerate(((st1, s1), (st2, s2))):
                    if e:
                        sp.wait_ge(e_lo, 2 * e + m - 1)
                    sp.dma_start(dst, src).then_inc(d_stage[m], 16)
            with sp.Fori(0, SUPERS) as s:
                sp.wait_ge(added, 2 + 20 * s + 20)
                for tt in range(2):
                    for c in range(4):
                        sp.dma_start(out_dram.rearrange("n (j tt) d -> tt n j d", tt=2)[tt, :, ds(4 * s + c, 1), :],
                                     xn[tt * N:(tt + 1) * N, ds(4 * s + c, 1), :]).then_inc(d_out, 16)
            sp.wait_ge(d_out, 16 * 8 * SUPERS)

        @block.gpsimd
        def _(pool):
            n = 0

            def step(ins):
                nonlocal n
                n += 1
                ins.then_inc(const_step, 1)
                pool.wait_ge(const_step, n)

            step(pool.memset(ident[:, :], 0.0))
            step(pool.affine_select(out=ident[:, :], in_=ident[:, :], compare_op=ALU.not_equal, fill=1.0,
                                    base=0, pattern=[[-1, P]], channel_multiplier=1))
            pool.memset(ones_row[:, :], 1.0).then_inc(const_step, 1)
            n += 1
            step(pool.memset(sel0[:, :], WS / 2))
            step(pool.memset(sel0[:, 4 * N:6 * N], WS))
            step(pool.memset(sel1[:, :], WS))
            for sel, slots, neg in ((sel0, BIAS_SLOTS0, nlow0), (sel1, BIAS_SLOTS1, nlow1)):
                v = sel[:, :].rearrange("q (s n) -> q s n", n=N)
                step(pool.affine_select(out=v, in_=v, compare_op=ALU.is_ge, fill=0.0, base=0,
                                        pattern=[[-1, slots], [0, N]], channel_multiplier=1))
                step(pool.affine_select(out=v, in_=v, compare_op=ALU.is_ge, fill=0.0, base=slots,
                                        pattern=[[1, slots], [0, N]], channel_multiplier=-1))
                for between in range(1, slots):
                    step(pool.affine_select(out=v, in_=v, compare_op=ALU.not_equal, fill=0.0, base=-between,
                                            pattern=[[-1, slots], [0, N]], channel_multiplier=1))
                step(pool.memset(neg[:, :], -1.0))
                step(pool.affine_select(out=neg[:, :], in_=neg[:, :], compare_op=ALU.is_ge, fill=0.0, base=-slots,
                                        pattern=[[0, 1]], channel_multiplier=1))
            step(pool.memset(before[:, :, :], 1.0))
            step(pool.affine_select(out=before[:, :, :], in_=before[:, :, :], compare_op=ALU.is_gt, fill=0.0,
                                    base=0, pattern=[[1, E], [-1, E]], channel_multiplier=0))
            assert n == CONSTS, n

            pool.wait_ge(d_x0, 32)
            for slot in range(2):
                pool.tensor_copy(xs[:, slot, :], xn[:, slot, :]).then_inc(x_staged, 1)
            pool.wait_ge(d_x1, 32)
            with pool.Fori(1, TILES // 2) as i:
                for slot in range(2):
                    pool.wait_ge(x_tr, 2 * i + slot - 1)
                    pool.tensor_copy(xs[:, slot, :], xn[:, ds(2 * i + slot, 1), :].rearrange("p a c -> p (a c)")
                                     ).then_inc(x_staged, 1)
            pool.wait_ge(m_step, 23)
            pool.tensor_copy(xs[:, :, :], xn[:, 0:4, :]).then_inc(xs_ready, 1)
            with pool.Fori(1, 2 * CH) as h:
                pool.wait_ge(xt_ps, 2 * h)
                pool.tensor_copy(xs[:, :, :], xn[:, ds(4 * h, 4), :]).then_inc(xs_ready, 1)

        @block.tensor
        def _(pe):
            pe.wait_ge(const_step, 3)
            pe.wait_ge(d_cond, 16)
            for k in range(KD):
                mm = pe.transpose(ps[:, 6, k * N:(k + 1) * N], cond_n[:, k * P:(k + 1) * P], ident[0:N, 0:N])
            mm.then_inc(cond_t, 1)
            def x_transpose(j, slot):
                pe.wait_ge(x_staged, j + 1)
                for k in range(KD):
                    mm = pe.transpose(ps[:, 4 + slot, k * P:(k + 1) * P], xs[:, slot, k * P:(k + 1) * P], ident[:, :])
                mm.then_inc(x_tr, 1)

            def gate_ps(u, s):
                return ps[:, u, s * N:(s + 1) * N] if s < 6 else ps[:, 2 + u, (s - 6) * N:(s - 5) * N]

            def x_part(u, slot, wait):
                if wait is not None:
                    pe.wait_ge(xt_lo, wait)
                pe.matmul(ps[:, u, 0:6 * N], brow0, sel0[:, 0:6 * N], start=True, stop=False, skip_group_check=True)
                pe.matmul(ps[:, 2 + u, 0:2 * N], brow0, sel0[:, 6 * N:8 * N], start=True, stop=False,
                          skip_group_check=True)
                for s, g in enumerate(GATE_ORDER):
                    o = gate_ps(u, s)
                    for k in range(KD):
                        cols = slice(k * GATES + g * P, k * GATES + (g + 1) * P)
                        hi = xt[:, slot, 0, k * P + u * N:k * P + (u + 1) * N]
                        lo = xt[:, slot, 1, k * P + u * N:k * P + (u + 1) * N]
                        for w, v in ((wx_h, hi), (wx_l, hi), (wx_h, lo)):
                            pe.matmul(o, w[:, cols], v, start=False, stop=False, skip_group_check=True)

            def h_part(t, u):
                pe.wait_ge(h_hi, t + 1)
                for slots in (range(6), range(6, 8)):
                    for low in (0, 1):
                        if low and slots[0] == 0:
                            pe.wait_ge(h_lo, t + 1)
                        for s in slots:
                            g = GATE_ORDER[s]
                            o = gate_ps(u, s)
                            for k in range(KD):
                                cols = slice(k * GATES + g * P, k * GATES + (g + 1) * P)
                                v = hb[:, u, low, k * N:(k + 1) * N]
                                for w in ((wh_h,) if low else (wh_h, wh_l)):
                                    mm = pe.matmul(o, w[:, cols], v, start=False, stop=low == 1, skip_group_check=True)
                    mm.then_inc(ifg_done if slots[0] == 0 else o_done, 1)

            def lstm_turn(i, weights, last):
                x_transpose(2 * i + 1, 1)
                h_part(4 * i, 0)
                x_part(1, 0, None)
                h_part(4 * i + 1, 1)
                x_part(0, 1, 2 * i + 2)
                if not last:
                    x_transpose(2 * i + 2, 0)
                h_part(4 * i + 2, 0)
                x_part(1, 1, None)
                h_part(4 * i + 3, 1)
                if not last:
                    x_part(0, 0, 2 * i + 3)
                if weights:
                    pe.wait_ge(wq_step, 5 * i + 5)
                    for q in range(4):
                        mm = pe.transpose(ps[:, 6, q * P:(q + 1) * P], wd[:, q * P:(q + 1) * P], ident[:, :])
                    mm.then_inc(w_tr, 1)

            x_transpose(0, 0)
            pe.wait_ge(prep_v, PREP0)
            x_part(0, 0, 1)
            with pe.Fori(0, PIECES // 2) as i:
                lstm_turn(i, True, False)
            with pe.Fori(PIECES // 2, T // 4 - 1) as i:
                lstm_turn(i, False, False)
            lstm_turn(T // 4 - 1, False, True)

            def spread(n):
                pe.wait_ge(m_col, n + 1)
                pe.transpose(ps[0:1, 7, 0:P], colmax[:, n:n + 1], ident[:, :]).then_inc(m_row, 1)
                pe.wait_ge(m_top, n + 1)
                pe.matmul(ps[:, 7, 256 + n:257 + n], ones_row[:, :], top[:, n:n + 1],
                          start=True, stop=True).then_inc(m_all, 1)

            def ffn_pass(first_piece, *free):
                with pe.Fori(0, CH) as cc:
                    for it in range(IT):
                        for s, base in free:
                            pe.wait_ge(s, base + 1 + IT * cc + it)
                        piece = first_piece + it
                        for half in range(2):
                            o = ps[:, 2 * (it % 3) + half, :]
                            r = [v[:, :, ds(16 * cc + 8 * half, 8), :] for v in (xh_v, xl_v)]
                            n = 0
                            for k in range(KD):
                                for w, x in ((wt_h, 0), (wt_l, 0), (wt_h, 1)):
                                    mm = pe.matmul(o, w[:, piece, k * P:(k + 1) * P], r[x][:, k, :, :],
                                                   start=n == 0, stop=n == 5)
                                    n += 1
                        mm.then_inc(pair_done, 1)

            spread(0)
            pe.wait_ge(wt_lo_done, PIECES // 2)
            pe.wait_ge(xq_lo, 8)
            ffn_pass(0, (pair_free_a, 0))
            spread(1)
            pe.wait_ge(pair_free_a, 3 + BLOCKS)
            ffn_pass(IT, (pair_free_v, 0))
            spread(2)
            spread(3)
            pe.wait_ge(pair_free_v, 3 + BLOCKS)
            ffn_pass(IT, (pair_free_a, BLOCKS))
            spread(4)

            def down_turn(cc, first):
                for half in range(2):
                    for ot in range(KD):
                        if not (first and half == 0):
                            pe.wait_ge(xt_sb, 4 * cc + 2 * half + ot - 1)
                        pe.wait_ge(xs_ready, 2 * cc + half + 1)
                        for c in range(4):
                            mm = pe.transpose(ps[:, 2 + ot, c * P:(c + 1) * P], xs[:, c, ot * P:(ot + 1) * P],
                                              ident[:, :])
                        mm.then_inc(xt_ps, 1)
                    for ot in range(KD):
                        if not (first and half == 0):
                            pe.wait_ge(x2_new, 4 * cc + 2 * half + ot - 1)
                        n = 0
                        for it in range(IT):
                            if half == 0 and ot == 0:
                                pe.wait_ge(o_lo, IT * cc + it + 1)
                            piece = 2 * IT + ot * (I0 // D) + it // 2
                            cols = slice((it % 2) * P, (it % 2 + 1) * P)
                            at = [(IT * cc + it) * 2 * BLOCK + v * BLOCK + half * 512 for v in range(2)]
                            for w, x in ((wt_h, 0), (wt_l, 0), (wt_h, 1)):
                                mm = pe.matmul(ps[:, ot, :], w[:, piece, cols], big16[:, ds(at[x], 512)],
                                               start=n == 0, stop=n == 3 * IT - 1)
                                n += 1
                        mm.then_inc(down, 1)
                        if not (first and half == 0 and ot == 0):
                            x2_transpose(4 * cc + 2 * half + ot - 1, 1 - ot, first and half == 0)

            def x2_transpose(unit, ot, no_wait):
                pe.wait_ge(x2_new, unit + 1)
                if not no_wait:
                    pe.wait_ge(x2_tok, unit - 1)
                for c in range(4):
                    mm = pe.transpose(ps[:, 4 + ot, c * P:(c + 1) * P], x2s[ot][:, c * P:(c + 1) * P], ident[:, :])
                mm.then_inc(x2_tr, 1)

            down_turn(0, True)
            with pe.Fori(1, CH) as cc:
                down_turn(cc, False)
            x2_transpose(4 * CH - 1, 1, False)

            pe.wait_ge(d_moe_small, 64)
            pe.transpose(ps[:, 7, 0:SLOTS * HT], b1_n[:, :], ident[0:SLOTS * HT, 0:SLOTS * HT]).then_inc(b1_tr, 1)
            pe.wait_ge(x2_lo, 4 * CH)

            def rnn_step(t, first=False):
                if not first:
                    pe.wait_ge(r_hi, t)
                pe.matmul(ps[:, 6, 0:SC], brow1[:, :], sel1[:, :], start=True, stop=False, skip_group_check=True)

                def products(wh, wl, hi, lo, last):
                    for low in (0, 1):
                        for o in range(KD):
                            for k in range(KD):
                                cols = slice(k * D + o * P, k * D + (o + 1) * P)
                                for w in ((wh,) if low else (wh, wl)):
                                    mm = pe.matmul(ps[:, 6, o * N:(o + 1) * N], w[:, cols], (lo if low else hi)(k),
                                                   start=False, stop=last and low == 1, skip_group_check=True)
                    return mm

                def at(v, when):
                    return lambda k: v[:, ds(k * T * N + when * N, N)]

                products(rx_h, rx_l, at(xh, t), at(xl, t), False)
                if first:
                    mm = products(rh_h, rh_l, lambda k: r0[:, 0, k * N:(k + 1) * N],
                                  lambda k: r0[:, 1, k * N:(k + 1) * N], True)
                else:
                    pe.wait_ge(r_lo, t)
                    mm = products(rh_h, rh_l, at(xh, t - 1), at(xl, t - 1), True)
                mm.then_inc(r_sum, 1)

            rnn_step(0, True)
            with pe.Fori(1, EARLY_STEPS) as t:
                rnn_step(t)

            def expert_up(s, e, m, rhs):
                pe.wait_ge(e_lo, 2 * e + 2)
                for ht in range(HT):
                    pe.wait_ge(gelu, 4 * m + ht + 1)
                    n = 0
                    for k in range(KD):
                        for low, x in ((0, 0), (1, 0), (0, 1)):
                            mm = pe.matmul(ps[:, ht, :], big16[:, ds(e * EXP + low * 1024 + k * H1 + ht * P, P)],
                                           rhs[x][:, k, :, :], start=n == 0, stop=n == 5)
                            n += 1
                    mm.then_inc(up1, 1)

            def expert_down(s, e, m, u):
                pe.wait_ge(split_lo, 2 + 4 * m + 4)
                for b in range(2):
                    pe.wait_ge(added, 20 * s + 2 * e + b + 1)
                    for tt in range(2):
                        n = 0
                        for ht in range(HT):
                            for hp, wp in ((0, 0), (0, 1), (1, 0)):
                                mm = pe.matmul(ps[:, 4 + b, tt * D:(tt + 1) * D],
                                               h1(u, hp, ht)[:, (2 * b + tt) * P:(2 * b + tt + 1) * P],
                                               big16[:, ds(e * EXP + 2048 + wp * 1024 + ht * D, D)],
                                               start=n == 0 and tt == 0, stop=n == 11, skip_group_check=True)
                                n += 1
                    mm.then_inc(down1, 1)

            def superchunk(s, with_rnn):
                if not with_rnn and s is None:
                    return
                rhs = [v[:, :, ds(SUPER_T * s, SUPER_T), :] for v in (xh_v, xl_v)]
                for tt in range(4):
                    n = 0
                    for k in range(KD):
                        for w, v in ((wr_h, xh), (wr_l, xh), (wr_h, xl)):
                            mm = pe.matmul(ps[:, 7, tt * E:(tt + 1) * E], v[:, ds(k * T * N + (SUPER_T * s + 2 * tt) * N, P)],
                                           w[:, k * E:(k + 1) * E], start=n == 0 and tt == 0, stop=n == 5,
                                           skip_group_check=True)
                            n += 1
                mm.then_inc(route, 1)
                with pe.Fori(0, SLOTS // GROUP) as g:
                    for u in range(GROUP):
                        e = GROUP * g + u
                        m = SLOTS * s + e
                        expert_up(s, e, m, rhs)
                        if u:
                            expert_down(s, e - 1, m - 1, u - 1)
                        if with_rnn:
                            rnn_step(EARLY_STEPS + m)
                    expert_down(s, GROUP * g + GROUP - 1, SLOTS * s + GROUP * g + GROUP - 1, GROUP - 1)
                pe.wait_ge(w9_done, s + 1)
                for tt in range(4):
                    mm = pe.transpose(ps[0:SLOTS, 7, tt * P:(tt + 1) * P], w9[:, tt, :], ident[:, :])
                mm.then_inc(w9_tr, 1)
                pe.wait_ge(w9t_done, s + 1)
                for b in range(2):
                    pe.wait_ge(added, 20 * s + 2 * SLOTS + b + 1)
                    for tt in range(2):
                        mm = pe.matmul(ps[:, 4 + b, tt * D:(tt + 1) * D],
                                       w9t[:, (2 * b + tt) * P:(2 * b + tt + 1) * P], b2_all[:, :],
                                       start=tt == 0, stop=True, skip_group_check=True)
                    mm.then_inc(down1, 1)

            pe.wait_ge(r_hi, SUPER_T)
            pe.wait_ge(r_lo, SUPER_T)
            pe.wait_ge(b1_ready, 1)
            with pe.Fori(0, RNN_SUPERS) as s:
                superchunk(s, True)
            pe.wait_ge(r_lo, T)
            with pe.Fori(RNN_SUPERS, SUPERS) as s:
                superchunk(s, False)

        @block.scalar
        def _(act):
            act.sem_inc(pair_free_a, 3)
            act.sem_inc(gelu, 4)

            def x_high(n, slot):
                act.wait_ge(x_tr, n)
                act.activation(xt[:, slot, 0, :], ps[:, 4 + slot, 0:KD * P], ACT.Copy).then_inc(xt_hi, 1)

            def lstm_step(t, u):
                act.wait_ge(ifg_done, t + 1)
                act.activation(tg[:, 0:6 * N], ps[:, u, 0:6 * N], ACT.Tanh, scale=1 / WS).then_inc(ifg_tanh, 1)
                act.wait_ge(o_done, t + 1)
                act.activation(tg[:, 6 * N:8 * N], ps[:, 2 + u, 0:2 * N], ACT.Tanh, scale=1 / WS).then_inc(o_tanh, 1)
                act.wait_ge(c_done, t + 1)
                act.activation(tc, cstate[:, 0:SC], ACT.Tanh, scale=0.5).then_inc(c_tanh, 1)

            def lstm_turn(i, weights, last):
                for r in range(4):
                    lstm_step(4 * i + r, r % 2)
                    if r == 0:
                        x_high(2 * i + 2, 1)
                    if r == 2 and not last:
                        x_high(2 * i + 3, 0)
                if weights:
                    act.wait_ge(w_tr, i + 1)
                    act.activation(wt_h[:, ds(2 * i, 2), :], ps[:, 6, :].rearrange("p (q c) -> p q c", q=2), ACT.Copy,
                                   scale=WS).then_inc(wt_hi_done, 1)

            x_high(1, 0)
            with act.Fori(0, PIECES // 2) as i:
                lstm_turn(i, True, False)
            with act.Fori(PIECES // 2, T // 4 - 1) as i:
                lstm_turn(i, False, False)
            lstm_turn(T // 4 - 1, False, True)

            act.wait_ge(m_step, 2)
            for c in range(8):
                if c >= 2:
                    act.wait_ge(xq_lo, c - 1)
                act.activation(qb[c % 2], hs[:, c * BLOCK:(c + 1) * BLOCK], ACT.Copy, scale=col(C_IH)).then_inc(xq_int, 1)

            def pair(it):
                return ps[:, 2 * (it % 3):2 * (it % 3) + 2, :].rearrange("p b c -> p (b c)")

            def blk(p):
                return big[:, ds(p * BLOCK, BLOCK)]

            act.wait_ge(m_step, 4)
            act.wait_ge(xq_lo, 8)
            act.wait_ge(prep_v, PREP1)
            with act.Fori(0, CH) as cc:
                for it in range(IT):
                    act.wait_ge(pair_done, IT * cc + it + 1)
                    act.activation(blk(IT * cc + it), pair(it), ACT.Copy, scale=col(C_U)).then_inc(pair_free_a, 1)
            act.wait_ge(m_step, 9)
            act.wait_ge(pair_free_a, 3 + BLOCKS)
            with act.Fori(0, CH) as cc:
                for it in range(IT):
                    p = IT * cc + it
                    act.wait_ge(gated, p + 1)
                    act.activation(qb[it % 2], blk(p), ACT.Copy, scale=col(C_IG)).then_inc(gate_q, 1)
                    act.wait_ge(m_step, 8)
                    act.wait_ge(gate_q, p + 1)
                    act.activation(blk(p), qb[it % 2], ACT.Tanh, scale=col(C_SGH)).then_inc(gate_t, 1)
                    act.wait_ge(m_step, 8)
                    act.wait_ge(gate_t, p + 1)
                    act.activation(sq[it % 2], blk(p), ACT.Copy, bias=32768.0, scale=32768.0).then_inc(gate_s, 1)
            act.wait_ge(m_step, 18)
            with act.Fori(0, CH) as cc:
                for it in range(IT):
                    p = IT * cc + it
                    act.wait_ge(pair_done, 2 * BLOCKS + p + 1)
                    act.wait_ge(prod, p + 1)
                    act.activation(qb[it % 2], pair(it), ACT.Copy, scale=col(C_FU)).then_inc(pair_free_a, 1)
                    act.activation(tmp_i[:, (2 + it % 2) * BLOCK:(3 + it % 2) * BLOCK], blk(p), ACT.Copy,
                                   scale=col(C_F2)).then_inc(gated_q, 1)

            act.wait_ge(m_step, 23)

            def down_turn(cc, first):
                for it in range(IT):
                    p = IT * cc + it
                    if not (first and it < 2):
                        act.wait_ge(o_lo, p - 1)
                    act.activation(qb[it % 2], blk(p), ACT.Copy, scale=col(C_F3)).then_inc(o_int, 1)
                for half in range(2):
                    for ot in range(KD):
                        n = 4 * cc + 2 * half + ot
                        act.wait_ge(xt_ps, n + 1)
                        if not (first and half == 0):
                            act.wait_ge(x2_new, n - 1)
                        act.activation(xts[ot], ps[:, 2 + ot, :], ACT.Copy).then_inc(xt_sb, 1)
                        if not (first and half == 0 and ot == 0):
                            x2_token(n - 1, 1 - ot, (cc if ot or half else cc - 1), (half if ot else 1 - half))

            def x2_token(n, ot, cc, half):
                act.wait_ge(x2_tr, n + 1)
                act.activation(xn[:, ds(8 * cc + 4 * half, 4), ot * P:(ot + 1) * P],
                               ps[:, 4 + ot, :].rearrange("p (c d) -> p c d", c=4), ACT.Copy).then_inc(x2_tok, 1)

            down_turn(0, True)
            with act.Fori(1, CH) as cc:
                down_turn(cc, False)
            x2_token(4 * CH - 1, 1, CH - 1, 1)

            act.wait_ge(b1_tr, 1)
            act.activation(b1_t[:, :], ps[:, 7, 0:SLOTS * HT], ACT.Copy).then_inc(b1_ready, 1)
            act.wait_ge(b1_ready, 1)

            def rnn_tanh(t):
                act.wait_ge(r_sum, t + 1)
                act.activation(hr[:, :], ps[:, 6, 0:SC], ACT.Tanh, scale=1 / WS).then_inc(r_tanh, 1)

            def expert_high(e):
                for m in range(2):
                    act.wait_ge(d_stage[m], 16 * e + 16)
                    act.activation(big16[:, ds(e * EXP + m * 2048, 1024)], stage[:, m, :], ACT.Copy,
                                   scale=WS).then_inc(e_hi, 1)
                    rnn_tanh(2 * e + m)

            with act.Fori(0, SLOTS) as e:
                expert_high(e)
            rnn_tanh(2 * SLOTS)

            def superchunk(s, with_rnn):
                act.wait_ge(route_z, s + 1)
                act.activation(ee[:, :, :], zz[:, :, :], ACT.Exp).then_inc(route_e, 1)
                with act.Fori(0, SLOTS // GROUP) as g:
                    for u in range(GROUP):
                        e = GROUP * g + u
                        m = SLOTS * s + e
                        for ht in range(HT):
                            act.wait_ge(up1, 4 * m + ht + 1)
                            act.wait_ge(split_lo, 4 * m + ht + 1)
                            act.activation(hf[ht % 2], ps[:, ht, :], ACT.Gelu, scale=1 / WS,
                                           bias=b1_t[:, ds(HT * e + ht, 1)]).then_inc(gelu, 1)
                        if with_rnn:
                            rnn_tanh(EARLY_STEPS + m)

            act.wait_ge(x2_tok, 4 * CH)
            with act.Fori(0, RNN_SUPERS) as s:
                superchunk(s, True)
            with act.Fori(RNN_SUPERS, SUPERS) as s:
                superchunk(s, False)

        @block.vector
        def _(dve):
            dve.sem_inc(pair_free_v, 3)
            dve.sem_inc(gated, 2)
            dve.sem_inc(prod, 2)
            dve.sem_inc(split_lo, 2)
            dve.sem_inc(added, 2)
            n_prep = 0

            def prep(ins):
                nonlocal n_prep
                n_prep += 1
                ins.then_inc(prep_v, 1)

            def split(hi, lo, src, scale):
                prep(dve.tensor_scalar(hi, src, scale, None, ALU.mult))
                dve.wait_ge(prep_v, n_prep)
                prep(dve.scalar_tensor_tensor(out=lo, in0=src, scalar=scale, in1=hi, op0=ALU.mult, op1=ALU.subtract))

            prep(dve.memset(cstate[:, 0:SC], 0.0))
            dve.wait_ge(cond_t, 1)
            c0 = ps[:, 6, 0:SC]
            dve.tensor_scalar(hb[:, 0, 0, :], c0, 2.0, None, ALU.mult).then_inc(h_hi, 1)
            dve.wait_ge(h_hi, 1)
            dve.scalar_tensor_tensor(out=hb[:, 0, 1, :], in0=c0, scalar=2.0, in1=hb[:, 0, 0, :],
                                     op0=ALU.mult, op1=ALU.subtract).then_inc(h_lo, 1)

            def x_low(n, slot):
                dve.wait_ge(xt_hi, n)
                dve.tensor_tensor(xt[:, slot, 1, :], ps[:, 4 + slot, 0:KD * P], xt[:, slot, 0, :],
                                  ALU.subtract).then_inc(xt_lo, 1)

            split(r0[:, 0, :], r0[:, 1, :], c0, 1.0)
            x_low(1, 0)
            dve.wait_ge(d_w0, 32)
            dve.wait_ge(d_b, 16 * 8)
            dve.wait_ge(const_step, CONSTS)
            for hi, lo, raw, scale in ((wx_h, wx_l, wx_raw, WS), (wh_h, wh_l, wh_raw, WS / 2)):
                hv, lv, rv = (v.rearrange("p (k c) -> p k c", k=KD) for v in (hi, lo, raw))
                for c0_, c1_, f in ((0, 3 * D, 0.5), (3 * D, 4 * D, 1.0)):
                    split(hv[:, :, c0_:c1_], lv[:, :, c0_:c1_], rv[:, :, c0_:c1_], scale * f)
            for bh, br, raw, neg in ((bhi0, brow0, braw0, nlow0), (bhi1, brow1, braw1, nlow1)):
                prep(dve.tensor_copy(bh[:, :], raw[:, :]))
                dve.wait_ge(prep_v, n_prep)
                prep(dve.scalar_tensor_tensor(out=br[:, :], in0=bh[:, :], scalar=neg[:, 0:1], in1=raw[:, :],
                                              op0=ALU.mult, op1=ALU.add))
            assert n_prep == PREP0

            def lstm_step(t, u):
                dve.wait_ge(ifg_tanh, t + 1)
                dve.scalar_tensor_tensor(out=fc, in0=tg[:, SC:2 * SC], scalar=1.0, in1=cstate[:, 0:SC],
                                         op0=ALU.add, op1=ALU.mult).then_inc(fc_done, 1)
                dve.scalar_tensor_tensor(out=ig, in0=tg[:, 0:SC], scalar=1.0, in1=tg[:, 2 * SC:3 * SC],
                                         op0=ALU.add, op1=ALU.mult).then_inc(ig_done, 1)
                dve.wait_ge(fc_done, t + 1)
                dve.wait_ge(ig_done, t + 1)
                dve.scalar_tensor_tensor(out=cstate[:, 0:SC], in0=fc, scalar=0.5, in1=ig,
                                         op0=ALU.mult, op1=ALU.add).then_inc(c_done, 1)
                dve.wait_ge(c_tanh, t + 1)
                dve.wait_ge(o_tanh, t + 1)
                hi, h = hb[:, 1 - u, 0, :], hs[:, ds(t * SC, SC)]
                dve.scalar_tensor_tensor(out=hi, in0=tg[:, 3 * SC:4 * SC], scalar=1.0, in1=tc,
                                         op0=ALU.add, op1=ALU.mult).then_inc(h_hi, 1)
                dve.scalar_tensor_tensor(out=h, in0=tg[:, 3 * SC:4 * SC], scalar=1.0, in1=tc,
                                         op0=ALU.add, op1=ALU.mult).then_inc(hs_done, 1)
                dve.wait_ge(hs_done, t + 1)
                dve.wait_ge(h_hi, t + 2)
                dve.tensor_tensor(hb[:, 1 - u, 1, :], h, hi, ALU.subtract).then_inc(h_lo, 1)
                dve.tensor_reduce(maxes[:, 0, ds(t, 1)], h, AX.X, ALU.max, apply_absolute_value=True).then_inc(hmax_done, 1)

            def lstm_turn(i, weights, last):
                w = wn[:, ds(2 * i, 2), :].rearrange("p q (b c) -> p (q b) c", c=WBLK) if weights else None
                s16, i16 = blk_s[:, 0, :], blk_s[:, 1, :]
                for r in range(4):
                    lstm_step(4 * i + r, r % 2)
                    if r == 0:
                        x_low(2 * i + 2, 1)
                        if weights:
                            dve.tensor_reduce(blk_s[:, 2, :], w, AX.X, ALU.max,
                                              apply_absolute_value=True).then_inc(wq_step, 1)
                            dve.wait_ge(wq_step, 5 * i + 1)
                            dve.tensor_scalar(s16, blk_s[:, 2, :], 1 / 7.0, TINY, ALU.mult, ALU.max).then_inc(wq_step, 1)
                            dve.wait_ge(wq_step, 5 * i + 2)
                            dve.reciprocal(i16, s16).then_inc(wq_step, 1)
                    if r == 1 and weights:
                        dve.wait_ge(wq_step, 5 * i + 3)
                        dve.tensor_tensor(w16.rearrange("p (b c) -> p b c", c=WBLK), w,
                                          i16.unsqueeze(2).broadcast_to([P, 16, WBLK]), ALU.mult).then_inc(wq_step, 1)
                    if r == 2:
                        if not last:
                            x_low(2 * i + 3, 0)
                        if weights:
                            dve.wait_ge(wq_step, 5 * i + 4)
                            dve.tensor_tensor(wd.rearrange("p (b c) -> p b c", c=WBLK),
                                              w16.rearrange("p (b c) -> p b c", c=WBLK),
                                              s16.unsqueeze(2).broadcast_to([P, 16, WBLK]), ALU.mult).then_inc(wq_step, 1)
                if weights:
                    dve.wait_ge(wt_hi_done, i + 1)
                    dve.scalar_tensor_tensor(out=wt_l[:, ds(2 * i, 2), :],
                                             in0=ps[:, 6, :].rearrange("p (q c) -> p q c", q=2), scalar=WS,
                                             in1=wt_h[:, ds(2 * i, 2), :], op0=ALU.mult,
                                             op1=ALU.subtract).then_inc(wt_lo_done, 1)

            dve.wait_ge(d_ffn, 48)
            with dve.Fori(0, PIECES // 2) as i:
                lstm_turn(i, True, False)
            with dve.Fori(PIECES // 2, T // 4 - 1) as i:
                lstm_turn(i, False, False)
            lstm_turn(T // 4 - 1, False, True)

            def greatest(n, row, cols):
                dve.tensor_reduce(colmax[:, n:n + 1], maxes[:, row, 0:cols], AX.X, ALU.max).then_inc(m_col, 1)
                dve.wait_ge(m_row, n + 1)
                dve.tensor_reduce(top[:, n:n + 1], ps[0:1, 7, 0:P], AX.X, ALU.max).then_inc(m_top, 1)
                dve.wait_ge(m_all, n + 1)
                return ps[:, 7, 256 + n:257 + n]

            n_step = 0

            def mstep(ins):
                nonlocal n_step
                n_step += 1
                ins.then_inc(m_step, 1)
                dve.wait_ge(m_step, n_step)

            dve.wait_ge(hmax_done, T)
            m = greatest(0, 0, T)
            mstep(dve.tensor_scalar(col(C_SH), m, 1 / QMAX, 2 * TINY, ALU.mult, ALU.max))
            mstep(dve.reciprocal(col(C_IH), col(C_SH)))
            mstep(dve.tensor_scalar(col(C_U), col(C_SH), 0.5 / WS, None, ALU.mult))
            mstep(dve.memset(col(C_R), 0.0))
            assert n_step == 4
            for c in range(8):
                dve.wait_ge(xq_int, c + 1)
                hi, lo = (v[:, :, 8 * c:8 * c + 8, :].rearrange("p k t n -> p t k n") for v in (xh_v, xl_v))
                q = qb[c % 2].rearrange("p (t k n) -> p t k n", k=KD, n=N)
                dve.tensor_copy(hi, q).then_inc(xq_hi, 1)
                dve.wait_ge(xq_hi, c + 1)
                dve.tensor_tensor(lo, q, hi, ALU.subtract).then_inc(xq_lo, 1)

            dve.wait_ge(d_rnn, 64)
            split(rx_h[:, :], rx_l[:, :], rx_raw, WS)
            split(rh_h[:, :], rh_l[:, :], rh_raw, WS)
            split(wr_h[:, :], wr_l[:, :], wr_raw[:, :], WS)
            assert n_prep == PREP1
            dve.wait_ge(d_moe_small, 64)
            prep(dve.tensor_scalar(b2_all[:, :], b2_all[:, :], WS, None, ALU.mult))
            prep(dve.memset(w9[:, :, E:SLOTS], 1 / WS))

            def pair(it):
                return ps[:, 2 * (it % 3):2 * (it % 3) + 2, :].rearrange("p b c -> p (b c)")

            def blk(p):
                return big[:, ds(p * BLOCK, BLOCK)]

            def abs_max(out_, in_):
                return dve.tensor_reduce(out_, in_, AX.X, ALU.max, apply_absolute_value=True)

            with dve.Fori(0, CH) as cc:
                for it in range(IT):
                    dve.wait_ge(pair_free_a, 3 + IT * cc + it + 1)
                    abs_max(maxes[:, 1, ds(IT * cc + it, 1)], blk(IT * cc + it)).then_inc(gate_max, 1)
            dve.wait_ge(gate_max, BLOCKS)
            m = greatest(1, 1, BLOCKS)
            mstep(dve.tensor_scalar(col(C_T1), m, 1 / QMAX, None, ALU.mult))
            mstep(dve.tensor_scalar(col(C_SG), col(C_T1), TINY, None, ALU.max))
            mstep(dve.reciprocal(col(C_IG), col(C_SG)))
            mstep(dve.tensor_scalar(col(C_SGH), col(C_SG), 0.5, None, ALU.mult))
            mstep(dve.tensor_scalar(col(C_SG16), col(C_SG), 1 / 65536.0, None, ALU.mult))
            assert n_step == 9
            with dve.Fori(0, CH) as cc:
                for it in range(IT):
                    p = IT * cc + it
                    dve.wait_ge(pair_done, BLOCKS + p + 1)
                    abs_max(maxes[:, 2, ds(p, 1)], pair(it)).then_inc(pair_free_v, 1)
                    dve.wait_ge(gate_s, p + 1)
                    dve.tensor_tensor(blk(p), qb[it % 2], sq[it % 2], ALU.mult).then_inc(gated, 1)
                    dve.wait_ge(gated, p + 3)
                    abs_max(maxes[:, 3, ds(p, 1)], blk(p)).then_inc(gated_max, 1)
            dve.wait_ge(pair_free_v, 3 + BLOCKS)
            dve.wait_ge(gated_max, BLOCKS)
            m = greatest(2, 2, BLOCKS)
            mstep(dve.tensor_scalar(col(C_T1), m, col(C_U), 1 / QMAX, ALU.mult, ALU.mult))
            mstep(dve.tensor_scalar(col(C_SU), col(C_T1), TINY, None, ALU.max))
            mstep(dve.reciprocal(col(C_ISU), col(C_SU)))
            mstep(dve.tensor_scalar(col(C_FU), col(C_ISU), col(C_U), None, ALU.mult))
            m = greatest(3, 3, BLOCKS)
            mstep(dve.tensor_scalar(col(C_T2), m, col(C_SG16), 1 / QMAX, ALU.mult, ALU.mult))
            mstep(dve.tensor_scalar(col(C_S2), col(C_T2), TINY, None, ALU.max))
            mstep(dve.reciprocal(col(C_T3), col(C_S2)))
            mstep(dve.tensor_scalar(col(C_F2), col(C_T3), col(C_SG16), None, ALU.mult))
            mstep(dve.tensor_scalar(col(C_T4), col(C_S2), col(C_SU), None, ALU.mult))
            assert n_step == 18
            with dve.Fori(0, CH) as cc:
                for it in range(IT):
                    p = IT * cc + it
                    dve.wait_ge(gated_q, p + 1)
                    dve.wait_ge(pair_free_a, 3 + BLOCKS + p + 1)
                    dve.tensor_tensor(blk(p), qb[it % 2], tmp_i[:, (2 + it % 2) * BLOCK:(3 + it % 2) * BLOCK],
                                      ALU.mult).then_inc(prod, 1)
                    dve.wait_ge(prod, p + 3)
                    abs_max(maxes[:, 1, ds(p, 1)], blk(p)).then_inc(prod_max, 1)
            dve.wait_ge(prod_max, BLOCKS)
            m = greatest(4, 1, BLOCKS)
            mstep(dve.tensor_scalar(col(C_T1), m, col(C_T4), 1 / QMAX, ALU.mult, ALU.mult))
            mstep(dve.tensor_scalar(col(C_S3), col(C_T1), TINY, None, ALU.max))
            mstep(dve.reciprocal(col(C_T3), col(C_S3)))
            mstep(dve.tensor_scalar(col(C_F3), col(C_T3), col(C_T4), None, ALU.mult))
            mstep(dve.tensor_scalar(col(C_OUT), col(C_S3), 1 / WS, None, ALU.mult))
            assert n_step == 23

            def down_turn(cc, first):
                for it in range(IT):
                    p = IT * cc + it
                    dve.wait_ge(o_int, p + 1)
                    hi = big16[:, ds(p * 2 * BLOCK, BLOCK)]
                    lo = big16[:, ds(p * 2 * BLOCK + BLOCK, BLOCK)]
                    dve.tensor_copy(hi, qb[it % 2]).then_inc(o_hi, 1)
                    dve.wait_ge(o_hi, p + 1)
                    dve.tensor_tensor(lo, qb[it % 2], hi, ALU.subtract).then_inc(o_lo, 1)
                for half in range(2):
                    for ot in range(KD):
                        n = 4 * cc + 2 * half + ot
                        dve.wait_ge(down, n + 1)
                        dve.wait_ge(xt_sb, n + 1)
                        if not (first and half == 0):
                            dve.wait_ge(x2_tr, n - 1)
                        dve.scalar_tensor_tensor(out=x2s[ot], in0=ps[:, ot, :], scalar=col(C_OUT), in1=xts[ot],
                                                 op0=ALU.mult, op1=ALU.add).then_inc(x2_new, 1)
                        dve.wait_ge(x2_new, n + 1)
                        src = x2s[ot].rearrange("p (t n) -> p t n", n=N)
                        hi = xh_v[:, ot, ds(16 * cc + 8 * half, 8), :]
                        lo = xl_v[:, ot, ds(16 * cc + 8 * half, 8), :]
                        dve.tensor_copy(hi, src).then_inc(x2_hi, 1)
                        dve.wait_ge(x2_hi, n + 1)
                        dve.tensor_tensor(lo, src, hi, ALU.subtract).then_inc(x2_lo, 1)

            down_turn(0, True)
            with dve.Fori(1, CH) as cc:
                down_turn(cc, False)

            def rnn_split(t):
                dve.wait_ge(r_tanh, t + 1)
                hi, lo = (v[:, :, ds(t, 1), :].rearrange("p k a n -> p k (a n)") for v in (xh_v, xl_v))
                new = hr[:, :].rearrange("p (k n) -> p k n", k=KD)
                dve.tensor_copy(hi, new).then_inc(r_hi, 1)
                dve.wait_ge(r_hi, t + 1)
                dve.tensor_tensor(lo, new, hi, ALU.subtract).then_inc(r_lo, 1)

            with dve.Fori(0, SLOTS) as e:
                for m in range(2):
                    dve.wait_ge(e_hi, 2 * e + m + 1)
                    at = e * EXP + m * 2048
                    dve.scalar_tensor_tensor(out=big16[:, ds(at + 1024, 1024)], in0=stage[:, m, :], scalar=WS,
                                             in1=big16[:, ds(at, 1024)], op0=ALU.mult,
                                             op1=ALU.subtract).then_inc(e_lo, 1)
                    rnn_split(2 * e + m)
            rnn_split(2 * SLOTS)

            def router(s):
                k = 0

                def link(ins):
                    nonlocal k
                    k += 1
                    ins.then_inc(route_step, 1)
                    dve.wait_ge(route_step, ROUTE_STEPS * s + k)

                def over_e(v):
                    return v.unsqueeze(2).broadcast_to([P, 4, E])

                lv = ps[:, 7, 0:4 * E].rearrange("p (t e) -> p t e", e=E)
                dve.wait_ge(route, s + 1)
                link(dve.scalar_tensor_tensor(out=lg[:, :, :], in0=lv, scalar=1 / WS,
                                              in1=rb_all[:, :].unsqueeze(1).broadcast_to([P, 4, E]),
                                              op0=ALU.mult, op1=ALU.add))
                link(dve.tensor_reduce(mrow[:, 0:4], lg[:, :, :], AX.X, ALU.max))
                dve.tensor_tensor(zz[:, :, :], lg[:, :, :], over_e(mrow[:, 0:4]), ALU.subtract).then_inc(route_z, 1)
                mine = lg[:, :, :].unsqueeze(3).broadcast_to([P, 4, E, E])
                other = lg[:, :, :].unsqueeze(2).broadcast_to([P, 4, E, E])
                link(dve.tensor_tensor(cmp_a[:, :, :, :], other, mine, ALU.is_ge))
                link(dve.tensor_tensor(cmp_b[:, :, :, :], other, mine, ALU.is_gt))
                for tt in range(4):
                    last = dve.tensor_tensor(cmp_a[:, tt, :, :], cmp_a[:, tt, :, :], before[:, :, :], ALU.mult)
                link(last)
                link(dve.tensor_tensor(cmp_b[:, :, :, :], cmp_b[:, :, :, :], cmp_a[:, :, :, :], ALU.max))
                link(dve.tensor_reduce(rank[:, :, :], cmp_b[:, :, :, :], AX.X, ALU.add))
                dve.wait_ge(route_e, s + 1)
                link(dve.tensor_reduce(mrow[:, 4:8], ee[:, :, :], AX.X, ALU.add))
                link(dve.reciprocal(mrow[:, 8:12], mrow[:, 4:8]))
                link(dve.tensor_scalar(mrow[:, 12:16], mrow[:, 8:12], 1 / WS, None, ALU.mult))
                link(dve.tensor_tensor(ee[:, :, :], ee[:, :, :], over_e(mrow[:, 12:16]), ALU.mult))
                dve.scalar_tensor_tensor(out=w9[:, :, 0:E], in0=rank[:, :, :], scalar=2.0, in1=ee[:, :, :],
                                         op0=ALU.is_lt, op1=ALU.mult).then_inc(w9_done, 1)
                assert k == ROUTE_STEPS

            def split_expert(m, u):
                for ht in range(HT):
                    dve.wait_ge(gelu, 4 + 4 * m + ht + 1)
                    dve.tensor_copy(h1(u, 0, ht), hf[ht % 2]).then_inc(split_hi, 1)
                    dve.wait_ge(split_hi, 4 * m + ht + 1)
                    dve.tensor_tensor(h1(u, 1, ht), hf[ht % 2], h1(u, 0, ht), ALU.subtract).then_inc(split_lo, 1)

            def add_expert(s, e):
                dve.wait_ge(w9_done, s + 1)
                for b in range(2):
                    dve.wait_ge(down1, 20 * s + 2 * e + b + 1)
                    dve.wait_ge(added, 20 * s + 2 * e + b + 1)
                    for tt in range(2):
                        tile = xn[:, ds(4 * s + 2 * b + tt, 1), :].rearrange("p a c -> p (a c)")
                        ins = dve.scalar_tensor_tensor(out=tile, in0=ps[:, 4 + b, tt * D:(tt + 1) * D],
                                                       scalar=w9[:, 2 * b + tt, ds(e, 1)], in1=tile,
                                                       op0=ALU.mult, op1=ALU.add)
                    ins.then_inc(added, 1)

            def superchunk(s, with_rnn):
                router(s)
                with dve.Fori(0, SLOTS // GROUP) as g:
                    for u in range(GROUP):
                        e = GROUP * g + u
                        m = SLOTS * s + e
                        split_expert(m, u)
                        if u:
                            add_expert(s, e - 1)
                        if with_rnn:
                            rnn_split(EARLY_STEPS + m)
                    add_expert(s, GROUP * g + GROUP - 1)
                dve.wait_ge(w9_tr, s + 1)
                dve.tensor_copy(w9t[:, :], ps[0:SLOTS, 7, :]).then_inc(w9t_done, 1)
                for b in range(2):
                    n = 20 * s + 2 * SLOTS + b + 1
                    dve.wait_ge(down1, n)
                    dve.wait_ge(added, n)
                    tiles = xn[:, ds(4 * s + 2 * b, 2), :]
                    dve.tensor_tensor(tiles, ps[:, 4 + b, :].rearrange("p (t c) -> p t c", t=2), tiles,
                                      ALU.add).then_inc(added, 1)

            dve.wait_ge(x2_tok, 4 * CH)
            with dve.Fori(0, RNN_SUPERS) as s:
                superchunk(s, True)
            with dve.Fori(RNN_SUPERS, SUPERS) as s:
                superchunk(s, False)


_INS = ['x', 'cond_1024', 'L0_cond_Wx', 'L0_cond_Wh', 'L0_cond_b', 'L0_ffn_w_gate', 'L0_ffn_w_up', 'L0_ffn_w_down',
        'L1_cond_Wx', 'L1_cond_Wh', 'L1_cond_b', 'L1_ffn_router_w', 'L1_ffn_router_b', 'L1_ffn_sw1', 'L1_ffn_sb1',
        'L1_ffn_sw2', 'L1_ffn_sb2', 'L1_ffn_rw1', 'L1_ffn_rb1', 'L1_ffn_rw2', 'L1_ffn_rb2']


def kernel(**inputs):
    import numpy as _np
    import concourse.bacc as _bacc
    from concourse import mybir as _mybir
    from concourse.bass_utils import run_bass_kernel_spmd as _run

    nc = _bacc.Bacc("TRN2", target_bir_lowering=False, num_devices=1)
    arrays, args = {}, {}
    for name in _INS:
        v = _np.ascontiguousarray(inputs[name])
        arrays[f"in_{name}"] = v
        args[name] = nc.dram_tensor(f"in_{name}", v.shape, _mybir.dt.from_np(v.dtype), kind="ExternalInput").ap()
    out = nc.dram_tensor("out_0", (N, T, D), F32, kind="ExternalOutput").ap()
    mixed_layers(nc, args, out)
    r = _run(nc, [arrays], core_ids=[0])
    return r.results[0]["out_0"]
```

```python
from contextlib import ExitStack

import concourse.bass as bass
from concourse import mybir

ALU = mybir.AluOpType
ACT = mybir.ActivationFunctionType
AX = mybir.AxisListType
F32 = mybir.dt.float32
F16 = mybir.dt.float16
I16 = mybir.dt.int16
U16 = mybir.dt.uint16
I32 = mybir.dt.int32
U32 = mybir.dt.uint32
ds = bass.ds

P = 128
N = 64
T = 64
D = 256
KD = D // P
SC = KD * N
TILES = T // 2
GATES = 4 * D
I0 = 768
IT = I0 // P
H1 = 512
HT = H1 // P
E = 8
SLOTS = E + 1
SUPERS = 8
SUPER_T = T // SUPERS
GROUP = 3
CH = 4
BLOCK = 1024
BLOCKS = CH * IT
WBLK = 32
PIECES = 3 * I0 // P
QMAX = 32767.0
TINY = 1e-12
WS = 256.0
BIAS_SLOTS0 = GATES // P
BIAS_SLOTS1 = D // P
GATE_ORDER = [0, 1, 2, 3, 6, 7, 4, 5]
EARLY_FILLS = 4

REGION = T * N
TOP_K = 2
HALVES = 2
UROWS = HALVES * P
UNITS = T * N * TOP_K // UROWS + E
DUMMY = E
ROW = 2 * D + 2 * 2 * SLOTS
W_AT = D
DST_AT = D + SLOTS
RING = 4
NOWHERE = 1.0e6
K_DST, K_LANE, K_BASE, K_UNIT = 0, TILES, TILES + HALVES, TILES + HALVES + E
K_COLS = K_UNIT + UNITS


def mixed_layers(nc, a, rows_dram, pairs_dram, out):
    with ExitStack() as ctx:
        def sb(name, shape, dt):
            return ctx.enter_context(nc.sbuf_tensor(name, shape, dt))

        def sem(name):
            return ctx.enter_context(nc.semaphore(name))

        ps = ctx.enter_context(nc.psum_tensor("ps", [P, 8, 512], F32))

        big = sb("big", [P, BLOCKS * BLOCK], F32)
        big16 = big[:, :].bitcast(F16)
        xn = sb("xn", [P, TILES, D], F32)
        xh = sb("xh", [P, T * SC], F16)
        xl = sb("xl", [P, T * SC], F16)
        xh_v = xh[:, :].rearrange("p (k t n) -> p k t n", k=KD, n=N)
        xl_v = xl[:, :].rearrange("p (k t n) -> p k t n", k=KD, n=N)
        wt_h = sb("wt_h", [P, PIECES, D], F16)
        wt_l = sb("wt_l", [P, PIECES, D], F16)
        rx_h = sb("rx_h", [P, KD * D], F16)
        rx_l = sb("rx_l", [P, KD * D], F16)
        rh_h = sb("rh_h", [P, KD * D], F16)
        rh_l = sb("rh_l", [P, KD * D], F16)
        tmp = sb("tmp", [P, 4096], F32)
        ident = sb("ident", [P, P], F32)
        ones_row = sb("ones_row", [1, P], F32)
        cstate = sb("cstate", [P, 2 * SC], F32)
        r0 = sb("r0", [P, 2, SC], F16)
        sel1 = sb("sel1", [2 * BIAS_SLOTS1, SC], F16)
        braw1 = sb("braw1", [2 * BIAS_SLOTS1, P], F32)
        bhi1 = sb("bhi1", [2 * BIAS_SLOTS1, P], F16)
        brow1 = sb("brow1", [2 * BIAS_SLOTS1, P], F16)
        nlow0 = sb("nlow0", [2 * BIAS_SLOTS0, 1], F32)
        nlow1 = sb("nlow1", [2 * BIAS_SLOTS1, 1], F32)
        wr_raw = sb("wr_raw", [P, KD * E], F32)
        wr_h = sb("wr_h", [P, KD * E], F16)
        wr_l = sb("wr_l", [P, KD * E], F16)
        rb_all = sb("rb_all", [P, E], F32)
        b1_n = sb("b1_n", [SLOTS * HT, P], F32)
        b1_t = sb("b1_t", [P, SLOTS * HT], F32)
        b2_all = sb("b2_all", [SLOTS, D], F32)
        maxes = sb("maxes", [P, 4, 64], F32)
        colmax = sb("colmax", [P, 8], F32)
        top = sb("top", [1, 8], F32)
        sc = sb("sc", [P, 24], F32)
        blk_s = sb("blk_s", [P, 3, 16], F32)
        lg = sb("lg", [P, 4, E], F32)
        zz = sb("zz", [P, 4, E], F32)
        ee = sb("ee", [P, 4, E], F32)
        mrow = sb("mrow", [P, 16], F32)
        before = sb("before", [P, E, E], F32)
        rank = sb("rank", [P, 4, E], F32)
        consts = sb("shape_consts", [P, K_COLS], F32)
        ident16 = sb("ident16", [P, P], F16)
        tri16 = sb("tri16", [P, P], F16)
        ones16 = sb("ones16", [P, P], F16)
        chosen = sb("chosen", [P, 4, E], F16)
        carry = sb("carry", [P, 2, E], F32)
        row_j = sb("row_j", [P, 4, TOP_K], U32)
        w9 = sb("w9", [P, 4, SLOTS], F32)
        hr = sb("hr", [P, SC], F32)

        cond_n = tmp[0:N, 0:D]
        sel0 = tmp[0:2 * BIAS_SLOTS0, 256:512].bitcast(F16)
        braw0 = tmp[0:2 * BIAS_SLOTS0, 512:640]
        bhi0 = tmp[0:2 * BIAS_SLOTS0, 640:704].bitcast(F16)
        brow0 = tmp[0:2 * BIAS_SLOTS0, 704:768].bitcast(F16)
        w9t = tmp[0:SLOTS, 3072:3584]
        cmp_a = tmp[:, 3584:3840].rearrange("p (t e j) -> p t e j", e=E, j=E)
        cmp_b = tmp[:, 3840:4096].rearrange("p (t e j) -> p t e j", e=E, j=E)

        def part(start, cols):
            return big[:, start:start + cols]

        wx_h = part(0, 1024).bitcast(F16)
        wx_l = part(1024, 1024).bitcast(F16)
        wh_h = part(2048, 1024).bitcast(F16)
        wh_l = part(3072, 1024).bitcast(F16)
        wn = part(4096, PIECES * D).rearrange("p (q c) -> p q c", c=D)
        wx_raw = part(8704, 2048)
        wh_raw = part(10752, 2048)
        rx_raw = part(12800, 512)
        rh_raw = part(13312, 512)
        tg = part(13824, 512)
        fc = part(14336, SC)
        ig = part(14464, SC)
        tc = part(14592, SC)
        hb = part(14720, 2 * SC).bitcast(F16).rearrange("p (s h c) -> p s h c", s=2, h=2)
        xt = part(14976, 512).bitcast(F16).rearrange("p (s h c) -> p s h c", s=2, h=2)
        wd = part(15488, 512)
        w16 = part(16000, 256).bitcast(I16)
        hs = part(16384, T * SC)

        tmp_i = tmp[:, :].bitcast(I16)
        tmp_u = tmp[:, :].bitcast(U16)
        qb = [tmp_i[:, i * BLOCK:(i + 1) * BLOCK] for i in range(2)]
        sq = [tmp_u[:, (2 + i) * BLOCK:(3 + i) * BLOCK] for i in range(2)]
        xts = [tmp[:, 2048 + 512 * i:2560 + 512 * i] for i in range(2)]
        x2s = [tmp[:, 3072 + 512 * i:3584 + 512 * i] for i in range(2)]
        xs = tmp[:, 1024:2048].rearrange("p (c d) -> p c d", c=4)
        stage = tmp[:, 0:2048].rearrange("p (m c) -> p m c", m=2)
        hf = [tmp[:, 2048 + 512 * i:2560 + 512 * i] for i in range(2)]
        EXP = 4096
        H1_AT = SLOTS * EXP

        def h1(part_, ht):
            at = H1_AT + part_ * 2048 + ht * 512
            return big16[:, at:at + 512]

        rows = wt_h[:, :, :].rearrange("p q c -> p (q c)")[:, 0:4 * ROW].rearrange("p (t c) -> p t c", c=ROW)
        empty = wt_l[:, :, :].rearrange("p q c -> p (q c)")[:, 0:ROW]
        rows32 = wt_h[:, :, :].rearrange("p q c -> p (q c)")[:, 0:4 * ROW].bitcast(F32).rearrange(
            "p (t c) -> p t c", c=ROW // 2)
        empty32 = empty.bitcast(F32)
        spare = wt_l[:, :, :].rearrange("p q c -> p (q c)").bitcast(F32)[:, 512:]
        count = spare[:, 0:6 * E].rearrange("p (i e) -> p i e", e=E)
        place = spare[:, 48:48 + 4 * E].rearrange("p (t e) -> p t e", e=E)
        place_j = spare[:, 80:80 + 4 * TOP_K * E].rearrange("p (t j e) -> p t j e", j=TOP_K, e=E)
        tiles_i = spare[:, 144:144 + E].bitcast(I32)
        fill_i = spare[:, 152:152 + HALVES * E].bitcast(U32)
        dst_i = spare[:, 176:176 + HALVES * RING].bitcast(U32)
        unit_f = spare[:, 192:192 + 2 * UNITS].rearrange("p (i u) -> p i u", i=2)
        unit_i = spare[:, 512:512 + 2 * UNITS].bitcast(I32).rearrange("p (i u) -> p i u", i=2)
        xr = [xh[:, u * HALVES * ROW:(u + 1) * HALVES * ROW].rearrange("p (h c) -> p h c", h=HALVES) for u in range(RING)]
        xr32 = [xh[:, u * HALVES * ROW:(u + 1) * HALVES * ROW].bitcast(F32).rearrange("p (h c) -> p h c", h=HALVES)
                for u in range(RING)]
        XT = 2 * KD * UROWS
        xrt = [xl[:, u * XT:(u + 1) * XT] for u in range(2)]
        H = HT * UROWS
        h1r = [xl[:, 2 * XT + 2 * u * H:2 * XT + 2 * (u + 1) * H] for u in range(2)]
        hfr = [tmp[:, 2048 + u * H:2048 + (u + 1) * H] for u in range(2)]
        yr = [tmp[:, u * HALVES * D:(u + 1) * HALVES * D] for u in range(RING)]
        reached = tmp[:, 3072:3072 + UNITS * E].rearrange("p (i e) -> p i e", e=E)
        pairs = big[:, 0:SUPERS * 2048].rearrange("p (s t c) -> p s t c", s=SUPERS, t=4)

        block_v = big[:, :].rearrange("p (b c) -> p b c", c=BLOCK)

        d_x0, d_x1, d_cond, d_w0, d_b, d_ffn, d_rnn, d_moe_small, d_out = (
            sem(s) for s in ("d_x0", "d_x1", "d_cond", "d_w0", "d_b", "d_ffn", "d_rnn", "d_moe_small", "d_out"))
        d_stage = [sem("d_stage1"), sem("d_stage2")]
        const_step = sem("const_step")
        cond_t = sem("cond_t")
        prep_v = sem("prep_v")
        h_hi = sem("h_hi")
        h_lo = sem("h_lo")
        ifg_done, o_done = sem("ifg_done"), sem("o_done")
        ifg_tanh, o_tanh, c_tanh = sem("ifg_tanh"), sem("o_tanh"), sem("c_tanh")
        fc_done, ig_done, c_done, hs_done, hmax_done = (
            sem(s) for s in ("fc_done", "ig_done", "c_done", "hs_done", "hmax_done"))
        x_staged, xs_ready = sem("x_staged"), sem("xs_ready")
        x_tr, xt_hi, xt_lo = sem("x_tr"), sem("xt_hi"), sem("xt_lo")
        wq_step = sem("wq_step")
        w_tr, wt_hi_done, wt_lo_done = sem("w_tr"), sem("wt_hi_done"), sem("wt_lo_done")
        m_col, m_row, m_top, m_all, m_step = (sem(s) for s in ("m_col", "m_row", "m_top", "m_all", "m_step"))
        xq_int, xq_hi, xq_lo = sem("xq_int"), sem("xq_hi"), sem("xq_lo")
        pair_done, pair_free_v, pair_free_a = sem("pair_done"), sem("pair_free_v"), sem("pair_free_a")
        gate_max = sem("gate_max")
        gate_q, gate_t, gate_s, gated, gated_max = (
            sem(s) for s in ("gate_q", "gate_t", "gate_s", "gated", "gated_max"))
        up_q, gated_q, prod, prod_max = sem("up_q"), sem("gated_q"), sem("prod"), sem("prod_max")
        o_int, o_hi, o_lo = sem("o_int"), sem("o_hi"), sem("o_lo")
        xt_ps, xt_sb, down, x2_new, x2_hi, x2_lo, x2_tr, x2_tok = (
            sem(s) for s in ("xt_ps", "xt_sb", "down", "x2_new", "x2_hi", "x2_lo", "x2_tr", "x2_tok"))
        e_hi, e_lo = sem("e_hi"), sem("e_lo")
        b1_tr, b1_ready = sem("b1_tr"), sem("b1_ready")
        r_sum, r_tanh, r_hi, r_lo = sem("r_sum"), sem("r_tanh"), sem("r_hi"), sem("r_lo")
        d_const, empty_made, d_rows, d_pairs = sem("d_const"), sem("empty_made"), sem("d_rows"), sem("d_pairs")
        d_super = [sem(f"d_super{i}") for i in range(SUPERS)]
        placed_sum, row_ps, row_copied, row_tail, row_idx, filled = (
            sem(s) for s in ("placed_sum", "row_ps", "row_copied", "row_tail", "row_idx", "filled"))
        table, rows_go, result_go = sem("table"), sem("rows_go"), sem("result_go")
        u_load = [sem(f"u_load{i}") for i in range(RING)]
        u_out = [sem(f"u_out{i}") for i in range(RING)]
        u_tr, u_xt, u_up, u_gelu, u_hi, u_lo, u_down, u_y, u_dst = (
            sem(s) for s in ("u_tr", "u_xt", "u_up", "u_gelu", "u_hi", "u_lo", "u_down", "u_y", "u_dst"))
        summed = sem("summed")
        up1, gelu, split_hi, split_lo, down1, added = (
            sem(s) for s in ("up1", "gelu", "split_hi", "split_lo", "down1", "added"))
        route, route_step, route_z, route_e, w9_done, w9_tr, w9t_done, route_c, carried = (
            sem(s) for s in ("route", "route_step", "route_z", "route_e", "w9_done", "w9_tr", "w9t_done", "route_c", "carried"))

        CONSTS = 6 + (2 + BIAS_SLOTS0 - 1 + 2) + (2 + BIAS_SLOTS1 - 1 + 2) + 2 + 4
        PREP0 = 15
        PREP1 = PREP0 + 6
        ROUTE_STEPS = 18
        TABLE_STEPS = 16
        (C_SH, C_IH, C_U, C_SG, C_IG, C_SGH, C_SG16, C_S2, C_F2, C_SU, C_ISU, C_FU, C_S3, C_F3, C_OUT,
         C_T1, C_T2, C_T3, C_T4, C_R) = range(20)

        def col(c):
            return sc[:, c:c + 1]

        x_dram, out_dram = a["x"], out
        block = ctx.enter_context(nc.Block())

        @block.sync
        def _(sp):
            sp.dma_start(cond_n[:, :], a["cond_1024"]).then_inc(d_cond, 16)
            first = TILES // 8
            for j0, j1, s in ((0, first, d_x0), (first, TILES, d_x1)):
                for tt in range(2):
                    sp.dma_start(xn[tt * N:(tt + 1) * N, j0:j1, :],
                                 x_dram.rearrange("n (j tt) d -> tt n j d", tt=2)[tt, :, j0:j1, :]).then_inc(s, 16)
                if j0 == 0:
                    for dst, name in ((wx_raw, "L0_cond_Wx"), (wh_raw, "L0_cond_Wh")):
                        sp.dma_start(dst.rearrange("p (k c) -> p k c", k=KD),
                                     a[name].rearrange("(k p) c -> p k c", p=P)).then_inc(d_w0, 16)
                    b0 = a["L0_cond_b"].rearrange("(g c) -> g c", c=P)
                    b1 = a["L1_cond_b"].rearrange("(g c) -> g c", c=P)
                    for half in range(2):
                        at = half * BIAS_SLOTS0
                        sp.dma_start(braw0[at:at + 4, :], b0[0:4, :]).then_inc(d_b, 16)
                        sp.dma_start(braw0[at + 4:at + 6, :], b0[6:8, :]).then_inc(d_b, 16)
                        sp.dma_start(braw0[at + 6:at + 8, :], b0[4:6, :]).then_inc(d_b, 16)
                        at = half * BIAS_SLOTS1
                        sp.dma_start(braw1[at:at + BIAS_SLOTS1, :], b1).then_inc(d_b, 16)
            sp.dma_start(wn[:, 0:IT, :], a["L0_ffn_w_gate"].rearrange("(q p) c -> p q c", p=P)).then_inc(d_ffn, 16)
            sp.dma_start(wn[:, IT:2 * IT, :], a["L0_ffn_w_up"].rearrange("(q p) c -> p q c", p=P)).then_inc(d_ffn, 16)
            sp.dma_start(wn[:, 2 * IT:3 * IT, :].rearrange("p (o s) c -> p o (s c)", o=KD),
                         a["L0_ffn_w_down"].rearrange("(o p) c -> p o c", p=P)).then_inc(d_ffn, 16)
            for dst, name in ((rx_raw, "L1_cond_Wx"), (rh_raw, "L1_cond_Wh")):
                sp.dma_start(dst.rearrange("p (k c) -> p k c", k=KD),
                             a[name].rearrange("(k p) c -> p k c", p=P)).then_inc(d_rnn, 16)
            sp.dma_start(wr_raw[:, :].rearrange("p (k c) -> p k c", k=KD),
                         a["L1_ffn_router_w"].rearrange("(k p) c -> p k c", p=P)).then_inc(d_rnn, 16)
            sp.dma_start(rb_all[:, :], a["L1_ffn_router_b"].rearrange("(a e) -> a e", a=1).broadcast_to([P, E])).then_inc(d_rnn, 16)
            sp.dma_start(consts[:, :], a["consts"]).then_inc(d_const, 16)
            sp.dma_start(b1_n[0:E * HT, :], a["L1_ffn_rb1"].rearrange("e (h c) -> (e h) c", c=P)).then_inc(d_moe_small, 16)
            sp.dma_start(b1_n[E * HT:SLOTS * HT, :], a["L1_ffn_sb1"].rearrange("(h c) -> h c", c=P)).then_inc(d_moe_small, 16)
            sp.dma_start(b2_all[0:E, :], a["L1_ffn_rb2"]).then_inc(d_moe_small, 16)
            sp.dma_start(b2_all[E:SLOTS, :], a["L1_ffn_sb2"].rearrange("(a c) -> a c", a=1)).then_inc(d_moe_small, 16)

            w1_v = a["L1_ffn_rw1"].rearrange("e (k p) c -> p e k c", p=P)
            w2_v = a["L1_ffn_rw2"].rearrange("e (k p) c -> p e k c", p=P)
            st1 = stage[:, 0, :].rearrange("p (k c) -> p k c", k=KD)
            st2 = stage[:, 1, :].rearrange("p (k c) -> p k c", k=HT)
            sp.wait_ge(down, 4 * CH)
            sp.wait_ge(x2_tok, 4 * CH)
            for q in range(SLOTS):
                e = (q + E) % SLOTS
                s1 = w1_v[:, e] if e < E else a["L1_ffn_sw1"].rearrange("(k p) c -> p k c", p=P)
                s2 = w2_v[:, e] if e < E else a["L1_ffn_sw2"].rearrange("(k p) c -> p k c", p=P)
                for m, (dst, src) in enumerate(((st1, s1), (st2, s2))):
                    if q:
                        sp.wait_ge(e_lo, 2 * q + m - 1)
                    sp.dma_start(dst, src).then_inc(d_stage[m], 16)
            sp.wait_ge(d_rows, 16 * (TOP_K * TILES + HALVES * E + 1))
            sp.wait_ge(table, TABLE_STEPS)

            def load(i, u):
                tile = sp.value_load(unit_i[0:1, 1, ds(i, 1)], min_val=0, max_val=E * REGION // UROWS + DUMMY - 1)
                sp.dma_start(xr[u].bitcast(I16), rows_dram.rearrange("(a h p) c -> p a h c", h=HALVES, p=P)[
                    :, ds(tile, 1), :, :].rearrange("p a h c -> p (a h) c")).then_inc(u_load[u], 16)

            for u in range(RING):
                load(u, u)
            with sp.Fori(1, UNITS // RING) as g:
                for u in range(RING):
                    sp.wait_ge(u_dst, RING * g + u - RING + 1)
                    load(RING * g + u, u)
            sp.wait_ge(u_down, UNITS)
            sp.wait_ge(u_y, UNITS)
            for u in range(RING):
                sp.wait_ge(u_out[u], 16 * HALVES * (UNITS // RING))
            for s in range(SUPERS):
                for tt in range(2):
                    sp.dma_start(pairs[tt * N:(tt + 1) * N, s, :, :],
                                 pairs_dram.rearrange("(n j tt two) d -> tt n j (two d)", tt=2, two=2, n=N)[
                                     tt, :, 4 * s:4 * s + 4, :]).then_inc(d_super[s], 16)
            for s in range(SUPERS):
                sp.wait_ge(summed, 2 * s + 2)
                for tt in range(2):
                    sp.dma_start(out_dram.rearrange("n (j tt) d -> tt n j d", tt=2)[tt, :, 4 * s:4 * s + 4, :],
                                 xn[tt * N:(tt + 1) * N, 4 * s:4 * s + 4, :]).then_inc(d_out, 16)
            sp.wait_ge(d_out, 16 * 2 * SUPERS)

        @block.gpsimd
        def _(pool):
            n = 0

            def step(ins):
                nonlocal n
                n += 1
                ins.then_inc(const_step, 1)
                pool.wait_ge(const_step, n)

            step(pool.memset(ident[:, :], 0.0))
            step(pool.affine_select(out=ident[:, :], in_=ident[:, :], compare_op=ALU.not_equal, fill=1.0,
                                    base=0, pattern=[[-1, P]], channel_multiplier=1))
            pool.memset(ones_row[:, :], 1.0).then_inc(const_step, 1)
            n += 1
            step(pool.memset(sel0[:, :], WS / 2))
            step(pool.memset(sel0[:, 4 * N:6 * N], WS))
            step(pool.memset(sel1[:, :], WS))
            for sel, slots, neg in ((sel0, BIAS_SLOTS0, nlow0), (sel1, BIAS_SLOTS1, nlow1)):
                v = sel[:, :].rearrange("q (s n) -> q s n", n=N)
                step(pool.affine_select(out=v, in_=v, compare_op=ALU.is_ge, fill=0.0, base=0,
                                        pattern=[[-1, slots], [0, N]], channel_multiplier=1))
                step(pool.affine_select(out=v, in_=v, compare_op=ALU.is_ge, fill=0.0, base=slots,
                                        pattern=[[1, slots], [0, N]], channel_multiplier=-1))
                for between in range(1, slots):
                    step(pool.affine_select(out=v, in_=v, compare_op=ALU.not_equal, fill=0.0, base=-between,
                                            pattern=[[-1, slots], [0, N]], channel_multiplier=1))
                step(pool.memset(neg[:, :], -1.0))
                step(pool.affine_select(out=neg[:, :], in_=neg[:, :], compare_op=ALU.is_ge, fill=0.0, base=-slots,
                                        pattern=[[0, 1]], channel_multiplier=1))
            step(pool.memset(before[:, :, :], 1.0))
            step(pool.affine_select(out=before[:, :, :], in_=before[:, :, :], compare_op=ALU.is_gt, fill=0.0,
                                    base=0, pattern=[[1, E], [-1, E]], channel_multiplier=0))
            step(pool.tensor_copy(ident16[:, :], ident[:, :]))
            step(pool.memset(ones16[:, :], 1.0))
            step(pool.memset(tri16[:, :], 1.0))
            step(pool.affine_select(out=tri16[:, :], in_=tri16[:, :], compare_op=ALU.is_gt, fill=0.0, base=0,
                                    pattern=[[1, P]], channel_multiplier=-1))
            assert n == CONSTS, n

            pool.wait_ge(d_x0, 32)
            for slot in range(2):
                pool.tensor_copy(xs[:, slot, :], xn[:, slot, :]).then_inc(x_staged, 1)
            pool.wait_ge(d_x1, 32)
            with pool.Fori(1, TILES // 2) as i:
                for slot in range(2):
                    pool.wait_ge(x_tr, 2 * i + slot - 1)
                    pool.tensor_copy(xs[:, slot, :], xn[:, ds(2 * i + slot, 1), :].rearrange("p a c -> p (a c)")
                                     ).then_inc(x_staged, 1)
            pool.wait_ge(m_step, 23)
            pool.tensor_copy(xs[:, :, :], xn[:, 0:4, :]).then_inc(xs_ready, 1)
            with pool.Fori(1, 2 * CH) as h:
                pool.wait_ge(xt_ps, 2 * h)
                pool.tensor_copy(xs[:, :, :], xn[:, ds(4 * h, 4), :]).then_inc(xs_ready, 1)

            pool.wait_ge(down, 4 * CH)
            pool.memset(empty[:, :], 0.0).then_inc(empty_made, 1)
            pool.wait_ge(empty_made, 1)
            pool.memset(empty32[:, DST_AT:DST_AT + SLOTS], NOWHERE).then_inc(empty_made, 1)
            pool.memset(rows32[:, :, DST_AT + E:DST_AT + SLOTS], NOWHERE).then_inc(empty_made, 1)
            pool.wait_ge(empty_made, 3)
            pool.dma_start(rows_dram.rearrange("(a p) c -> p a c", p=P)[:, E * REGION // P:, :],
                           empty.bitcast(I16).unsqueeze(1).broadcast_to([P, DUMMY * HALVES, ROW])).then_inc(d_rows, 16)

            def to_rows(src, index):
                pool.indirect_dma_start(rows_dram[:, :], bass.IndirectOffsetOnAxis(index, 0), src, None,
                                        bounds_check=E * REGION - 1, oob_is_err=False).then_inc(d_rows, 16)

            with pool.Fori(0, SUPERS) as s:
                pool.wait_ge(row_idx, s + 1)
                pool.wait_ge(row_tail, 2 * s + 2)
                pool.wait_ge(row_copied, 2 + 2 * s + 2)
                pool.sem_inc(rows_go, 1)
                for tt in range(4):
                    for j in range(TOP_K):
                        to_rows(rows[:, tt, :].bitcast(I16), row_j[:, tt, j:j + 1])
            pool.wait_ge(filled, HALVES)
            for e in range(HALVES * E):
                to_rows(empty.bitcast(I16), fill_i[:, e:e + 1])

            with pool.Fori(0, UNITS // RING) as g:
                for u in range(RING):
                    pool.wait_ge(u_y, RING * g + u + 1)
                    pool.wait_ge(u_dst, RING * g + u + 1)
                    pool.sem_inc(result_go, 1)
                    for h in range(HALVES):
                        at = HALVES * u + h
                        pool.indirect_dma_start(pairs_dram[:, :], bass.IndirectOffsetOnAxis(dst_i[:, at:at + 1], 0),
                                                yr[u][:, h * D:(h + 1) * D], None, bounds_check=TOP_K * T * N - 1,
                                                oob_is_err=False).then_inc(u_out[u], 16)

        @block.tensor
        def _(pe):
            pe.wait_ge(const_step, 3)
            pe.wait_ge(d_cond, 16)
            for k in range(KD):
                mm = pe.transpose(ps[:, 6, k * N:(k + 1) * N], cond_n[:, k * P:(k + 1) * P], ident[0:N, 0:N])
            mm.then_inc(cond_t, 1)
            def x_transpose(j, slot):
                pe.wait_ge(x_staged, j + 1)
                for k in range(KD):
                    mm = pe.transpose(ps[:, 4 + slot, k * P:(k + 1) * P], xs[:, slot, k * P:(k + 1) * P], ident[:, :])
                mm.then_inc(x_tr, 1)

            def gate_ps(u, s):
                return ps[:, u, s * N:(s + 1) * N] if s < 6 else ps[:, 2 + u, (s - 6) * N:(s - 5) * N]

            def x_part(u, slot, wait):
                if wait is not None:
                    pe.wait_ge(xt_lo, wait)
                pe.matmul(ps[:, u, 0:6 * N], brow0, sel0[:, 0:6 * N], start=True, stop=False, skip_group_check=True)
                pe.matmul(ps[:, 2 + u, 0:2 * N], brow0, sel0[:, 6 * N:8 * N], start=True, stop=False,
                          skip_group_check=True)
                for s, g in enumerate(GATE_ORDER):
                    o = gate_ps(u, s)
                    for k in range(KD):
                        cols = slice(k * GATES + g * P, k * GATES + (g + 1) * P)
                        hi = xt[:, slot, 0, k * P + u * N:k * P + (u + 1) * N]
                        lo = xt[:, slot, 1, k * P + u * N:k * P + (u + 1) * N]
                        for w, v in ((wx_h, hi), (wx_l, hi), (wx_h, lo)):
                            pe.matmul(o, w[:, cols], v, start=False, stop=False, skip_group_check=True)

            def h_part(t, u):
                pe.wait_ge(h_hi, t + 1)
                for slots in (range(6), range(6, 8)):
                    for low in (0, 1):
                        if low and slots[0] == 0:
                            pe.wait_ge(h_lo, t + 1)
                        for s in slots:
                            g = GATE_ORDER[s]
                            o = gate_ps(u, s)
                            for k in range(KD):
                                cols = slice(k * GATES + g * P, k * GATES + (g + 1) * P)
                                v = hb[:, u, low, k * N:(k + 1) * N]
                                for w in ((wh_h,) if low else (wh_h, wh_l)):
                                    mm = pe.matmul(o, w[:, cols], v, start=False, stop=low == 1, skip_group_check=True)
                    mm.then_inc(ifg_done if slots[0] == 0 else o_done, 1)

            def lstm_turn(i, weights, last):
                x_transpose(2 * i + 1, 1)
                h_part(4 * i, 0)
                x_part(1, 0, None)
                h_part(4 * i + 1, 1)
                x_part(0, 1, 2 * i + 2)
                if not last:
                    x_transpose(2 * i + 2, 0)
                h_part(4 * i + 2, 0)
                x_part(1, 1, None)
                h_part(4 * i + 3, 1)
                if not last:
                    x_part(0, 0, 2 * i + 3)
                if weights:
                    pe.wait_ge(wq_step, 5 * i + 5)
                    for q in range(4):
                        mm = pe.transpose(ps[:, 6, q * P:(q + 1) * P], wd[:, q * P:(q + 1) * P], ident[:, :])
                    mm.then_inc(w_tr, 1)

            x_transpose(0, 0)
            pe.wait_ge(prep_v, PREP0)
            x_part(0, 0, 1)
            with pe.Fori(0, PIECES // 2) as i:
                lstm_turn(i, True, False)
            with pe.Fori(PIECES // 2, T // 4 - 1) as i:
                lstm_turn(i, False, False)
            lstm_turn(T // 4 - 1, False, True)

            def spread(n):
                pe.wait_ge(m_col, n + 1)
                pe.transpose(ps[0:1, 7, 0:P], colmax[:, n:n + 1], ident[:, :]).then_inc(m_row, 1)
                pe.wait_ge(m_top, n + 1)
                pe.matmul(ps[:, 7, 256 + n:257 + n], ones_row[:, :], top[:, n:n + 1],
                          start=True, stop=True).then_inc(m_all, 1)

            def ffn_pass(first_piece, *free):
                with pe.Fori(0, CH) as cc:
                    for it in range(IT):
                        for s, base in free:
                            pe.wait_ge(s, base + 1 + IT * cc + it)
                        piece = first_piece + it
                        for half in range(2):
                            o = ps[:, 2 * (it % 3) + half, :]
                            r = [v[:, :, ds(16 * cc + 8 * half, 8), :] for v in (xh_v, xl_v)]
                            n = 0
                            for k in range(KD):
                                for w, x in ((wt_h, 0), (wt_l, 0), (wt_h, 1)):
                                    mm = pe.matmul(o, w[:, piece, k * P:(k + 1) * P], r[x][:, k, :, :],
                                                   start=n == 0, stop=n == 5)
                                    n += 1
                        mm.then_inc(pair_done, 1)

            spread(0)
            pe.wait_ge(wt_lo_done, PIECES // 2)
            pe.wait_ge(xq_lo, 8)
            ffn_pass(0, (pair_free_a, 0))
            spread(1)
            pe.wait_ge(pair_free_a, 3 + BLOCKS)
            ffn_pass(IT, (pair_free_v, 0))
            spread(2)
            spread(3)
            pe.wait_ge(pair_free_v, 3 + BLOCKS)
            ffn_pass(IT, (pair_free_a, BLOCKS))
            spread(4)

            def down_turn(cc, first):
                for half in range(2):
                    for ot in range(KD):
                        if not (first and half == 0):
                            pe.wait_ge(xt_sb, 4 * cc + 2 * half + ot - 1)
                        pe.wait_ge(xs_ready, 2 * cc + half + 1)
                        for c in range(4):
                            mm = pe.transpose(ps[:, 2 + ot, c * P:(c + 1) * P], xs[:, c, ot * P:(ot + 1) * P],
                                              ident[:, :])
                        mm.then_inc(xt_ps, 1)
                    for ot in range(KD):
                        if not (first and half == 0):
                            pe.wait_ge(x2_new, 4 * cc + 2 * half + ot - 1)
                        n = 0
                        for it in range(IT):
                            if half == 0 and ot == 0:
                                pe.wait_ge(o_lo, IT * cc + it + 1)
                            piece = 2 * IT + ot * (I0 // D) + it // 2
                            cols = slice((it % 2) * P, (it % 2 + 1) * P)
                            at = [(IT * cc + it) * 2 * BLOCK + v * BLOCK + half * 512 for v in range(2)]
                            for w, x in ((wt_h, 0), (wt_l, 0), (wt_h, 1)):
                                mm = pe.matmul(ps[:, ot, :], w[:, piece, cols], big16[:, ds(at[x], 512)],
                                               start=n == 0, stop=n == 3 * IT - 1)
                                n += 1
                        mm.then_inc(down, 1)
                        if not (first and half == 0 and ot == 0):
                            x2_transpose(4 * cc + 2 * half + ot - 1, 1 - ot, first and half == 0)

            def x2_transpose(unit, ot, no_wait):
                pe.wait_ge(x2_new, unit + 1)
                if not no_wait:
                    pe.wait_ge(x2_tok, unit - 1)
                for c in range(4):
                    mm = pe.transpose(ps[:, 4 + ot, c * P:(c + 1) * P], x2s[ot][:, c * P:(c + 1) * P], ident[:, :])
                mm.then_inc(x2_tr, 1)

            down_turn(0, True)
            with pe.Fori(1, CH) as cc:
                down_turn(cc, False)
            x2_transpose(4 * CH - 1, 1, False)

            pe.wait_ge(d_moe_small, 64)
            pe.transpose(ps[:, 7, 0:SLOTS * HT], b1_n[:, :], ident[0:SLOTS * HT, 0:SLOTS * HT]).then_inc(b1_tr, 1)
            pe.wait_ge(x2_lo, 4 * CH)

            def rnn_step(t, first=False):
                if not first:
                    pe.wait_ge(r_hi, t)
                pe.matmul(ps[:, 6, 0:SC], brow1[:, :], sel1[:, :], start=True, stop=False, skip_group_check=True)

                def products(wh, wl, hi, lo, last):
                    for low in (0, 1):
                        for o in range(KD):
                            for k in range(KD):
                                cols = slice(k * D + o * P, k * D + (o + 1) * P)
                                for w in ((wh,) if low else (wh, wl)):
                                    mm = pe.matmul(ps[:, 6, o * N:(o + 1) * N], w[:, cols], (lo if low else hi)(k),
                                                   start=False, stop=last and low == 1, skip_group_check=True)
                    return mm

                def at(v, when):
                    return lambda k: v[:, ds(k * T * N + when * N, N)]

                products(rx_h, rx_l, at(xh, t), at(xl, t), False)
                if first:
                    mm = products(rh_h, rh_l, lambda k: r0[:, 0, k * N:(k + 1) * N],
                                  lambda k: r0[:, 1, k * N:(k + 1) * N], True)
                else:
                    pe.wait_ge(r_lo, t)
                    mm = products(rh_h, rh_l, at(xh, t - 1), at(xl, t - 1), True)
                mm.then_inc(r_sum, 1)

            rnn_step(0, True)
            with pe.Fori(1, SUPER_T) as t:
                rnn_step(t)

            def superchunk(c, with_rnn):
                def rnn(r):
                    if with_rnn:
                        rnn_step(SUPER_T * c + SUPER_T + r)

                def tokens(v, tt, k):
                    return v[:, ds(k * T * N + (SUPER_T * c + 2 * tt) * N, P)]

                pe.wait_ge(added, 2 * c + 1)
                pe.wait_ge(w9t_done, c + 1)
                for tt in range(4):
                    n = 0
                    for k in range(KD):
                        for w, v in ((wr_h, xh), (wr_l, xh), (wr_h, xl)):
                            mm = pe.matmul(ps[:, 7, tt * E:(tt + 1) * E], tokens(v, tt, k),
                                           w[:, k * E:(k + 1) * E], start=n == 0 and tt == 0, stop=n == 5,
                                           skip_group_check=True)
                            n += 1
                mm.then_inc(route, 1)
                rhs = [v[:, :, ds(SUPER_T * c, SUPER_T), :] for v in (xh_v, xl_v)]
                for ht in range(HT):
                    pe.wait_ge(gelu, 4 * c + ht + 1)
                    if ht < 2:
                        pe.wait_ge(row_copied, 2 * c + ht + 1)
                    n = 0
                    for k in range(KD):
                        for low, x in ((0, 0), (1, 0), (0, 1)):
                            at = E * EXP + low * 1024 + k * H1 + ht * P
                            mm = pe.matmul(ps[:, ht, :], big16[:, at:at + P], rhs[x][:, k, :, :], start=n == 0, stop=n == 5)
                            n += 1
                    mm.then_inc(up1, 1)
                    rnn(ht)
                pe.wait_ge(route_c, c + 1)
                pe.wait_ge(gelu, 4 * c + 4 + 2)
                for tt in range(5):
                    o = ps[:, 7, 64 + tt * E:64 + (tt + 1) * E]
                    if tt < 4:
                        mm = pe.matmul(o, tri16[:, :], chosen[:, tt, :], start=tt == 0, stop=tt == 0, skip_group_check=True)
                    for before_ in range(tt):
                        mm = pe.matmul(o, ones16[:, :], chosen[:, before_, :], start=False, stop=before_ == tt - 1,
                                       skip_group_check=True)
                mm.then_inc(placed_sum, 1)
                for b in range(2):
                    for t2 in range(2):
                        for part_, v in enumerate((xh, xl)):
                            for k in range(KD):
                                at = t2 * 512 + part_ * D + k * P
                                mm = pe.transpose(ps[:, b, :].bitcast(F16)[:, at:at + P], tokens(v, 2 * b + t2, k),
                                                  ident16[:, :])
                    mm.then_inc(row_ps, 1)
                rnn(4)
                pe.wait_ge(w9_done, c + 1)
                pe.wait_ge(row_idx, c + 1)
                for tt in range(4):
                    mm = pe.transpose(ps[0:SLOTS, 7, tt * P:(tt + 1) * P], w9[:, tt, :], ident[:, :])
                mm.then_inc(w9_tr, 1)
                pe.wait_ge(split_lo, 2 + 4 * c + 4)
                for tt in range(4):
                    b, o = tt // 2, ps[:, 4 + tt // 2, (tt % 2) * D:(tt % 2 + 1) * D]
                    n = 0
                    for ht in range(HT):
                        for hp, wp in ((0, 0), (0, 1), (1, 0)):
                            at = E * EXP + 2048 + wp * 1024 + ht * D
                            pe.matmul(o, h1(hp, ht)[:, tt * P:(tt + 1) * P], big16[:, at:at + D],
                                      start=n == 0 and tt % 2 == 0, stop=False, skip_group_check=True)
                            n += 1
                    if tt == 0:
                        pe.wait_ge(w9t_done, c + 2)
                    mm = pe.matmul(o, w9t[:, tt * P:(tt + 1) * P], b2_all[:, :], start=False, stop=True,
                                   skip_group_check=True)
                    if tt % 2:
                        mm.then_inc(down1, 1)
                    if tt < 3:
                        rnn(5 + tt)

            pe.wait_ge(r_hi, SUPER_T)
            pe.wait_ge(r_lo, SUPER_T)
            pe.wait_ge(b1_ready, 1)
            pe.wait_ge(e_lo, 2)
            with pe.Fori(0, SUPERS - 1) as c:
                superchunk(c, True)
                pe.wait_ge(r_lo, SUPER_T * c + 2 * SUPER_T)
            superchunk(SUPERS - 1, False)

            pe.wait_ge(e_lo, 2 * SLOTS)
            pe.wait_ge(table, TABLE_STEPS)
            pe.wait_ge(row_copied, 2 + 2 * SUPERS)
            pe.wait_ge(gelu, 4 + 4 * SUPERS)
            pe.wait_ge(added, 2 * SUPERS + 1)

            def expert(i):
                return pe.value_load(unit_i[0:1, 0, ds(i, 1)], min_val=0, max_val=E)

            def unit_transpose(i, g, u):
                pe.wait_ge(u_load[u], 16 * g + 16)
                if not (isinstance(i, int) and i < 2):
                    pe.wait_ge(u_xt, i - 1)
                for part_ in range(2):
                    for k in range(KD):
                        for h in range(HALVES):
                            at = ((part_ * KD + k) * HALVES + h) * P
                            mm = pe.transpose(ps[:, 4 + u % 2, :].bitcast(F16)[:, at:at + P],
                                              xr[u][:, h, (part_ * KD + k) * P:(part_ * KD + k + 1) * P], ident16[:, :])
                mm.then_inc(u_tr, 1)

            def unit_up(i, u, e):
                pe.wait_ge(u_xt, i + 1)
                for ht in range(HT):
                    if ht % 2 == 0 and not (isinstance(i, int) and i < 2):
                        pe.wait_ge(u_gelu, 2 * i - 3 + ht // 2)
                    n = 0
                    for k in range(KD):
                        for low, x in ((0, 0), (1, 0), (0, 1)):
                            at = (x * KD + k) * UROWS
                            mm = pe.matmul(ps[:, 2 * (u % 2) + ht // 2, (ht % 2) * UROWS:(ht % 2 + 1) * UROWS],
                                           big16[:, ds(e * EXP + low * 1024 + k * H1 + ht * P, P)],
                                           xrt[u % 2][:, at:at + UROWS], start=n == 0 and ht % 2 == 0, stop=n == 5,
                                           skip_group_check=True)
                            n += 1
                    if ht % 2:
                        mm.then_inc(u_up, 1)

            def unit_down(i, u, e):
                pe.wait_ge(u_lo, 2 * i + 2)
                if not (isinstance(i, int) and i < 2):
                    pe.wait_ge(u_y, i - 1)
                n = 0
                for ht in range(HT):
                    for hp, wp in ((0, 0), (0, 1), (1, 0)):
                        for h in range(HALVES):
                            at = hp * H + ht * UROWS + h * P
                            mm = pe.matmul(ps[:, 6 + u % 2, h * D:(h + 1) * D], h1r[u % 2][:, at:at + P],
                                           big16[:, ds(e * EXP + 2048 + wp * 1024 + ht * D, D)],
                                           start=n == 0, stop=n >= 22, skip_group_check=True)
                            n += 1
                mm.then_inc(u_down, 1)

            unit_transpose(0, 0, 0)
            unit_transpose(1, 0, 1)
            unit_up(0, 0, expert(0))

            def units(g, last):
                now = expert(RING * g)
                for u in range(RING):
                    i = RING * g + u
                    if not (last and u + 2 >= RING):
                        unit_transpose(i + 2, g + (u + 2) // RING, (u + 2) % RING)
                    if not (last and u + 1 >= RING):
                        then = expert(i + 1)
                        unit_up(i + 1, (u + 1) % RING, then)
                    unit_down(i, u, now)
                    now = then

            units(0, False)
            with pe.Fori(1, UNITS // RING - 1) as g:
                units(g, False)
            units(UNITS // RING - 1, True)

        @block.scalar
        def _(act):
            act.sem_inc(pair_free_a, 3)
            act.sem_inc(gelu, 4)
            act.sem_inc(row_copied, 2)

            def x_high(n, slot):
                act.wait_ge(x_tr, n)
                act.activation(xt[:, slot, 0, :], ps[:, 4 + slot, 0:KD * P], ACT.Copy).then_inc(xt_hi, 1)

            def lstm_step(t, u):
                act.wait_ge(ifg_done, t + 1)
                act.activation(tg[:, 0:6 * N], ps[:, u, 0:6 * N], ACT.Tanh, scale=1 / WS).then_inc(ifg_tanh, 1)
                act.wait_ge(o_done, t + 1)
                act.activation(tg[:, 6 * N:8 * N], ps[:, 2 + u, 0:2 * N], ACT.Tanh, scale=1 / WS).then_inc(o_tanh, 1)
                act.wait_ge(c_done, t + 1)
                act.activation(tc, cstate[:, 0:SC], ACT.Tanh, scale=0.5).then_inc(c_tanh, 1)

            def lstm_turn(i, weights, last):
                for r in range(4):
                    lstm_step(4 * i + r, r % 2)
                    if r == 0:
                        x_high(2 * i + 2, 1)
                    if r == 2 and not last:
                        x_high(2 * i + 3, 0)
                if weights:
                    act.wait_ge(w_tr, i + 1)
                    act.activation(wt_h[:, ds(2 * i, 2), :], ps[:, 6, :].rearrange("p (q c) -> p q c", q=2), ACT.Copy,
                                   scale=WS).then_inc(wt_hi_done, 1)

            x_high(1, 0)
            with act.Fori(0, PIECES // 2) as i:
                lstm_turn(i, True, False)
            with act.Fori(PIECES // 2, T // 4 - 1) as i:
                lstm_turn(i, False, False)
            lstm_turn(T // 4 - 1, False, True)

            act.wait_ge(m_step, 2)
            for c in range(8):
                if c >= 2:
                    act.wait_ge(xq_lo, c - 1)
                act.activation(qb[c % 2], hs[:, c * BLOCK:(c + 1) * BLOCK], ACT.Copy, scale=col(C_IH)).then_inc(xq_int, 1)

            def pair(it):
                return ps[:, 2 * (it % 3):2 * (it % 3) + 2, :].rearrange("p b c -> p (b c)")

            def blk(p):
                return big[:, ds(p * BLOCK, BLOCK)]

            act.wait_ge(m_step, 4)
            act.wait_ge(xq_lo, 8)
            act.wait_ge(prep_v, PREP1)
            with act.Fori(0, CH) as cc:
                for it in range(IT):
                    act.wait_ge(pair_done, IT * cc + it + 1)
                    act.activation(blk(IT * cc + it), pair(it), ACT.Copy, scale=col(C_U)).then_inc(pair_free_a, 1)
            act.wait_ge(m_step, 9)
            act.wait_ge(pair_free_a, 3 + BLOCKS)
            with act.Fori(0, CH) as cc:
                for it in range(IT):
                    p = IT * cc + it
                    act.wait_ge(gated, p + 1)
                    act.activation(qb[it % 2], blk(p), ACT.Copy, scale=col(C_IG)).then_inc(gate_q, 1)
                    act.wait_ge(m_step, 8)
                    act.wait_ge(gate_q, p + 1)
                    act.activation(blk(p), qb[it % 2], ACT.Tanh, scale=col(C_SGH)).then_inc(gate_t, 1)
                    act.wait_ge(m_step, 8)
                    act.wait_ge(gate_t, p + 1)
                    act.activation(sq[it % 2], blk(p), ACT.Copy, bias=32768.0, scale=32768.0).then_inc(gate_s, 1)
            act.wait_ge(m_step, 18)
            with act.Fori(0, CH) as cc:
                for it in range(IT):
                    p = IT * cc + it
                    act.wait_ge(pair_done, 2 * BLOCKS + p + 1)
                    act.wait_ge(prod, p + 1)
                    act.activation(qb[it % 2], pair(it), ACT.Copy, scale=col(C_FU)).then_inc(pair_free_a, 1)
                    act.activation(tmp_i[:, (2 + it % 2) * BLOCK:(3 + it % 2) * BLOCK], blk(p), ACT.Copy,
                                   scale=col(C_F2)).then_inc(gated_q, 1)

            act.wait_ge(m_step, 23)

            def down_turn(cc, first):
                for it in range(IT):
                    p = IT * cc + it
                    if not (first and it < 2):
                        act.wait_ge(o_lo, p - 1)
                    act.activation(qb[it % 2], blk(p), ACT.Copy, scale=col(C_F3)).then_inc(o_int, 1)
                for half in range(2):
                    for ot in range(KD):
                        n = 4 * cc + 2 * half + ot
                        act.wait_ge(xt_ps, n + 1)
                        if not (first and half == 0):
                            act.wait_ge(x2_new, n - 1)
                        act.activation(xts[ot], ps[:, 2 + ot, :], ACT.Copy).then_inc(xt_sb, 1)
                        if not (first and half == 0 and ot == 0):
                            x2_token(n - 1, 1 - ot, (cc if ot or half else cc - 1), (half if ot else 1 - half))

            def x2_token(n, ot, cc, half):
                act.wait_ge(x2_tr, n + 1)
                act.activation(xn[:, ds(8 * cc + 4 * half, 4), ot * P:(ot + 1) * P],
                               ps[:, 4 + ot, :].rearrange("p (c d) -> p c d", c=4), ACT.Copy).then_inc(x2_tok, 1)

            down_turn(0, True)
            with act.Fori(1, CH) as cc:
                down_turn(cc, False)
            x2_token(4 * CH - 1, 1, CH - 1, 1)

            act.wait_ge(b1_tr, 1)
            act.activation(b1_t[:, :], ps[:, 7, 0:SLOTS * HT], ACT.Copy).then_inc(b1_ready, 1)
            act.wait_ge(b1_ready, 1)

            def rnn_tanh(t):
                act.wait_ge(r_sum, t + 1)
                act.activation(hr[:, :], ps[:, 6, 0:SC], ACT.Tanh, scale=1 / WS).then_inc(r_tanh, 1)

            def expert_high(q, e, m):
                act.wait_ge(d_stage[m], 16 * q + 16)
                act.activation(big16[:, ds(e * EXP + m * 2048, 1024)], stage[:, m, :], ACT.Copy,
                               scale=WS).then_inc(e_hi, 1)

            for q in range(EARLY_FILLS):
                for m in range(2):
                    expert_high(q, (q + E) % SLOTS, m)
                    rnn_tanh(2 * q + m)

            def superchunk(c, with_rnn, with_fill):
                def rnn(r):
                    if with_rnn:
                        rnn_tanh(SUPER_T * c + SUPER_T + r)

                act.wait_ge(route_z, c + 1)
                act.activation(ee[:, :, :], zz[:, :, :], ACT.Exp).then_inc(route_e, 1)
                for ht in range(HT):
                    act.wait_ge(up1, 4 * c + ht + 1)
                    act.wait_ge(split_lo, 4 * c + ht + 1)
                    act.activation(hf[ht % 2], ps[:, ht, :], ACT.Gelu, scale=1 / WS,
                                   bias=b1_t[:, HT * E + ht:HT * E + ht + 1]).then_inc(gelu, 1)
                    rnn(ht)
                rnn(4)
                for b in range(2):
                    act.wait_ge(row_ps, 2 * c + b + 1)
                    act.wait_ge(d_rows, 16 + 128 * c)
                    act.activation(rows[:, 2 * b:2 * b + 2, 0:2 * D],
                                   ps[:, b, :].bitcast(F16).rearrange("p (t c) -> p t c", t=2),
                                   ACT.Copy).then_inc(row_copied, 1)
                    if with_fill:
                        expert_high(c + EARLY_FILLS, c + EARLY_FILLS - 1, b)
                    rnn(5 + b)
                rnn(7)

            act.wait_ge(x2_tok, 4 * CH)
            with act.Fori(0, SLOTS - EARLY_FILLS) as c:
                superchunk(c, True, True)
            with act.Fori(SLOTS - EARLY_FILLS, SUPERS - 1) as c:
                superchunk(c, True, False)
            superchunk(SUPERS - 1, False, False)

            act.wait_ge(table, TABLE_STEPS)
            act.wait_ge(split_lo, 2 + 4 * SUPERS)

            def unit_xt(i, u):
                act.wait_ge(u_tr, i + 1)
                if not (isinstance(i, int) and i < 2):
                    act.wait_ge(u_up, 2 * i - 2)
                act.activation(xrt[u % 2], ps[:, 4 + u % 2, :].bitcast(F16), ACT.Copy).then_inc(u_xt, 1)

            def unit_gelu(i, u):
                e = act.value_load(unit_i[0:1, 0, ds(i, 1)], min_val=0, max_val=E)
                for b in range(2):
                    act.wait_ge(u_up, 2 * i + b + 1)
                    if not (isinstance(i, int) and i < 2):
                        act.wait_ge(u_lo, 2 * i - 3 + b)
                    for ht in (2 * b, 2 * b + 1):
                        ins = act.activation(hfr[u % 2][:, ht * UROWS:(ht + 1) * UROWS],
                                             ps[:, 2 * (u % 2) + b, (ht % 2) * UROWS:(ht % 2 + 1) * UROWS], ACT.Gelu,
                                             scale=1 / WS, bias=b1_t[:, ds(HT * e + ht, 1)])
                    ins.then_inc(u_gelu, 1)

            unit_xt(0, 0)
            unit_xt(1, 1)
            unit_gelu(0, 0)

            def units(g, last):
                for u in range(RING):
                    i = RING * g + u
                    if not (last and u + 2 >= RING):
                        unit_xt(i + 2, (u + 2) % RING)
                    if not (last and u + 1 >= RING):
                        unit_gelu(i + 1, (u + 1) % RING)

            units(0, False)
            with act.Fori(1, UNITS // RING - 1) as g:
                units(g, False)
            units(UNITS // RING - 1, True)

        @block.vector
        def _(dve):
            dve.sem_inc(pair_free_v, 3)
            dve.sem_inc(gated, 2)
            dve.sem_inc(prod, 2)
            dve.sem_inc(split_lo, 2)
            dve.sem_inc(added, 1)
            dve.sem_inc(w9t_done, 1)
            n_prep = 0

            def prep(ins):
                nonlocal n_prep
                n_prep += 1
                ins.then_inc(prep_v, 1)

            def split(hi, lo, src, scale):
                prep(dve.tensor_scalar(hi, src, scale, None, ALU.mult))
                dve.wait_ge(prep_v, n_prep)
                prep(dve.scalar_tensor_tensor(out=lo, in0=src, scalar=scale, in1=hi, op0=ALU.mult, op1=ALU.subtract))

            prep(dve.memset(cstate[:, 0:SC], 0.0))
            dve.wait_ge(cond_t, 1)
            c0 = ps[:, 6, 0:SC]
            dve.tensor_scalar(hb[:, 0, 0, :], c0, 2.0, None, ALU.mult).then_inc(h_hi, 1)
            dve.wait_ge(h_hi, 1)
            dve.scalar_tensor_tensor(out=hb[:, 0, 1, :], in0=c0, scalar=2.0, in1=hb[:, 0, 0, :],
                                     op0=ALU.mult, op1=ALU.subtract).then_inc(h_lo, 1)

            def x_low(n, slot):
                dve.wait_ge(xt_hi, n)
                dve.tensor_tensor(xt[:, slot, 1, :], ps[:, 4 + slot, 0:KD * P], xt[:, slot, 0, :],
                                  ALU.subtract).then_inc(xt_lo, 1)

            split(r0[:, 0, :], r0[:, 1, :], c0, 1.0)
            x_low(1, 0)
            dve.wait_ge(d_w0, 32)
            dve.wait_ge(d_b, 16 * 8)
            dve.wait_ge(const_step, CONSTS)
            for hi, lo, raw, scale in ((wx_h, wx_l, wx_raw, WS), (wh_h, wh_l, wh_raw, WS / 2)):
                hv, lv, rv = (v.rearrange("p (k c) -> p k c", k=KD) for v in (hi, lo, raw))
                for c0_, c1_, f in ((0, 3 * D, 0.5), (3 * D, 4 * D, 1.0)):
                    split(hv[:, :, c0_:c1_], lv[:, :, c0_:c1_], rv[:, :, c0_:c1_], scale * f)
            for bh, br, raw, neg in ((bhi0, brow0, braw0, nlow0), (bhi1, brow1, braw1, nlow1)):
                prep(dve.tensor_copy(bh[:, :], raw[:, :]))
                dve.wait_ge(prep_v, n_prep)
                prep(dve.scalar_tensor_tensor(out=br[:, :], in0=bh[:, :], scalar=neg[:, 0:1], in1=raw[:, :],
                                              op0=ALU.mult, op1=ALU.add))
            assert n_prep == PREP0

            def lstm_step(t, u):
                dve.wait_ge(ifg_tanh, t + 1)
                dve.scalar_tensor_tensor(out=fc, in0=tg[:, SC:2 * SC], scalar=1.0, in1=cstate[:, 0:SC],
                                         op0=ALU.add, op1=ALU.mult).then_inc(fc_done, 1)
                dve.scalar_tensor_tensor(out=ig, in0=tg[:, 0:SC], scalar=1.0, in1=tg[:, 2 * SC:3 * SC],
                                         op0=ALU.add, op1=ALU.mult).then_inc(ig_done, 1)
                dve.wait_ge(fc_done, t + 1)
                dve.wait_ge(ig_done, t + 1)
                dve.scalar_tensor_tensor(out=cstate[:, 0:SC], in0=fc, scalar=0.5, in1=ig,
                                         op0=ALU.mult, op1=ALU.add).then_inc(c_done, 1)
                dve.wait_ge(c_tanh, t + 1)
                dve.wait_ge(o_tanh, t + 1)
                hi, h = hb[:, 1 - u, 0, :], hs[:, ds(t * SC, SC)]
                dve.scalar_tensor_tensor(out=hi, in0=tg[:, 3 * SC:4 * SC], scalar=1.0, in1=tc,
                                         op0=ALU.add, op1=ALU.mult).then_inc(h_hi, 1)
                dve.scalar_tensor_tensor(out=h, in0=tg[:, 3 * SC:4 * SC], scalar=1.0, in1=tc,
                                         op0=ALU.add, op1=ALU.mult).then_inc(hs_done, 1)
                dve.wait_ge(hs_done, t + 1)
                dve.wait_ge(h_hi, t + 2)
                dve.tensor_tensor(hb[:, 1 - u, 1, :], h, hi, ALU.subtract).then_inc(h_lo, 1)
                dve.tensor_reduce(maxes[:, 0, ds(t, 1)], h, AX.X, ALU.max, apply_absolute_value=True).then_inc(hmax_done, 1)

            def lstm_turn(i, weights, last):
                w = wn[:, ds(2 * i, 2), :].rearrange("p q (b c) -> p (q b) c", c=WBLK) if weights else None
                s16, i16 = blk_s[:, 0, :], blk_s[:, 1, :]
                for r in range(4):
                    lstm_step(4 * i + r, r % 2)
                    if r == 0:
                        x_low(2 * i + 2, 1)
                        if weights:
                            dve.tensor_reduce(blk_s[:, 2, :], w, AX.X, ALU.max,
                                              apply_absolute_value=True).then_inc(wq_step, 1)
                            dve.wait_ge(wq_step, 5 * i + 1)
                            dve.tensor_scalar(s16, blk_s[:, 2, :], 1 / 7.0, TINY, ALU.mult, ALU.max).then_inc(wq_step, 1)
                            dve.wait_ge(wq_step, 5 * i + 2)
                            dve.reciprocal(i16, s16).then_inc(wq_step, 1)
                    if r == 1 and weights:
                        dve.wait_ge(wq_step, 5 * i + 3)
                        dve.tensor_tensor(w16.rearrange("p (b c) -> p b c", c=WBLK), w,
                                          i16.unsqueeze(2).broadcast_to([P, 16, WBLK]), ALU.mult).then_inc(wq_step, 1)
                    if r == 2:
                        if not last:
                            x_low(2 * i + 3, 0)
                        if weights:
                            dve.wait_ge(wq_step, 5 * i + 4)
                            dve.tensor_tensor(wd.rearrange("p (b c) -> p b c", c=WBLK),
                                              w16.rearrange("p (b c) -> p b c", c=WBLK),
                                              s16.unsqueeze(2).broadcast_to([P, 16, WBLK]), ALU.mult).then_inc(wq_step, 1)
                if weights:
                    dve.wait_ge(wt_hi_done, i + 1)
                    dve.scalar_tensor_tensor(out=wt_l[:, ds(2 * i, 2), :],
                                             in0=ps[:, 6, :].rearrange("p (q c) -> p q c", q=2), scalar=WS,
                                             in1=wt_h[:, ds(2 * i, 2), :], op0=ALU.mult,
                                             op1=ALU.subtract).then_inc(wt_lo_done, 1)

            dve.wait_ge(d_ffn, 48)
            with dve.Fori(0, PIECES // 2) as i:
                lstm_turn(i, True, False)
            with dve.Fori(PIECES // 2, T // 4 - 1) as i:
                lstm_turn(i, False, False)
            lstm_turn(T // 4 - 1, False, True)

            def greatest(n, row, cols):
                dve.tensor_reduce(colmax[:, n:n + 1], maxes[:, row, 0:cols], AX.X, ALU.max).then_inc(m_col, 1)
                dve.wait_ge(m_row, n + 1)
                dve.tensor_reduce(top[:, n:n + 1], ps[0:1, 7, 0:P], AX.X, ALU.max).then_inc(m_top, 1)
                dve.wait_ge(m_all, n + 1)
                return ps[:, 7, 256 + n:257 + n]

            n_step = 0

            def mstep(ins):
                nonlocal n_step
                n_step += 1
                ins.then_inc(m_step, 1)
                dve.wait_ge(m_step, n_step)

            dve.wait_ge(hmax_done, T)
            m = greatest(0, 0, T)
            mstep(dve.tensor_scalar(col(C_SH), m, 1 / QMAX, 2 * TINY, ALU.mult, ALU.max))
            mstep(dve.reciprocal(col(C_IH), col(C_SH)))
            mstep(dve.tensor_scalar(col(C_U), col(C_SH), 0.5 / WS, None, ALU.mult))
            mstep(dve.memset(col(C_R), 0.0))
            assert n_step == 4
            for c in range(8):
                dve.wait_ge(xq_int, c + 1)
                hi, lo = (v[:, :, 8 * c:8 * c + 8, :].rearrange("p k t n -> p t k n") for v in (xh_v, xl_v))
                q = qb[c % 2].rearrange("p (t k n) -> p t k n", k=KD, n=N)
                dve.tensor_copy(hi, q).then_inc(xq_hi, 1)
                dve.wait_ge(xq_hi, c + 1)
                dve.tensor_tensor(lo, q, hi, ALU.subtract).then_inc(xq_lo, 1)

            dve.wait_ge(d_rnn, 64)
            split(rx_h[:, :], rx_l[:, :], rx_raw, WS)
            split(rh_h[:, :], rh_l[:, :], rh_raw, WS)
            split(wr_h[:, :], wr_l[:, :], wr_raw[:, :], WS)
            assert n_prep == PREP1
            dve.wait_ge(d_moe_small, 64)
            prep(dve.tensor_scalar(b2_all[:, :], b2_all[:, :], WS, None, ALU.mult))
            prep(dve.memset(w9[:, :, E:SLOTS], 1 / WS))

            def pair(it):
                return ps[:, 2 * (it % 3):2 * (it % 3) + 2, :].rearrange("p b c -> p (b c)")

            def blk(p):
                return big[:, ds(p * BLOCK, BLOCK)]

            def abs_max(out_, in_):
                return dve.tensor_reduce(out_, in_, AX.X, ALU.max, apply_absolute_value=True)

            with dve.Fori(0, CH) as cc:
                for it in range(IT):
                    dve.wait_ge(pair_free_a, 3 + IT * cc + it + 1)
                    abs_max(maxes[:, 1, ds(IT * cc + it, 1)], blk(IT * cc + it)).then_inc(gate_max, 1)
            dve.wait_ge(gate_max, BLOCKS)
            m = greatest(1, 1, BLOCKS)
            mstep(dve.tensor_scalar(col(C_T1), m, 1 / QMAX, None, ALU.mult))
            mstep(dve.tensor_scalar(col(C_SG), col(C_T1), TINY, None, ALU.max))
            mstep(dve.reciprocal(col(C_IG), col(C_SG)))
            mstep(dve.tensor_scalar(col(C_SGH), col(C_SG), 0.5, None, ALU.mult))
            mstep(dve.tensor_scalar(col(C_SG16), col(C_SG), 1 / 65536.0, None, ALU.mult))
            assert n_step == 9
            with dve.Fori(0, CH) as cc:
                for it in range(IT):
                    p = IT * cc + it
                    dve.wait_ge(pair_done, BLOCKS + p + 1)
                    abs_max(maxes[:, 2, ds(p, 1)], pair(it)).then_inc(pair_free_v, 1)
                    dve.wait_ge(gate_s, p + 1)
                    dve.tensor_tensor(blk(p), qb[it % 2], sq[it % 2], ALU.mult).then_inc(gated, 1)
                    dve.wait_ge(gated, p + 3)
                    abs_max(maxes[:, 3, ds(p, 1)], blk(p)).then_inc(gated_max, 1)
            dve.wait_ge(pair_free_v, 3 + BLOCKS)
            dve.wait_ge(gated_max, BLOCKS)
            m = greatest(2, 2, BLOCKS)
            mstep(dve.tensor_scalar(col(C_T1), m, col(C_U), 1 / QMAX, ALU.mult, ALU.mult))
            mstep(dve.tensor_scalar(col(C_SU), col(C_T1), TINY, None, ALU.max))
            mstep(dve.reciprocal(col(C_ISU), col(C_SU)))
            mstep(dve.tensor_scalar(col(C_FU), col(C_ISU), col(C_U), None, ALU.mult))
            m = greatest(3, 3, BLOCKS)
            mstep(dve.tensor_scalar(col(C_T2), m, col(C_SG16), 1 / QMAX, ALU.mult, ALU.mult))
            mstep(dve.tensor_scalar(col(C_S2), col(C_T2), TINY, None, ALU.max))
            mstep(dve.reciprocal(col(C_T3), col(C_S2)))
            mstep(dve.tensor_scalar(col(C_F2), col(C_T3), col(C_SG16), None, ALU.mult))
            mstep(dve.tensor_scalar(col(C_T4), col(C_S2), col(C_SU), None, ALU.mult))
            assert n_step == 18
            with dve.Fori(0, CH) as cc:
                for it in range(IT):
                    p = IT * cc + it
                    dve.wait_ge(gated_q, p + 1)
                    dve.wait_ge(pair_free_a, 3 + BLOCKS + p + 1)
                    dve.tensor_tensor(blk(p), qb[it % 2], tmp_i[:, (2 + it % 2) * BLOCK:(3 + it % 2) * BLOCK],
                                      ALU.mult).then_inc(prod, 1)
                    dve.wait_ge(prod, p + 3)
                    abs_max(maxes[:, 1, ds(p, 1)], blk(p)).then_inc(prod_max, 1)
            dve.wait_ge(prod_max, BLOCKS)
            m = greatest(4, 1, BLOCKS)
            mstep(dve.tensor_scalar(col(C_T1), m, col(C_T4), 1 / QMAX, ALU.mult, ALU.mult))
            mstep(dve.tensor_scalar(col(C_S3), col(C_T1), TINY, None, ALU.max))
            mstep(dve.reciprocal(col(C_T3), col(C_S3)))
            mstep(dve.tensor_scalar(col(C_F3), col(C_T3), col(C_T4), None, ALU.mult))
            mstep(dve.tensor_scalar(col(C_OUT), col(C_S3), 1 / WS, None, ALU.mult))
            assert n_step == 23

            def down_turn(cc, first):
                for it in range(IT):
                    p = IT * cc + it
                    dve.wait_ge(o_int, p + 1)
                    hi = big16[:, ds(p * 2 * BLOCK, BLOCK)]
                    lo = big16[:, ds(p * 2 * BLOCK + BLOCK, BLOCK)]
                    dve.tensor_copy(hi, qb[it % 2]).then_inc(o_hi, 1)
                    dve.wait_ge(o_hi, p + 1)
                    dve.tensor_tensor(lo, qb[it % 2], hi, ALU.subtract).then_inc(o_lo, 1)
                for half in range(2):
                    for ot in range(KD):
                        n = 4 * cc + 2 * half + ot
                        dve.wait_ge(down, n + 1)
                        dve.wait_ge(xt_sb, n + 1)
                        if not (first and half == 0):
                            dve.wait_ge(x2_tr, n - 1)
                        dve.scalar_tensor_tensor(out=x2s[ot], in0=ps[:, ot, :], scalar=col(C_OUT), in1=xts[ot],
                                                 op0=ALU.mult, op1=ALU.add).then_inc(x2_new, 1)
                        dve.wait_ge(x2_new, n + 1)
                        src = x2s[ot].rearrange("p (t n) -> p t n", n=N)
                        hi = xh_v[:, ot, ds(16 * cc + 8 * half, 8), :]
                        lo = xl_v[:, ot, ds(16 * cc + 8 * half, 8), :]
                        dve.tensor_copy(hi, src).then_inc(x2_hi, 1)
                        dve.wait_ge(x2_hi, n + 1)
                        dve.tensor_tensor(lo, src, hi, ALU.subtract).then_inc(x2_lo, 1)

            down_turn(0, True)
            with dve.Fori(1, CH) as cc:
                down_turn(cc, False)

            def rnn_split(t):
                dve.wait_ge(r_tanh, t + 1)
                hi, lo = (v[:, :, ds(t, 1), :].rearrange("p k a n -> p k (a n)") for v in (xh_v, xl_v))
                new = hr[:, :].rearrange("p (k n) -> p k n", k=KD)
                dve.tensor_copy(hi, new).then_inc(r_hi, 1)
                dve.wait_ge(r_hi, t + 1)
                dve.tensor_tensor(lo, new, hi, ALU.subtract).then_inc(r_lo, 1)

            def expert_low(q, e, m):
                dve.wait_ge(e_hi, 2 * q + m + 1)
                at = e * EXP + m * 2048
                dve.scalar_tensor_tensor(out=big16[:, ds(at + 1024, 1024)], in0=stage[:, m, :], scalar=WS,
                                         in1=big16[:, ds(at, 1024)], op0=ALU.mult,
                                         op1=ALU.subtract).then_inc(e_lo, 1)

            for q in range(EARLY_FILLS):
                for m in range(2):
                    expert_low(q, (q + E) % SLOTS, m)
                    rnn_split(2 * q + m)

            dve.wait_ge(d_const, 16)
            dve.tensor_copy(carry[:, 0, :], consts[:, K_BASE:K_BASE + E]).then_inc(carried, 1)

            def over_e(v):
                return v.unsqueeze(2).broadcast_to([P, 4, E])

            def superchunk(c, with_rnn, with_fill):
                k = 0

                def link(ins):
                    nonlocal k
                    k += 1
                    ins.then_inc(route_step, 1)
                    dve.wait_ge(route_step, ROUTE_STEPS * c + k)

                def rnn(r):
                    if with_rnn:
                        rnn_split(SUPER_T * c + SUPER_T + r)

                def hidden(ht):
                    dve.wait_ge(gelu, 4 + 4 * c + ht + 1)
                    dve.tensor_copy(h1(0, ht), hf[ht % 2]).then_inc(split_hi, 1)
                    dve.wait_ge(split_hi, 4 * c + ht + 1)
                    dve.tensor_tensor(h1(1, ht), hf[ht % 2], h1(0, ht), ALU.subtract).then_inc(split_lo, 1)

                lv = ps[:, 7, 0:4 * E].rearrange("p (t e) -> p t e", e=E)
                dve.wait_ge(route, c + 1)
                link(dve.scalar_tensor_tensor(out=lg[:, :, :], in0=lv, scalar=1 / WS,
                                              in1=rb_all[:, :].unsqueeze(1).broadcast_to([P, 4, E]),
                                              op0=ALU.mult, op1=ALU.add))
                link(dve.tensor_reduce(mrow[:, 0:4], lg[:, :, :], AX.X, ALU.max))
                dve.tensor_tensor(zz[:, :, :], lg[:, :, :], over_e(mrow[:, 0:4]), ALU.subtract).then_inc(route_z, 1)
                mine = lg[:, :, :].unsqueeze(3).broadcast_to([P, 4, E, E])
                other = lg[:, :, :].unsqueeze(2).broadcast_to([P, 4, E, E])
                link(dve.tensor_tensor(cmp_a[:, :, :, :], other, mine, ALU.is_ge))
                link(dve.tensor_tensor(cmp_b[:, :, :, :], other, mine, ALU.is_gt))
                hidden(0)
                rnn(0)
                for tt in range(4):
                    last = dve.tensor_tensor(cmp_a[:, tt, :, :], cmp_a[:, tt, :, :], before[:, :, :], ALU.mult)
                link(last)
                link(dve.tensor_tensor(cmp_b[:, :, :, :], cmp_b[:, :, :, :], cmp_a[:, :, :, :], ALU.max))
                hidden(1)
                rnn(1)
                link(dve.tensor_reduce(rank[:, :, :], cmp_b[:, :, :, :], AX.X, ALU.add))
                dve.tensor_scalar(chosen[:, :, :], rank[:, :, :], float(TOP_K), None, ALU.is_lt).then_inc(route_c, 1)
                dve.wait_ge(route_e, c + 1)
                link(dve.tensor_reduce(mrow[:, 4:8], ee[:, :, :], AX.X, ALU.add))
                link(dve.reciprocal(mrow[:, 8:12], mrow[:, 4:8]))
                link(dve.tensor_scalar(mrow[:, 12:16], mrow[:, 8:12], 1 / WS, None, ALU.mult))
                hidden(2)
                rnn(2)
                link(dve.tensor_tensor(ee[:, :, :], ee[:, :, :], over_e(mrow[:, 12:16]), ALU.mult))
                link(dve.scalar_tensor_tensor(out=w9[:, :, 0:E], in0=rank[:, :, :], scalar=float(TOP_K), in1=ee[:, :, :],
                                              op0=ALU.is_lt, op1=ALU.mult))
                dve.sem_inc(w9_done, 1)
                dve.wait_ge(d_rows, 16 + 128 * c)
                dve.wait_ge(empty_made, 3)
                dve.tensor_copy(rows32[:, :, W_AT:W_AT + SLOTS], w9[:, :, :]).then_inc(row_tail, 1)
                dve.tensor_tensor(rows32[:, :, DST_AT:DST_AT + E], rank[:, :, :],
                                  over_e(consts[:, ds(K_DST + 4 * c, 4)]), ALU.add).then_inc(row_tail, 1)
                hidden(3)
                rnn(3)
                dve.wait_ge(placed_sum, c + 1)
                dve.wait_ge(carried, c + 1)
                link(dve.tensor_tensor(place[:, :, :], ps[:, 7, 64:64 + 4 * E].rearrange("p (t e) -> p t e", e=E),
                                       carry[:, 0, :].unsqueeze(1).broadcast_to([P, 4, E]), ALU.add))
                link(dve.tensor_tensor(carry[:, 1, :], ps[:, 7, 64 + 4 * E:64 + 5 * E], carry[:, 0, :], ALU.add))
                dve.tensor_copy(carry[:, 0, :], carry[:, 1, :]).then_inc(carried, 1)
                link(dve.scalar_tensor_tensor(out=place_j[:, :, 0, :], in0=rank[:, :, :], scalar=0.0, in1=place[:, :, :],
                                              op0=ALU.is_equal, op1=ALU.mult))
                link(dve.scalar_tensor_tensor(out=place_j[:, :, 1, :], in0=rank[:, :, :], scalar=1.0, in1=place[:, :, :],
                                              op0=ALU.is_equal, op1=ALU.mult))
                link(dve.tensor_reduce(place[:, :, 0:TOP_K], place_j[:, :, :, :], AX.X, ALU.add))
                dve.tensor_copy(row_j[:, :, :], place[:, :, 0:TOP_K]).then_inc(row_idx, 1)
                rnn(4)
                dve.wait_ge(w9_tr, c + 1)
                dve.tensor_scalar(w9t[:, :], ps[0:SLOTS, 7, :], WS, None, ALU.mult).then_inc(w9t_done, 1)
                if with_fill:
                    expert_low(c + EARLY_FILLS, c + EARLY_FILLS - 1, 0)
                rnn(5)
                if with_fill:
                    expert_low(c + EARLY_FILLS, c + EARLY_FILLS - 1, 1)

                def add_shared(b):
                    dve.wait_ge(down1, 2 * c + b + 1)
                    tiles = xn[:, ds(4 * c + 2 * b, 2), :].rearrange("p t c -> p (t c)")
                    dve.scalar_tensor_tensor(out=tiles, in0=ps[:, 4 + b, :], scalar=1 / WS, in1=tiles,
                                             op0=ALU.mult, op1=ALU.add).then_inc(added, 1)

                rnn(6)
                add_shared(0)
                rnn(7)
                add_shared(1)
                k += 1
                dve.sem_inc(route_step, 1)
                assert k == ROUTE_STEPS, k

            dve.wait_ge(x2_tok, 4 * CH)
            with dve.Fori(0, SLOTS - EARLY_FILLS) as c:
                superchunk(c, True, True)
            with dve.Fori(SLOTS - EARLY_FILLS, SUPERS - 1) as c:
                superchunk(c, True, False)
            superchunk(SUPERS - 1, False, False)

            k = 0

            def row(ins):
                nonlocal k
                k += 1
                ins.then_inc(table, 1)
                dve.wait_ge(table, k)

            cnt, till, lim, over, first, end = (count[:, i, :] for i in range(6))
            unit = consts[:, K_UNIT:K_UNIT + UNITS]
            dve.wait_ge(carried, SUPERS + 1)
            dve.wait_ge(w9_tr, SUPERS)
            row(dve.tensor_tensor(cnt, carry[:, 0, :], consts[:, K_BASE:K_BASE + E], ALU.subtract))
            row(dve.tensor_scalar(tiles_i[:, :], cnt, 1 / UROWS, (UROWS / 2 - 0.5) / UROWS, ALU.mult, ALU.add))
            row(dve.tensor_copy(till, tiles_i[:, :]))
            row(dve.scalar_tensor_tensor(out=lim, in0=till, scalar=float(UROWS), in1=cnt, op0=ALU.mult, op1=ALU.subtract))
            for h in range(HALVES):
                lane = consts[:, K_LANE + h:K_LANE + h + 1]
                row(dve.tensor_scalar(over, lim, lane, NOWHERE, ALU.is_le, ALU.mult))
                dve.scalar_tensor_tensor(out=fill_i[:, h * E:(h + 1) * E], in0=carry[:, 0, :], scalar=lane, in1=over,
                                         op0=ALU.add, op1=ALU.add).then_inc(filled, 1)
                dve.wait_ge(filled, h + 1)
            square = cmp_a[:, 0, :, :]
            row(dve.tensor_tensor(square, before[:, :, :], till.unsqueeze(1).broadcast_to([P, E, E]), ALU.mult))
            row(dve.tensor_reduce(first, square, AX.X, ALU.add))
            row(dve.tensor_tensor(end, first, till, ALU.add))
            row(dve.tensor_tensor(reached, unit.unsqueeze(2).broadcast_to([P, UNITS, E]),
                                  end.unsqueeze(1).broadcast_to([P, UNITS, E]), ALU.is_ge))
            row(dve.tensor_reduce(unit_f[:, 0, :], reached, AX.X, ALU.add))
            row(dve.tensor_tensor(reached, reached, till.unsqueeze(1).broadcast_to([P, UNITS, E]), ALU.mult))
            row(dve.tensor_reduce(unit_f[:, 1, :], reached, AX.X, ALU.add))
            row(dve.tensor_copy(unit_i[:, 0, :], unit_f[:, 0, :]))
            row(dve.scalar_tensor_tensor(out=unit_f[:, 0, :], in0=unit_f[:, 0, :], scalar=REGION / UROWS, in1=unit,
                                         op0=ALU.mult, op1=ALU.add))
            row(dve.tensor_tensor(unit_i[:, 1, :], unit_f[:, 0, :], unit_f[:, 1, :], ALU.subtract))
            assert k == TABLE_STEPS, k

            def unit_split(i, u):
                for b in range(2):
                    n = 2 * i + b
                    cols = slice(b * 512, (b + 1) * 512)
                    dve.wait_ge(u_gelu, n + 1)
                    if b == 0 and not (isinstance(i, int) and i < 2):
                        dve.wait_ge(u_down, i - 1)
                    hi, lo = h1r[u % 2][:, 0:H][:, cols], h1r[u % 2][:, H:2 * H][:, cols]
                    dve.tensor_copy(hi, hfr[u % 2][:, cols]).then_inc(u_hi, 1)
                    dve.wait_ge(u_hi, n + 1)
                    dve.tensor_tensor(lo, hfr[u % 2][:, cols], hi, ALU.subtract).then_inc(u_lo, 1)

            def unit_result(i, g, u):
                e = dve.value_load(unit_i[0:1, 0, ds(i, 1)], min_val=0, max_val=E)
                dve.wait_ge(u_down, i + 1)
                if not (isinstance(g, int) and g == 0):
                    dve.wait_ge(u_out[u], 16 * HALVES * g)
                for h in range(HALVES):
                    ins = dve.tensor_scalar(yr[u][:, h * D:(h + 1) * D], ps[:, 6 + u % 2, h * D:(h + 1) * D],
                                            xr32[u][:, h, ds(W_AT + e, 1)], None, ALU.mult)
                ins.then_inc(u_y, 1)
                dve.tensor_copy(dst_i[:, HALVES * u:HALVES * (u + 1)],
                                xr32[u][:, :, ds(DST_AT + e, 1)].rearrange("p h a -> p (h a)")).then_inc(u_dst, 1)

            unit_split(0, 0)

            def units(g, last):
                for u in range(RING):
                    i = RING * g + u
                    if not (last and u + 1 >= RING):
                        unit_split(i + 1, (u + 1) % RING)
                    unit_result(i, g, u)

            units(0, False)
            with dve.Fori(1, UNITS // RING - 1) as g:
                units(g, False)
            units(UNITS // RING - 1, True)

            for s in range(SUPERS):
                dve.wait_ge(d_super[s], 32)
                for j in range(TOP_K):
                    tiles = xn[:, 4 * s:4 * s + 4, :]
                    dve.tensor_tensor(tiles, tiles, pairs[:, s, :, j * D:(j + 1) * D], ALU.add).then_inc(summed, 1)
                    dve.wait_ge(summed, 2 * s + j + 1)


_INS = ['x', 'cond_1024', 'L0_cond_Wx', 'L0_cond_Wh', 'L0_cond_b', 'L0_ffn_w_gate', 'L0_ffn_w_up', 'L0_ffn_w_down',
        'L1_cond_Wx', 'L1_cond_Wh', 'L1_cond_b', 'L1_ffn_router_w', 'L1_ffn_router_b', 'L1_ffn_sw1', 'L1_ffn_sb1',
        'L1_ffn_sw2', 'L1_ffn_sb2', 'L1_ffn_rw1', 'L1_ffn_rb1', 'L1_ffn_rw2', 'L1_ffn_rb2']


def kernel(**inputs):
    import numpy as _np
    import concourse.bacc as _bacc
    from concourse import mybir as _mybir
    from concourse.bass_utils import run_bass_kernel_spmd as _run

    nc = _bacc.Bacc("TRN2", target_bir_lowering=False, num_devices=1)
    arrays, args = {}, {}
    for name in _INS:
        v = _np.ascontiguousarray(inputs[name])
        arrays[f"in_{name}"] = v
        args[name] = nc.dram_tensor(f"in_{name}", v.shape, _mybir.dt.from_np(v.dtype), kind="ExternalInput").ap()
    k = _np.zeros((P, K_COLS), _np.float32)
    lanes = _np.arange(P)
    k[:, K_DST:K_DST + TILES] = TOP_K * ((lanes % N) * T + lanes // N)[:, None] + 2 * TOP_K * _np.arange(TILES)
    k[:, K_LANE:K_LANE + HALVES] = lanes[:, None] + P * _np.arange(HALVES)
    k[:, K_BASE:K_BASE + E] = REGION * _np.arange(E)
    k[:, K_UNIT:] = _np.arange(UNITS)
    arrays["consts"] = k
    args["consts"] = nc.dram_tensor("consts", k.shape, F32, kind="ExternalInput").ap()
    rows = nc.dram_tensor("rows", (E * REGION + DUMMY * UROWS, ROW), I16, kind="Internal").ap()
    pairs = nc.dram_tensor("pairs", (TOP_K * T * N, D), F32, kind="Internal").ap()
    out = nc.dram_tensor("out_0", (N, T, D), F32, kind="ExternalOutput").ap()
    mixed_layers(nc, args, rows, pairs, out)
    r = _run(nc, [arrays], core_ids=[0])
    return r.results[0]["out_0"]
```

```python
from contextlib import ExitStack

import concourse.bass as bass
from concourse import mybir

ALU = mybir.AluOpType
ACT = mybir.ActivationFunctionType
AX = mybir.AxisListType
F32 = mybir.dt.float32
F16 = mybir.dt.float16
I16 = mybir.dt.int16
U16 = mybir.dt.uint16
I32 = mybir.dt.int32
U32 = mybir.dt.uint32
ds = bass.ds

P = 128
N = 64
T = 64
D = 256
KD = D // P
SC = KD * N
TILES = T // 2
GATES = 4 * D
I0 = 768
IT = I0 // P
H1 = 512
HT = H1 // P
E = 8
SLOTS = E + 1
SUPERS = 8
SUPER_T = T // SUPERS
CH = 4
PAIRS = TILES // 2
NEXT = ((0, 1), (2, 3), (4,), (5,))
BLOCK = 1024
BLOCKS = CH * IT
WBLK = 32
PIECES = 3 * I0 // P
QMAX = 32767.0
TINY = 1e-12
WS = 256.0
BIAS_SLOTS0 = GATES // P
BIAS_SLOTS1 = D // P
GATE_ORDER = [0, 1, 2, 3, 6, 7, 4, 5]
EARLY_FILLS = 2

REGION = T * N
TOP_K = 2
HALVES = 2
UROWS = HALVES * P
UNITS = T * N * TOP_K // UROWS + E - 1
DUMMY = E - 1
ROW = 2 * D + 2 * 2 * SLOTS
W_AT = D
DST_AT = D + SLOTS
RING = 4
TURNS = -(-UNITS // RING)
LAST = UNITS - RING * (TURNS - 1)
NOWHERE = 1.0e6
K_DST, K_LANE, K_BASE, K_UNIT = 0, TILES, TILES + HALVES, TILES + HALVES + E
K_COLS = K_UNIT + UNITS


def mixed_layers(nc, a, rows_dram, pairs_dram, out):
    with ExitStack() as ctx:
        def sb(name, shape, dt):
            return ctx.enter_context(nc.sbuf_tensor(name, shape, dt))

        def sem(name):
            return ctx.enter_context(nc.semaphore(name))

        ps = ctx.enter_context(nc.psum_tensor("ps", [P, 8, 512], F32))

        big = sb("big", [P, BLOCKS * BLOCK], F32)
        big16 = big[:, :].bitcast(F16)
        xn = sb("xn", [P, TILES, D], F32)
        xh = sb("xh", [P, T * SC], F16)
        xl = sb("xl", [P, T * SC], F16)
        xh_v = xh[:, :].rearrange("p (k t n) -> p k t n", k=KD, n=N)
        xl_v = xl[:, :].rearrange("p (k t n) -> p k t n", k=KD, n=N)
        wt_h = sb("wt_h", [P, PIECES, D], F16)
        wt_l = sb("wt_l", [P, PIECES, D], F16)
        rx_h = sb("rx_h", [P, KD * D], F16)
        rx_l = sb("rx_l", [P, KD * D], F16)
        rh_h = sb("rh_h", [P, KD * D], F16)
        rh_l = sb("rh_l", [P, KD * D], F16)
        tmp = sb("tmp", [P, 4096], F32)
        ident = sb("ident", [P, P], F32)
        ones_row = sb("ones_row", [1, P], F32)
        cstate = sb("cstate", [P, 2 * SC], F32)
        r0 = sb("r0", [P, 2, SC], F16)
        sel1 = sb("sel1", [2 * BIAS_SLOTS1, SC], F16)
        braw1 = sb("braw1", [2 * BIAS_SLOTS1, P], F32)
        bhi1 = sb("bhi1", [2 * BIAS_SLOTS1, P], F16)
        brow1 = sb("brow1", [2 * BIAS_SLOTS1, P], F16)
        nlow0 = sb("nlow0", [2 * BIAS_SLOTS0, 1], F32)
        nlow1 = sb("nlow1", [2 * BIAS_SLOTS1, 1], F32)
        nlow2 = sb("nlow2", [3 * SLOTS, 1], F32)
        wr_raw = sb("wr_raw", [P, KD * E], F32)
        wr_h = sb("wr_h", [P, KD * E], F16)
        wr_l = sb("wr_l", [P, KD * E], F16)
        rb_all = sb("rb_all", [P, E], F32)
        b1_n = sb("b1_n", [SLOTS * HT, P], F32)
        b1_t = sb("b1_t", [P, SLOTS * HT], F32)
        b2_raw = sb("b2_raw", [3 * SLOTS, D], F32)
        b2_x = sb("b2_x", [3 * SLOTS, D], F16)
        maxes = sb("maxes", [P, 4, 64], F32)
        colmax = sb("colmax", [P, 8], F32)
        top = sb("top", [1, 8], F32)
        sc = sb("sc", [P, 24], F32)
        blk_s = sb("blk_s", [P, 3, 16], F32)
        mrow = sb("mrow", [P, 16], F32)
        before = sb("before", [P, E, E], F32)
        consts = sb("shape_consts", [P, K_COLS], F32)
        ident16 = sb("ident16", [P, P], F16)
        tri16 = sb("tri16", [P, P], F16)
        ones16 = sb("ones16", [P, P], F16)
        chosen = sb("chosen", [P, 4, E], F16)
        carry = sb("carry", [P, 2, E], F32)
        row_j = sb("row_j", [P, 4, TOP_K], U32)
        w9 = sb("w9", [P, 4, SLOTS], F32)
        w9x = sb("w9x", [P, 4, 3 * SLOTS], F16)

        cond_n = tmp[0:N, 0:D]
        sel0 = tmp[0:2 * BIAS_SLOTS0, 256:512].bitcast(F16)
        braw0 = tmp[0:2 * BIAS_SLOTS0, 512:640]
        bhi0 = tmp[0:2 * BIAS_SLOTS0, 640:704].bitcast(F16)
        brow0 = tmp[0:2 * BIAS_SLOTS0, 704:768].bitcast(F16)
        w9t = tmp[0:3 * SLOTS, 3072:3328].bitcast(F16)
        cmp_a = tmp[:, 3584:3840].rearrange("p (t e j) -> p t e j", e=E, j=E)
        cmp_b = tmp[:, 3840:4096].rearrange("p (t e j) -> p t e j", e=E, j=E)

        hr = cstate[:, SC:2 * SC]
        b2_hi = cstate[0:3 * SLOTS, 0:D // 2].bitcast(F16)

        def part(start, cols):
            return big[:, start:start + cols]

        wx_h = part(0, 1024).bitcast(F16)
        wx_l = part(1024, 1024).bitcast(F16)
        wh_h = part(2048, 1024).bitcast(F16)
        wh_l = part(3072, 1024).bitcast(F16)
        wn = part(4096, PIECES * D).rearrange("p (q c) -> p q c", c=D)
        wx_raw = part(8704, 2048)
        wh_raw = part(10752, 2048)
        rx_raw = part(12800, 512)
        rh_raw = part(13312, 512)
        gc = part(13824, 4 * SC)
        og = part(14336, SC)
        cell = gc[:, 3 * SC:4 * SC]
        igfc = cstate[:, :]
        tc = part(14592, SC)
        hb = part(14720, 2 * SC).bitcast(F16).rearrange("p (s h c) -> p s h c", s=2, h=2)
        xt = part(14976, 512).bitcast(F16).rearrange("p (s h c) -> p s h c", s=2, h=2)
        wd = part(15488, 512)
        w16 = part(16000, 256).bitcast(I16)
        hs = part(16384, T * SC)

        tmp_i = tmp[:, :].bitcast(I16)
        tmp_u = tmp[:, :].bitcast(U16)
        qb = [tmp_i[:, i * BLOCK:(i + 1) * BLOCK] for i in range(2)]
        sq = [tmp_u[:, (2 + i) * BLOCK:(3 + i) * BLOCK] for i in range(2)]
        x2h = [tmp[:, 2048 + 512 * i:2304 + 512 * i].bitcast(F16) for i in range(4)]
        x2l = [tmp[:, 2304 + 512 * i:2560 + 512 * i].bitcast(F16) for i in range(4)]
        xs = tmp[:, 1024:1536].rearrange("p (c d) -> p c d", c=2)
        stage = tmp[:, 0:2048].rearrange("p (m c) -> p m c", m=2)
        hf = [tmp[:, 2048 + 512 * i:2560 + 512 * i] for i in range(2)]
        EXP = 4096
        H1_AT = SLOTS * EXP

        def h1(part_, ht):
            at = H1_AT + part_ * 2048 + ht * 512
            return big16[:, at:at + 512]

        rows = wt_h[:, :, :].rearrange("p q c -> p (q c)")[:, 0:4 * ROW].rearrange("p (t c) -> p t c", c=ROW)
        empty = wt_l[:, :, :].rearrange("p q c -> p (q c)")[:, 0:ROW]
        rows32 = wt_h[:, :, :].rearrange("p q c -> p (q c)")[:, 0:4 * ROW].bitcast(F32).rearrange(
            "p (t c) -> p t c", c=ROW // 2)
        empty32 = empty.bitcast(F32)
        spare = wt_l[:, :, :].rearrange("p q c -> p (q c)").bitcast(F32)[:, 512:]
        count = spare[:, 0:6 * E].rearrange("p (i e) -> p i e", e=E)
        place = spare[:, 48:48 + 4 * E].rearrange("p (t e) -> p t e", e=E)
        place_j = spare[:, 80:80 + 4 * TOP_K * E].rearrange("p (t j e) -> p t j e", j=TOP_K, e=E)
        tiles_i = spare[:, 144:144 + E].bitcast(I32)
        fill_i = spare[:, 152:152 + HALVES * E].bitcast(U32)
        dst_i = spare[:, 176:176 + HALVES * RING].bitcast(U32)
        unit_f = spare[:, 192:192 + 2 * UNITS].rearrange("p (i u) -> p i u", i=2)
        lg, zz, ee, rank = (spare[:, at:at + 4 * E].rearrange("p (t e) -> p t e", e=E) for at in range(384, 512, 4 * E))
        unit_i = spare[:, 512:512 + 2 * UNITS].bitcast(I32).rearrange("p (i u) -> p i u", i=2)
        xr = [xh[:, u * HALVES * ROW:(u + 1) * HALVES * ROW].rearrange("p (h c) -> p h c", h=HALVES) for u in range(RING)]
        xr32 = [xh[:, u * HALVES * ROW:(u + 1) * HALVES * ROW].bitcast(F32).rearrange("p (h c) -> p h c", h=HALVES)
                for u in range(RING)]
        XT = 2 * KD * UROWS
        xrt = [xl[:, u * XT:(u + 1) * XT] for u in range(2)]
        H = HT * UROWS
        h1r = [xl[:, 2 * XT + 2 * u * H:2 * XT + 2 * (u + 1) * H] for u in range(2)]
        hfr = [tmp[:, 2048 + u * H:2048 + (u + 1) * H] for u in range(2)]
        yr = [tmp[:, u * HALVES * D:(u + 1) * HALVES * D] for u in range(RING)]
        reached = tmp[:, 3328:3328 + UNITS * E].rearrange("p (i e) -> p i e", e=E)
        pairs = big[:, 0:SUPERS * 2048].rearrange("p (s t c) -> p s t c", s=SUPERS, t=4)

        d_x0, d_x1, d_cond, d_wx, d_wh, d_b, d_ffn, d_rnn, d_moe_small, d_out = (
            sem(s) for s in ("d_x0", "d_x1", "d_cond", "d_wx", "d_wh", "d_b", "d_ffn", "d_rnn", "d_moe_small", "d_out"))
        d_stage = [sem("d_stage1"), sem("d_stage2")]
        const_step = sem("const_step")
        cond_t = sem("cond_t")
        prep_v = sem("prep_v")
        h_hi = sem("h_hi")
        h_lo = sem("h_lo")
        w0_hi = sem("w0_hi")
        ifg_done, o_done = sem("ifg_done"), sem("o_done")
        ifg_tanh, o_tanh, c_tanh = sem("ifg_tanh"), sem("o_tanh"), sem("c_tanh")
        igfc_done, c_done, hs_done, hmax_done = (
            sem(s) for s in ("igfc_done", "c_done", "hs_done", "hmax_done"))
        x_staged = sem("x_staged")
        x_tr, xt_hi, xt_lo = sem("x_tr"), sem("xt_hi"), sem("xt_lo")
        wq_step = sem("wq_step")
        w_tr, wt_hi_done, wt_lo_done = sem("w_tr"), sem("wt_hi_done"), sem("wt_lo_done")
        m_col, m_row, m_top, m_all, m_step = (sem(s) for s in ("m_col", "m_row", "m_top", "m_all", "m_step"))
        xq_int, xq_hi, xq_lo = sem("xq_int"), sem("xq_hi"), sem("xq_lo")
        pair_done, pair_free_v, pair_free_a = sem("pair_done"), sem("pair_free_v"), sem("pair_free_a")
        gate_max = sem("gate_max")
        gate_q, gate_t, gate_s, gated, gated_max = (
            sem(s) for s in ("gate_q", "gate_t", "gate_s", "gated", "gated_max"))
        gated_q, prod, prod_max = sem("gated_q"), sem("prod"), sem("prod_max")
        o_int, o_hi, o_lo = sem("o_int"), sem("o_hi"), sem("o_lo")
        down, x2_new, x2_hi, x2_lo, x2_tr, x2_out = (
            sem(s) for s in ("down", "x2_new", "x2_hi", "x2_lo", "x2_tr", "x2_out"))
        e_hi, e_lo = sem("e_hi"), sem("e_lo")
        b1_tr, b1_ready = sem("b1_tr"), sem("b1_ready")
        r_sum, r_tanh, r_hi, r_lo = sem("r_sum"), sem("r_tanh"), sem("r_hi"), sem("r_lo")
        d_const, empty_made, d_rows = sem("d_const"), sem("empty_made"), sem("d_rows")
        d_fill = [sem(f"d_fill{e}") for e in range(E)]
        d_super = [sem(f"d_super{i}") for i in range(SUPERS)]
        placed_sum, row_ps, row_copied, row_tail, row_idx, filled = (
            sem(s) for s in ("placed_sum", "row_ps", "row_copied", "row_tail", "row_idx", "filled"))
        table = sem("table")
        rows_go, result_go = sem("rows_go"), sem("result_go")
        u_load = [sem(f"u_load{i}") for i in range(RING)]
        u_out = [sem(f"u_out{i}") for i in range(RING)]
        u_tr, u_xt, u_up, u_gelu, u_hi, u_lo, u_down, u_y, u_dst = (
            sem(s) for s in ("u_tr", "u_xt", "u_up", "u_gelu", "u_hi", "u_lo", "u_down", "u_y", "u_dst"))
        summed = sem("summed")
        up1, gelu, split_lo, down1, added = (
            sem(s) for s in ("up1", "gelu", "split_lo", "down1", "added"))
        route, route_step, route_z, route_e, w9_done, w9_tr, w9t_done, route_c, carried = (
            sem(s) for s in ("route", "route_step", "route_z", "route_e", "w9_done", "w9_tr", "w9t_done", "route_c", "carried"))

        CONSTS = 9
        PREP_X = 17
        PREP0 = 21
        PREP1 = PREP0 + 6
        ROUTE_STEPS = 19
        TABLE_STEPS = 17
        (C_SH, C_IH, C_U, C_SG, C_IG, C_SGH, C_SG16, C_S2, C_F2, C_SU, C_ISU, C_FU, C_S3, C_F3, C_OUT,
         C_T1, C_T2, C_T3, C_T4, C_R) = range(20)

        def col(c):
            return sc[:, c:c + 1]

        def w0_parts():
            for hi, lo, raw, scale in ((wx_h, wx_l, wx_raw, WS), (wh_h, wh_l, wh_raw, WS / 2)):
                hv, lv, rv = (v.rearrange("p (k c) -> p k c", k=KD) for v in (hi, lo, raw))
                for c0, c1, f in ((0, 3 * D, 0.5), (3 * D, 4 * D, 1.0)):
                    yield hv[:, :, c0:c1], lv[:, :, c0:c1], rv[:, :, c0:c1], scale * f

        x_dram, out_dram = a["x"], out
        block = ctx.enter_context(nc.Block())

        @block.sync
        def _(sp):
            sp.dma_start(cond_n[:, :], a["cond_1024"]).then_inc(d_cond, 16)
            first = TILES // 8
            for j0, j1, s in ((0, first, d_x0), (first, TILES, d_x1)):
                for tt in range(2):
                    sp.dma_start(xn[tt * N:(tt + 1) * N, j0:j1, :],
                                 x_dram.rearrange("n (j tt) d -> tt n j d", tt=2)[tt, :, j0:j1, :]).then_inc(s, 16)
                if j0 == 0:
                    for dst, name, done in ((wx_raw, "L0_cond_Wx", d_wx), (wh_raw, "L0_cond_Wh", d_wh)):
                        sp.dma_start(dst.rearrange("p (k c) -> p k c", k=KD),
                                     a[name].rearrange("(k p) c -> p k c", p=P)).then_inc(done, 16)
                    b0 = a["L0_cond_b"].rearrange("(g c) -> g c", c=P)
                    b1 = a["L1_cond_b"].rearrange("(g c) -> g c", c=P)
                    for half in range(2):
                        at = half * BIAS_SLOTS0
                        sp.dma_start(braw0[at:at + 4, :], b0[0:4, :]).then_inc(d_b, 16)
                        sp.dma_start(braw0[at + 4:at + 6, :], b0[6:8, :]).then_inc(d_b, 16)
                        sp.dma_start(braw0[at + 6:at + 8, :], b0[4:6, :]).then_inc(d_b, 16)
                        at = half * BIAS_SLOTS1
                        sp.dma_start(braw1[at:at + BIAS_SLOTS1, :], b1).then_inc(d_b, 16)
            sp.dma_start(wn[:, 0:IT, :], a["L0_ffn_w_gate"].rearrange("(q p) c -> p q c", p=P)).then_inc(d_ffn, 16)
            sp.dma_start(wn[:, IT:2 * IT, :], a["L0_ffn_w_up"].rearrange("(q p) c -> p q c", p=P)).then_inc(d_ffn, 16)
            sp.dma_start(wn[:, 2 * IT:3 * IT, :].rearrange("p (o s) c -> p o (s c)", o=KD),
                         a["L0_ffn_w_down"].rearrange("(o p) c -> p o c", p=P)).then_inc(d_ffn, 16)
            for dst, name in ((rx_raw, "L1_cond_Wx"), (rh_raw, "L1_cond_Wh")):
                sp.dma_start(dst.rearrange("p (k c) -> p k c", k=KD),
                             a[name].rearrange("(k p) c -> p k c", p=P)).then_inc(d_rnn, 16)
            sp.dma_start(wr_raw[:, :].rearrange("p (k c) -> p k c", k=KD),
                         a["L1_ffn_router_w"].rearrange("(k p) c -> p k c", p=P)).then_inc(d_rnn, 16)
            sp.dma_start(rb_all[:, :], a["L1_ffn_router_b"].rearrange("(a e) -> a e", a=1).broadcast_to([P, E])).then_inc(d_rnn, 16)
            sp.dma_start(consts[:, :], a["consts"]).then_inc(d_const, 16)
            sp.dma_start(b1_n[0:E * HT, :], a["L1_ffn_rb1"].rearrange("e (h c) -> (e h) c", c=P)).then_inc(d_moe_small, 16)
            sp.dma_start(b1_n[E * HT:SLOTS * HT, :], a["L1_ffn_sb1"].rearrange("(h c) -> h c", c=P)).then_inc(d_moe_small, 16)
            for g in range(0, 3 * SLOTS, SLOTS):
                sp.dma_start(b2_raw[g:g + E, :], a["L1_ffn_rb2"]).then_inc(d_moe_small, 16)
                sp.dma_start(b2_raw[g + E:g + SLOTS, :], a["L1_ffn_sb2"].rearrange("(a c) -> a c", a=1)
                             ).then_inc(d_moe_small, 16)

            w1_v = a["L1_ffn_rw1"].rearrange("e (k p) c -> p e k c", p=P)
            w2_v = a["L1_ffn_rw2"].rearrange("e (k p) c -> p e k c", p=P)
            st1 = stage[:, 0, :].rearrange("p (k c) -> p k c", k=KD)
            st2 = stage[:, 1, :].rearrange("p (k c) -> p k c", k=HT)
            sp.wait_ge(o_lo, BLOCKS)
            for q in range(SLOTS):
                e = (q + E) % SLOTS
                s1 = w1_v[:, e] if e < E else a["L1_ffn_sw1"].rearrange("(k p) c -> p k c", p=P)
                s2 = w2_v[:, e] if e < E else a["L1_ffn_sw2"].rearrange("(k p) c -> p k c", p=P)
                for m, (dst, src) in enumerate(((st1, s1), (st2, s2))):
                    if q:
                        sp.wait_ge(e_lo, 2 * q + m - 1)
                    sp.dma_start(dst, src).then_inc(d_stage[m], 16)
            sp.wait_ge(d_rows, 16 * (TOP_K * TILES + 1))
            sp.wait_ge(table, TABLE_STEPS)

            def load(i, u):
                tile = sp.value_load(unit_i[0:1, 1, ds(i, 1)], min_val=0, max_val=E * REGION // UROWS + DUMMY - 1)
                sp.dma_start(xr[u].bitcast(I16), rows_dram.rearrange("(a h p) c -> p a h c", h=HALVES, p=P)[
                    :, ds(tile, 1), :, :].rearrange("p a h c -> p (a h) c")).then_inc(u_load[u], 16)

            def refill(g, u):
                sp.wait_ge(u_dst, RING * g + u - RING + 1)
                load(RING * g + u, u)

            for i in range(E):
                sp.wait_ge(d_fill[i], 16 * HALVES)
                if i < RING:
                    load(i, i)
                else:
                    refill(i // RING, i % RING)
            with sp.Fori(E // RING, TURNS - 1) as g:
                for u in range(RING):
                    refill(g, u)
            for u in range(LAST):
                refill(TURNS - 1, u)
            sp.wait_ge(u_down, UNITS)
            sp.wait_ge(u_y, UNITS)
            for u in range(RING):
                sp.wait_ge(u_out[u], 16 * HALVES * (TURNS if u < LAST else TURNS - 1))
            for s in range(SUPERS):
                for tt in range(2):
                    sp.dma_start(pairs[tt * N:(tt + 1) * N, s, :, :],
                                 pairs_dram.rearrange("(n j tt two) d -> tt n j (two d)", tt=2, two=2, n=N)[
                                     tt, :, 4 * s:4 * s + 4, :]).then_inc(d_super[s], 16)
            for s in range(SUPERS):
                sp.wait_ge(summed, 2 * s + 2)
                for tt in range(2):
                    sp.dma_start(out_dram.rearrange("n (j tt) d -> tt n j d", tt=2)[tt, :, 4 * s:4 * s + 4, :],
                                 xn[tt * N:(tt + 1) * N, 4 * s:4 * s + 4, :]).then_inc(d_out, 16)
            sp.wait_ge(d_out, 16 * 2 * SUPERS)

        @block.gpsimd
        def _(pool):
            n = 0

            def step(ins):
                nonlocal n
                n += 1
                ins.then_inc(const_step, 1)
                pool.wait_ge(const_step, n)

            step(pool.memset(ident[:, :], 0.0))
            step(pool.affine_select(out=ident[:, :], in_=ident[:, :], compare_op=ALU.not_equal, fill=1.0,
                                    base=0, pattern=[[-1, P]], channel_multiplier=1))
            pool.memset(ones_row[:, :], 1.0).then_inc(const_step, 1)
            n += 1
            pool.wait_ge(d_x0, 32)
            for slot in range(2):
                pool.tensor_copy(xs[:, slot, :], xn[:, slot, :]).then_inc(x_staged, 1)
            step(pool.memset(before[:, :, :], 1.0))
            step(pool.affine_select(out=before[:, :, :], in_=before[:, :, :], compare_op=ALU.is_gt, fill=0.0,
                                    base=0, pattern=[[1, E], [-1, E]], channel_multiplier=0))
            step(pool.tensor_copy(ident16[:, :], ident[:, :]))
            step(pool.memset(ones16[:, :], 1.0))
            step(pool.memset(tri16[:, :], 1.0))
            step(pool.affine_select(out=tri16[:, :], in_=tri16[:, :], compare_op=ALU.is_gt, fill=0.0, base=0,
                                    pattern=[[1, P]], channel_multiplier=-1))
            assert n == CONSTS, n

            pool.wait_ge(d_x1, 32)
            with pool.Fori(1, TILES // 2) as i:
                for slot in range(2):
                    pool.wait_ge(x_tr, 2 * i + slot - 1)
                    pool.tensor_copy(xs[:, slot, :], xn[:, ds(2 * i + slot, 1), :].rearrange("p a c -> p (a c)")
                                     ).then_inc(x_staged, 1)
            pool.wait_ge(down, PAIRS)
            pool.memset(empty[:, :], 0.0).then_inc(empty_made, 1)
            pool.wait_ge(empty_made, 1)
            pool.memset(empty32[:, DST_AT:DST_AT + SLOTS], NOWHERE).then_inc(empty_made, 1)
            pool.memset(rows32[:, :, DST_AT + E:DST_AT + SLOTS], NOWHERE).then_inc(empty_made, 1)
            pool.wait_ge(empty_made, 3)
            pool.dma_start(rows_dram.rearrange("(a p) c -> p a c", p=P)[:, E * REGION // P:, :],
                           empty.bitcast(I16).unsqueeze(1).broadcast_to([P, DUMMY * HALVES, ROW])).then_inc(d_rows, 16)

            def to_rows(src, index, done):
                pool.indirect_dma_start(rows_dram[:, :], bass.IndirectOffsetOnAxis(index, 0), src, None,
                                        bounds_check=E * REGION - 1, oob_is_err=False).then_inc(done, 16)

            def superchunk_rows(s, between=None):
                pool.wait_ge(row_idx, s + 1)
                pool.wait_ge(row_tail, 2 * s + 2)
                pool.wait_ge(row_copied, 2 + 2 * s + 2)
                pool.sem_inc(rows_go, 1)
                for tt in range(4):
                    for j in range(TOP_K):
                        to_rows(rows[:, tt, :].bitcast(I16), row_j[:, tt, j:j + 1], d_rows)
                    if tt == 2 and between is not None:
                        pool.wait_ge(filled, HALVES)
                        fill(between)

            def fill(e):
                for h in range(HALVES):
                    to_rows(empty.bitcast(I16), fill_i[:, h * E + e:h * E + e + 1], d_fill[e])

            with pool.Fori(0, SUPERS - 1) as s:
                superchunk_rows(s)
            superchunk_rows(SUPERS - 1, 0)
            for e in range(1, E):
                fill(e)

            def results(g, count):
                for u in range(count):
                    pool.wait_ge(u_y, RING * g + u + 1)
                    pool.wait_ge(u_dst, RING * g + u + 1)
                    pool.sem_inc(result_go, 1)
                    for h in range(HALVES):
                        at = HALVES * u + h
                        pool.indirect_dma_start(pairs_dram[:, :], bass.IndirectOffsetOnAxis(dst_i[:, at:at + 1], 0),
                                                yr[u][:, h * D:(h + 1) * D], None, bounds_check=TOP_K * T * N - 1,
                                                oob_is_err=False).then_inc(u_out[u], 16)

            with pool.Fori(0, TURNS - 1) as g:
                results(g, RING)
            results(TURNS - 1, LAST)

        @block.tensor
        def _(pe):
            pe.wait_ge(const_step, 3)
            pe.wait_ge(d_cond, 16)
            for k in range(KD):
                mm = pe.transpose(ps[:, 6, k * N:(k + 1) * N], cond_n[:, k * P:(k + 1) * P], ident[0:N, 0:N])
            mm.then_inc(cond_t, 1)
            def x_transpose(j, slot):
                pe.wait_ge(x_staged, j + 1)
                for k in range(KD):
                    mm = pe.transpose(ps[:, 4 + slot, k * P:(k + 1) * P], xs[:, slot, k * P:(k + 1) * P], ident[:, :])
                mm.then_inc(x_tr, 1)

            def gate_ps(u, s):
                return ps[:, u, s * N:(s + 1) * N] if s < 6 else ps[:, 2 + u, (s - 6) * N:(s - 5) * N]

            def x_part(u, slot, wait):
                if wait is not None:
                    pe.wait_ge(xt_lo, wait)
                pe.matmul(ps[:, u, 0:6 * N], brow0, sel0[:, 0:6 * N], start=True, stop=False, skip_group_check=True)
                pe.matmul(ps[:, 2 + u, 0:2 * N], brow0, sel0[:, 6 * N:8 * N], start=True, stop=False,
                          skip_group_check=True)
                for s, g in enumerate(GATE_ORDER):
                    o = gate_ps(u, s)
                    for k in range(KD):
                        cols = slice(k * GATES + g * P, k * GATES + (g + 1) * P)
                        hi = xt[:, slot, 0, k * P + u * N:k * P + (u + 1) * N]
                        lo = xt[:, slot, 1, k * P + u * N:k * P + (u + 1) * N]
                        for w, v in ((wx_h, hi), (wx_l, hi), (wx_h, lo)):
                            pe.matmul(o, w[:, cols], v, start=False, stop=False, skip_group_check=True)

            def h_part(t, u):
                pe.wait_ge(h_hi, t + 1)
                for slots in (range(6), range(6, 8)):
                    for low in (0, 1):
                        if low and slots[0] == 0:
                            pe.wait_ge(h_lo, t + 1)
                        for s in slots:
                            g = GATE_ORDER[s]
                            o = gate_ps(u, s)
                            for k in range(KD):
                                cols = slice(k * GATES + g * P, k * GATES + (g + 1) * P)
                                v = hb[:, u, low, k * N:(k + 1) * N]
                                for w in ((wh_h,) if low else (wh_h, wh_l)):
                                    mm = pe.matmul(o, w[:, cols], v, start=False, stop=low == 1, skip_group_check=True)
                    mm.then_inc(ifg_done if slots[0] == 0 else o_done, 1)

            def lstm_turn(i, w, last):
                x_transpose(2 * i + 1, 1)
                h_part(4 * i, 0)
                x_part(1, 0, None)
                h_part(4 * i + 1, 1)
                x_part(0, 1, 2 * i + 2)
                if not last:
                    x_transpose(2 * i + 2, 0)
                h_part(4 * i + 2, 0)
                x_part(1, 1, None)
                h_part(4 * i + 3, 1)
                if not last:
                    x_part(0, 0, 2 * i + 3)
                if w is not None:
                    pe.wait_ge(wq_step, 5 * w + 5)
                    for q in range(4):
                        mm = pe.transpose(ps[:, 6, q * P:(q + 1) * P], wd[:, q * P:(q + 1) * P], ident[:, :])
                    mm.then_inc(w_tr, 1)

            x_transpose(0, 0)
            pe.wait_ge(prep_v, PREP_X)
            x_part(0, 0, 1)
            pe.wait_ge(prep_v, PREP0)
            lstm_turn(0, None, False)
            with pe.Fori(1, 1 + PIECES // 2) as i:
                lstm_turn(i, i - 1, False)
            with pe.Fori(1 + PIECES // 2, T // 4 - 1) as i:
                lstm_turn(i, None, False)
            lstm_turn(T // 4 - 1, None, True)

            def spread(n):
                pe.wait_ge(m_col, n + 1)
                pe.transpose(ps[0:1, 7, 0:P], colmax[:, n:n + 1], ident[:, :]).then_inc(m_row, 1)
                pe.wait_ge(m_top, n + 1)
                pe.matmul(ps[:, 7, 256 + n:257 + n], ones_row[:, :], top[:, n:n + 1],
                          start=True, stop=True).then_inc(m_all, 1)

            def ffn_pass(first_piece, free, before_=None, maxima=(), chunk_ready=None):
                def chunk(cc, first):
                    if chunk_ready is not None:
                        pe.wait_ge(chunk_ready, 2 * cc + 2)
                    for it in range(IT):
                        pe.wait_ge(free[0], free[1] + 1 + IT * cc + it)
                        if first and it < 3 and before_ is not None:
                            pe.wait_ge(before_, BLOCKS + 1 + it)
                        piece = first_piece + it
                        for half in range(2):
                            o = ps[:, 2 * (it % 3) + half, :]
                            r = [v[:, :, ds(16 * cc + 8 * half, 8), :] for v in (xh_v, xl_v)]
                            n = 0
                            for k in range(KD):
                                for w, x in ((wt_h, 0), (wt_l, 0), (wt_h, 1)):
                                    mm = pe.matmul(o, w[:, piece, k * P:(k + 1) * P], r[x][:, k, :, :],
                                                   start=n == 0, stop=n == 5)
                                    n += 1
                        mm.then_inc(pair_done, 1)
                        if first and it == 2:
                            for m in maxima:
                                spread(m)

                chunk(0, True)
                with pe.Fori(1, CH) as cc:
                    chunk(cc, False)

            spread(0)
            pe.wait_ge(wt_lo_done, PIECES // 2)
            ffn_pass(0, (pair_free_a, 0), chunk_ready=xq_lo)
            ffn_pass(IT, (pair_free_v, 0), pair_free_a, maxima=(1,))
            ffn_pass(IT, (pair_free_a, BLOCKS), pair_free_v, maxima=(2, 3))
            spread(4)

            def down_products(cc, j, it):
                pieces = slice(2 * IT + it // 2, 2 * IT + it // 2 + I0 // D + 1, I0 // D)
                cols = slice((it % 2) * P, (it % 2 + 1) * P)
                for h in range(2):
                    for w, x in ((wt_h, 0), (wt_l, 0), (wt_h, 1)):
                        at = (IT * cc + it) * 2 * BLOCK + x * BLOCK + (2 * j + h) * P
                        mm = pe.matmul(ps[:, j, h * D:(h + 1) * D], big16[:, ds(at, P)], w[:, pieces, cols],
                                       start=it == 0 and h == 0 and w is wt_h and x == 0,
                                       stop=it == IT - 1 and x == 1, skip_group_check=True)
                return mm

            def x2_transpose(n, j, first):
                pe.wait_ge(x2_lo, n + 1)
                if not (first and j < 2):
                    pe.wait_ge(x2_out, n - 1)
                for part_, v in enumerate((x2h[j], x2l[j])):
                    for k in range(KD):
                        for h in range(2):
                            at = part_ * 512 + k * 2 * P + h * P
                            mm = pe.transpose(ps[:, 4 + j % 2, :].bitcast(F16)[:, at:at + P],
                                              v[:, h * D + k * P:h * D + (k + 1) * P], ident16[:, :])
                mm.then_inc(x2_tr, 1)

            def down_turn(cc, first):
                for j in range(4):
                    n = 4 * cc + j
                    pe.wait_ge(x2_new, n - 3)
                    for it in range(IT):
                        if j == 0:
                            pe.wait_ge(o_lo, IT * cc + it + 1)
                        mm = down_products(cc, j, it)
                    mm.then_inc(down, 1)
                    x2_transpose(n - 4, j, first)

            pe.wait_ge(const_step, CONSTS)
            pe.wait_ge(pair_free_a, 3 + 2 * BLOCKS)
            for it in range(IT):
                pe.wait_ge(o_lo, it + 1)
                for j in range(4):
                    mm = down_products(0, j, it)
                    if it == IT - 1:
                        mm.then_inc(down, 1)
            down_turn(1, True)
            with pe.Fori(2, CH) as cc:
                down_turn(cc, False)
            pe.wait_ge(d_moe_small, 16 * 8)
            pe.transpose(ps[:, 7, 0:SLOTS * HT], b1_n[:, :], ident[0:SLOTS * HT, 0:SLOTS * HT]).then_inc(b1_tr, 1)
            pe.wait_ge(x2_out, SUPER_T // 4)

            def rnn_step(t, first=False):
                if not first:
                    pe.wait_ge(r_hi, t)
                pe.matmul(ps[:, 6, 0:SC], brow1[:, :], sel1[:, :], start=True, stop=False, skip_group_check=True)

                def products(wh, wl, hi, lo, last):
                    for low in (0, 1):
                        for o in range(KD):
                            for k in range(KD):
                                cols = slice(k * D + o * P, k * D + (o + 1) * P)
                                for w in ((wh,) if low else (wh, wl)):
                                    mm = pe.matmul(ps[:, 6, o * N:(o + 1) * N], w[:, cols], (lo if low else hi)(k),
                                                   start=False, stop=last and low == 1, skip_group_check=True)
                    return mm

                def at(v, when):
                    return lambda k: v[:, ds(k * T * N + when * N, N)]

                products(rx_h, rx_l, at(xh, t), at(xl, t), False)
                if first:
                    mm = products(rh_h, rh_l, lambda k: r0[:, 0, k * N:(k + 1) * N],
                                  lambda k: r0[:, 1, k * N:(k + 1) * N], True)
                else:
                    pe.wait_ge(r_lo, t)
                    mm = products(rh_h, rh_l, at(xh, t - 1), at(xl, t - 1), True)
                mm.then_inc(r_sum, 1)

            rnn_step(0, True)
            x2_transpose(PAIRS - 4, 0, False)
            for j in range(1, 4):
                rnn_step(j)
                x2_transpose(PAIRS - 4 + j, j, False)
            with pe.Fori(4, SUPER_T) as t:
                rnn_step(t)
            pe.wait_ge(x2_out, PAIRS)

            def superchunk(c, with_rnn):
                def rnn(r):
                    if with_rnn:
                        rnn_step(SUPER_T * c + SUPER_T + r)

                def tokens(v, tt, k):
                    return v[:, ds(k * T * N + (SUPER_T * c + 2 * tt) * N, P)]

                def router():
                    for tt in range(4):
                        n = 0
                        for k in range(KD):
                            for w, v in ((wr_h, xh), (wr_l, xh), (wr_h, xl)):
                                yield pe.matmul(ps[:, 7, tt * E:(tt + 1) * E], tokens(v, tt, k),
                                                w[:, k * E:(k + 1) * E], start=n == 0 and tt == 0, stop=n == 5,
                                                skip_group_check=True)
                                n += 1

                pe.wait_ge(w9t_done, c + 1)
                rhs = [v[:, :, ds(SUPER_T * c, SUPER_T), :] for v in (xh_v, xl_v)]
                routing = router()
                for ht in range(HT):
                    pe.wait_ge(gelu, 4 * c + ht + 1)
                    if ht < 2:
                        pe.wait_ge(row_copied, 2 * c + ht + 1)
                    n = 0
                    for k in range(KD):
                        for low, x in ((0, 0), (1, 0), (0, 1)):
                            at = E * EXP + low * 1024 + k * H1 + ht * P
                            mm = pe.matmul(ps[:, ht, :], big16[:, at:at + P], rhs[x][:, k, :, :], start=n == 0, stop=n == 5)
                            n += 1
                            if ht == 0:
                                for _ in range(4):
                                    last = next(routing)
                    if ht == 0:
                        last.then_inc(route, 1)
                    mm.then_inc(up1, 1)
                    rnn(ht)
                pe.wait_ge(route_c, c + 1)
                pe.wait_ge(gelu, 4 * c + 4 + 2)
                for tt in range(5):
                    o = ps[:, 7, 64 + tt * E:64 + (tt + 1) * E]
                    if tt < 4:
                        mm = pe.matmul(o, tri16[:, :], chosen[:, tt, :], start=tt == 0, stop=tt == 0, skip_group_check=True)
                    for before_ in range(tt):
                        mm = pe.matmul(o, ones16[:, :], chosen[:, before_, :], start=False, stop=before_ == tt - 1,
                                       skip_group_check=True)
                mm.then_inc(placed_sum, 1)
                for b in range(2):
                    for t2 in range(2):
                        for part_, v in enumerate((xh, xl)):
                            for k in range(KD):
                                at = t2 * 512 + part_ * D + k * P
                                mm = pe.transpose(ps[:, b, :].bitcast(F16)[:, at:at + P], tokens(v, 2 * b + t2, k),
                                                  ident16[:, :])
                    mm.then_inc(row_ps, 1)
                rnn(4)
                def down(tt):
                    n = 0
                    for ht in range(HT):
                        for hp, wp in ((0, 0), (0, 1), (1, 0)):
                            at = E * EXP + 2048 + wp * 1024 + ht * D
                            pe.matmul(ps[:, 4 + tt // 2, (tt % 2) * D:(tt % 2 + 1) * D],
                                      h1(hp, ht)[:, tt * P:(tt + 1) * P], big16[:, at:at + D],
                                      start=n == 0 and tt % 2 == 0, stop=False, skip_group_check=True)
                            n += 1

                def second_biases(b):
                    for tt in (2 * b, 2 * b + 1):
                        mm = pe.matmul(ps[:, 4 + b, (tt % 2) * D:(tt % 2 + 1) * D], w9t[:, tt * P:(tt + 1) * P],
                                       b2_x[:, :], start=False, stop=True, skip_group_check=True)
                    mm.then_inc(down1, 1)

                pe.wait_ge(split_lo, 2 + 4 * c + 4)
                pe.wait_ge(added, 2 * c + 1)
                down(0)
                rnn(5)
                down(1)
                pe.wait_ge(w9_done, 2 * c + 2)
                pe.wait_ge(row_idx, c + 1)
                for tt in range(4):
                    mm = pe.transpose(ps[0:3 * SLOTS, 7, 256:512].bitcast(F16)[:, tt * P:(tt + 1) * P], w9x[:, tt, :],
                                      ident16[:, :])
                mm.then_inc(w9_tr, 1)
                rnn(6)
                pe.wait_ge(w9t_done, c + 2)
                second_biases(0)
                down(2)
                rnn(7)
                down(3)
                second_biases(1)

            pe.wait_ge(r_hi, SUPER_T)
            pe.wait_ge(r_lo, SUPER_T)
            pe.wait_ge(b1_ready, 1)
            pe.wait_ge(const_step, CONSTS)
            pe.wait_ge(e_lo, 2)
            with pe.Fori(0, SUPERS - 1) as c:
                superchunk(c, True)
                pe.wait_ge(r_lo, SUPER_T * c + 2 * SUPER_T)
            superchunk(SUPERS - 1, False)

            pe.wait_ge(e_lo, 2 * SLOTS)
            pe.wait_ge(table, TABLE_STEPS)
            pe.wait_ge(row_copied, 2 + 2 * SUPERS)
            pe.wait_ge(gelu, 4 + 4 * SUPERS)
            pe.wait_ge(added, 2 * SUPERS + 1)

            def expert(i):
                return pe.value_load(unit_i[0:1, 0, ds(i, 1)], min_val=0, max_val=E)

            def unit_transpose(i, g, u):
                pe.wait_ge(u_load[u], 16 * g + 16)
                if not (isinstance(i, int) and i < 2):
                    pe.wait_ge(u_xt, i - 1)
                for part_ in range(2):
                    for k in range(KD):
                        for h in range(HALVES):
                            at = ((part_ * KD + k) * HALVES + h) * P
                            mm = pe.transpose(ps[:, 4 + u % 2, :].bitcast(F16)[:, at:at + P],
                                              xr[u][:, h, (part_ * KD + k) * P:(part_ * KD + k + 1) * P], ident16[:, :])
                mm.then_inc(u_tr, 1)

            def unit_up(i, u, e):
                pe.wait_ge(u_xt, i + 1)
                for ht in range(HT):
                    if ht % 2 == 0 and not (isinstance(i, int) and i < 2):
                        pe.wait_ge(u_gelu, 2 * i - 3 + ht // 2)
                    n = 0
                    for k in range(KD):
                        for low, x in ((0, 0), (1, 0), (0, 1)):
                            at = (x * KD + k) * UROWS
                            mm = pe.matmul(ps[:, 2 * (u % 2) + ht // 2, (ht % 2) * UROWS:(ht % 2 + 1) * UROWS],
                                           big16[:, ds(e * EXP + low * 1024 + k * H1 + ht * P, P)],
                                           xrt[u % 2][:, at:at + UROWS], start=n == 0 and ht % 2 == 0, stop=n == 5,
                                           skip_group_check=True)
                            n += 1
                    if ht % 2:
                        mm.then_inc(u_up, 1)

            def unit_down(i, u, e):
                pe.wait_ge(u_lo, 2 * i + 2)
                if not (isinstance(i, int) and i < 2):
                    pe.wait_ge(u_y, i - 1)
                n = 0
                for ht in range(HT):
                    for hp, wp in ((0, 0), (0, 1), (1, 0)):
                        for h in range(HALVES):
                            at = hp * H + ht * UROWS + h * P
                            mm = pe.matmul(ps[:, 6 + u % 2, h * D:(h + 1) * D], h1r[u % 2][:, at:at + P],
                                           big16[:, ds(e * EXP + 2048 + wp * 1024 + ht * D, D)],
                                           start=n == 0, stop=n >= 22, skip_group_check=True)
                            n += 1
                mm.then_inc(u_down, 1)

            unit_transpose(0, 0, 0)
            unit_transpose(1, 0, 1)
            unit_up(0, 0, expert(0))

            def units(g, last):
                now = expert(RING * g)
                count = LAST if last else RING
                for u in range(count):
                    i = RING * g + u
                    if not (last and u + 2 >= count):
                        unit_transpose(i + 2, g + (u + 2) // RING, (u + 2) % RING)
                    if not (last and u + 1 >= count):
                        then = expert(i + 1)
                        unit_up(i + 1, (u + 1) % RING, then)
                    unit_down(i, u, now)
                    now = then

            units(0, False)
            with pe.Fori(1, TURNS - 1) as g:
                units(g, False)
            units(TURNS - 1, True)

        @block.scalar
        def _(act):
            act.sem_inc(pair_free_a, 3)
            act.sem_inc(gelu, 4)
            act.sem_inc(row_copied, 2)

            def x_high(n, slot):
                act.wait_ge(x_tr, n)
                act.activation(xt[:, slot, 0, :], ps[:, 4 + slot, 0:KD * P], ACT.Copy).then_inc(xt_hi, 1)

            def lstm_step(t, u):
                act.wait_ge(ifg_done, t + 1)
                act.activation(gc[:, 0:6 * N], ps[:, u, 0:6 * N], ACT.Tanh, scale=1 / WS).then_inc(ifg_tanh, 1)
                act.wait_ge(o_done, t + 1)
                act.activation(og, ps[:, 2 + u, 0:2 * N], ACT.Tanh, scale=1 / WS).then_inc(o_tanh, 1)
                act.wait_ge(c_done, t + 1)
                act.activation(tc, cell, ACT.Tanh, scale=0.5).then_inc(c_tanh, 1)

            def lstm_turn(i, w, last):
                for r in range(4):
                    lstm_step(4 * i + r, r % 2)
                    if r == 0:
                        x_high(2 * i + 2, 1)
                    if r == 2 and not last:
                        x_high(2 * i + 3, 0)
                if w is not None:
                    act.wait_ge(w_tr, w + 1)
                    act.activation(wt_h[:, ds(2 * w, 2), :], ps[:, 6, :].rearrange("p (q c) -> p q c", q=2), ACT.Copy,
                                   scale=WS).then_inc(wt_hi_done, 1)

            act.wait_ge(d_wx, 16)
            for i, (hi, lo, raw, scale) in enumerate(w0_parts()):
                if i == 2:
                    act.wait_ge(d_wh, 16)
                act.activation(hi, raw, ACT.Copy, scale=scale).then_inc(w0_hi, 1)
                if i == 1:
                    x_high(1, 0)
            lstm_turn(0, None, False)
            with act.Fori(1, 1 + PIECES // 2) as i:
                lstm_turn(i, i - 1, False)
            with act.Fori(1 + PIECES // 2, T // 4 - 1) as i:
                lstm_turn(i, None, False)
            lstm_turn(T // 4 - 1, None, True)

            act.wait_ge(m_step, 2)
            for c in range(8):
                if c >= 2:
                    act.wait_ge(xq_lo, c - 1)
                act.activation(qb[c % 2], hs[:, c * BLOCK:(c + 1) * BLOCK], ACT.Copy, scale=col(C_IH)).then_inc(xq_int, 1)

            def pair(it):
                return ps[:, 2 * (it % 3):2 * (it % 3) + 2, :].rearrange("p b c -> p (b c)")

            def blk(p):
                return big[:, ds(p * BLOCK, BLOCK)]

            act.wait_ge(m_step, 4)
            act.wait_ge(xq_lo, 8)
            act.wait_ge(prep_v, PREP1)
            with act.Fori(0, CH) as cc:
                for it in range(IT):
                    act.wait_ge(pair_done, IT * cc + it + 1)
                    act.activation(blk(IT * cc + it), pair(it), ACT.Copy, scale=col(C_U)).then_inc(pair_free_a, 1)
            act.wait_ge(m_step, 9)
            act.wait_ge(pair_free_a, 3 + BLOCKS)
            with act.Fori(0, CH) as cc:
                for it in range(IT):
                    p = IT * cc + it
                    act.wait_ge(gated, p + 1)
                    act.activation(qb[it % 2], blk(p), ACT.Copy, scale=col(C_IG)).then_inc(gate_q, 1)
                    act.wait_ge(m_step, 8)
                    act.wait_ge(gate_q, p + 1)
                    act.activation(blk(p), qb[it % 2], ACT.Tanh, scale=col(C_SGH)).then_inc(gate_t, 1)
                    act.wait_ge(m_step, 8)
                    act.wait_ge(gate_t, p + 1)
                    act.activation(sq[it % 2], blk(p), ACT.Copy, bias=32768.0, scale=32768.0).then_inc(gate_s, 1)
            act.wait_ge(m_step, 18)
            with act.Fori(0, CH) as cc:
                for it in range(IT):
                    p = IT * cc + it
                    act.wait_ge(pair_done, 2 * BLOCKS + p + 1)
                    act.wait_ge(prod, p + 1)
                    act.activation(qb[it % 2], pair(it), ACT.Copy, scale=col(C_FU)).then_inc(pair_free_a, 1)
                    act.activation(tmp_i[:, (2 + it % 2) * BLOCK:(3 + it % 2) * BLOCK], blk(p), ACT.Copy,
                                   scale=col(C_F2)).then_inc(gated_q, 1)

            act.wait_ge(m_step, 23)

            def o_integers(p, it, first):
                if not first:
                    act.wait_ge(o_lo, p - 1)
                act.activation(qb[it % 2], blk(p), ACT.Copy, scale=col(C_F3)).then_inc(o_int, 1)

            def x2_high(n, j, first):
                act.wait_ge(x2_new, n + 1)
                if not first:
                    act.wait_ge(x2_tr, n - 3)
                act.activation(x2h[j], xn[:, ds(2 * n, 2), :].rearrange("p t c -> p (t c)"), ACT.Copy).then_inc(x2_hi, 1)

            def x2_transposed(n, j):
                act.wait_ge(x2_tr, n + 1)
                for part_, v in enumerate((xh, xl)):
                    ins = act.activation(v[:, :].rearrange("p (k c) -> p k c", k=KD)[:, :, ds(2 * n * P, 2 * P)],
                                         ps[:, 4 + j % 2, :].bitcast(F16)[:, part_ * 512:(part_ + 1) * 512].rearrange(
                                             "p (k c) -> p k c", k=KD), ACT.Copy)
                ins.then_inc(x2_out, 1)

            def down_turn(cc, first, last):
                for j in range(4):
                    n = 4 * cc + j
                    x2_high(n, j, first)
                    if not last:
                        for it in NEXT[j]:
                            o_integers(IT * cc + IT + it, it, False)
                    if not first:
                        x2_transposed(n - 4, j)

            for p in range(2 * IT):
                o_integers(p, p % IT, p < 2)
            down_turn(0, True, True)
            with act.Fori(1, CH - 1) as cc:
                down_turn(cc, False, False)
            down_turn(CH - 1, False, True)
            act.wait_ge(b1_tr, 1)
            act.activation(b1_t[:, :], ps[:, 7, 0:SLOTS * HT], ACT.Copy).then_inc(b1_ready, 1)
            act.wait_ge(b1_ready, 1)

            def rnn_tanh(t):
                act.wait_ge(r_sum, t + 1)
                act.activation(hr[:, :], ps[:, 6, 0:SC], ACT.Tanh, scale=1 / WS).then_inc(r_tanh, 1)

            def expert_high(q, e, m):
                act.wait_ge(d_stage[m], 16 * q + 16)
                act.activation(big16[:, ds(e * EXP + m * 2048, 1024)], stage[:, m, :], ACT.Copy,
                               scale=WS).then_inc(e_hi, 1)

            for j in range(4):
                rnn_tanh(j)
                x2_transposed(PAIRS - 4 + j, j)
            for q in range(EARLY_FILLS):
                for m in range(2):
                    rnn_tanh(4 + 2 * q + m)
                    expert_high(q, (q + E) % SLOTS, m)

            def superchunk(c, with_rnn):
                def rnn(r):
                    if with_rnn:
                        rnn_tanh(SUPER_T * c + SUPER_T + r)

                def exponentials():
                    act.wait_ge(route_z, c + 1)
                    act.activation(ee[:, :, :], zz[:, :, :], ACT.Exp).then_inc(route_e, 1)

                def rows_out(b):
                    act.wait_ge(row_ps, 2 * c + b + 1)
                    act.wait_ge(d_rows, 16 + 128 * c)
                    act.activation(rows[:, 2 * b:2 * b + 2, 0:2 * D],
                                   ps[:, b, :].bitcast(F16).rearrange("p (t c) -> p t c", t=2),
                                   ACT.Copy).then_inc(row_copied, 1)

                if not with_rnn:
                    exponentials()
                for ht in range(HT):
                    act.wait_ge(up1, 4 * c + ht + 1)
                    act.wait_ge(split_lo, 4 * c + ht + 1)
                    if ht == 0:
                        act.wait_ge(added, 2 * c + 1)
                    for made in (hf[ht % 2], h1(0, ht)):
                        ins = act.activation(made, ps[:, ht, :], ACT.Gelu, scale=1 / WS,
                                             bias=b1_t[:, HT * E + ht:HT * E + ht + 1])
                    ins.then_inc(gelu, 1)
                    rnn(ht)
                    if ht == 1 and not with_rnn:
                        rows_out(0)
                        rows_out(1)
                if with_rnn:
                    exponentials()
                if with_rnn:
                    expert_high(c + EARLY_FILLS, c + EARLY_FILLS - 1, 0)
                rnn(4)
                for b in range(2):
                    if with_rnn:
                        rows_out(b)
                    rnn(5 + b)
                if with_rnn:
                    expert_high(c + EARLY_FILLS, c + EARLY_FILLS - 1, 1)
                rnn(7)

            act.wait_ge(x2_out, PAIRS)
            with act.Fori(0, SUPERS - 1) as c:
                superchunk(c, True)
            superchunk(SUPERS - 1, False)

            act.wait_ge(table, TABLE_STEPS)
            act.wait_ge(split_lo, 2 + 4 * SUPERS)

            def unit_xt(i, u):
                act.wait_ge(u_tr, i + 1)
                if not (isinstance(i, int) and i < 2):
                    act.wait_ge(u_up, 2 * i - 2)
                act.activation(xrt[u % 2], ps[:, 4 + u % 2, :].bitcast(F16), ACT.Copy).then_inc(u_xt, 1)

            def unit_gelu(i, u):
                e = act.value_load(unit_i[0:1, 0, ds(i, 1)], min_val=0, max_val=E)
                for b in range(2):
                    act.wait_ge(u_up, 2 * i + b + 1)
                    if not (isinstance(i, int) and i < 2):
                        act.wait_ge(u_lo, 2 * i - 3 + b)
                    for ht in (2 * b, 2 * b + 1):
                        ins = act.activation(hfr[u % 2][:, ht * UROWS:(ht + 1) * UROWS],
                                             ps[:, 2 * (u % 2) + b, (ht % 2) * UROWS:(ht % 2 + 1) * UROWS], ACT.Gelu,
                                             scale=1 / WS, bias=b1_t[:, ds(HT * e + ht, 1)])
                    ins.then_inc(u_gelu, 1)

            unit_xt(0, 0)
            unit_xt(1, 1)
            unit_gelu(0, 0)

            def units(g, last):
                count = LAST if last else RING
                for u in range(count):
                    i = RING * g + u
                    if not (last and u + 2 >= count):
                        unit_xt(i + 2, (u + 2) % RING)
                    if not (last and u + 1 >= count):
                        unit_gelu(i + 1, (u + 1) % RING)

            units(0, False)
            with act.Fori(1, TURNS - 1) as g:
                units(g, False)
            units(TURNS - 1, True)

        @block.vector
        def _(dve):
            dve.sem_inc(pair_free_v, 3)
            dve.sem_inc(gated, 2)
            dve.sem_inc(prod, 2)
            dve.sem_inc(split_lo, 2)
            dve.sem_inc(added, 1)
            dve.sem_inc(w9t_done, 1)
            n_prep = 0

            def prep(ins):
                nonlocal n_prep
                n_prep += 1
                ins.then_inc(prep_v, 1)

            def split(hi, lo, src, scale):
                prep(dve.tensor_scalar(hi, src, scale, None, ALU.mult))
                dve.wait_ge(prep_v, n_prep)
                prep(dve.scalar_tensor_tensor(out=lo, in0=src, scalar=scale, in1=hi, op0=ALU.mult, op1=ALU.subtract))

            prep(dve.memset(cell, 0.0))
            dve.wait_ge(const_step, 2)

            def selector(sel, neg, slots, scales):
                low, high = ident[0:2 * slots, 0:slots], ident[0:2 * slots, slots:2 * slots]
                v = sel[:, :].rearrange("q (s n) -> q s n", n=N)
                prep(dve.tensor_tensor(v, low.unsqueeze(2).broadcast_to([2 * slots, slots, N]),
                                       high.unsqueeze(2).broadcast_to([2 * slots, slots, N]), ALU.add))
                prep(dve.tensor_reduce(neg[:, :], high, AX.X, ALU.add))
                dve.wait_ge(prep_v, n_prep)
                prep(dve.tensor_scalar(neg[:, :], neg[:, :], -1.0, None, ALU.mult))
                for s0, s1, f in scales:
                    prep(dve.tensor_scalar(sel[:, s0 * N:s1 * N], sel[:, s0 * N:s1 * N], f, None, ALU.mult))

            selector(sel0, nlow0, BIAS_SLOTS0, ((0, 4, WS / 2), (4, 6, WS), (6, 8, WS / 2)))
            selector(sel1, nlow1, BIAS_SLOTS1, ((0, BIAS_SLOTS1, WS),))
            dve.wait_ge(cond_t, 1)
            c0 = ps[:, 6, 0:SC]
            dve.tensor_scalar(hb[:, 0, 0, :], c0, 2.0, None, ALU.mult).then_inc(h_hi, 1)
            dve.wait_ge(h_hi, 1)
            dve.scalar_tensor_tensor(out=hb[:, 0, 1, :], in0=c0, scalar=2.0, in1=hb[:, 0, 0, :],
                                     op0=ALU.mult, op1=ALU.subtract).then_inc(h_lo, 1)

            def x_low(n, slot):
                dve.wait_ge(xt_hi, n)
                dve.tensor_tensor(xt[:, slot, 1, :], ps[:, 4 + slot, 0:KD * P], xt[:, slot, 0, :],
                                  ALU.subtract).then_inc(xt_lo, 1)

            split(r0[:, 0, :], r0[:, 1, :], c0, 1.0)

            def bias(bh, br, raw, neg):
                prep(dve.tensor_copy(bh[:, :], raw[:, :]))
                dve.wait_ge(prep_v, n_prep)
                prep(dve.scalar_tensor_tensor(out=br[:, :], in0=bh[:, :], scalar=neg[:, 0:1], in1=raw[:, :],
                                              op0=ALU.mult, op1=ALU.add))

            for i, (hi, lo, raw, scale) in enumerate(w0_parts()):
                dve.wait_ge(w0_hi, i + 1)
                prep(dve.scalar_tensor_tensor(out=lo, in0=raw, scalar=scale, in1=hi, op0=ALU.mult, op1=ALU.subtract))
                if i == 1:
                    dve.wait_ge(d_b, 16 * 8)
                    dve.wait_ge(prep_v, 10)
                    x_low(1, 0)
                    bias(bhi0, brow0, braw0, nlow0)
                    assert n_prep == PREP_X
            bias(bhi1, brow1, braw1, nlow1)
            assert n_prep == PREP0

            def lstm_step(t, u):
                dve.wait_ge(ifg_tanh, t + 1)
                dve.scalar_tensor_tensor(out=igfc, in0=gc[:, 0:2 * SC], scalar=1.0, in1=gc[:, 2 * SC:4 * SC],
                                         op0=ALU.add, op1=ALU.mult).then_inc(igfc_done, 1)
                dve.wait_ge(igfc_done, t + 1)
                dve.scalar_tensor_tensor(out=cell, in0=igfc[:, SC:2 * SC], scalar=0.5, in1=igfc[:, 0:SC],
                                         op0=ALU.mult, op1=ALU.add).then_inc(c_done, 1)
                dve.wait_ge(c_tanh, t + 1)
                dve.wait_ge(o_tanh, t + 1)
                hi, h = hb[:, 1 - u, 0, :], hs[:, ds(t * SC, SC)]
                dve.scalar_tensor_tensor(out=hi, in0=og, scalar=1.0, in1=tc,
                                         op0=ALU.add, op1=ALU.mult).then_inc(h_hi, 1)
                dve.scalar_tensor_tensor(out=h, in0=og, scalar=1.0, in1=tc,
                                         op0=ALU.add, op1=ALU.mult).then_inc(hs_done, 1)
                dve.wait_ge(hs_done, t + 1)
                dve.wait_ge(h_hi, t + 2)
                dve.tensor_tensor(hb[:, 1 - u, 1, :], h, hi, ALU.subtract).then_inc(h_lo, 1)
                dve.tensor_reduce(maxes[:, 0, ds(t, 1)], h, AX.X, ALU.max, apply_absolute_value=True).then_inc(hmax_done, 1)

            def lstm_turn(i, w, last):
                if w is not None:
                    raw = wn[:, ds(2 * w, 2), :].rearrange("p q (b c) -> p (q b) c", c=WBLK)
                s16, i16 = blk_s[:, 0, :], blk_s[:, 1, :]
                for r in range(4):
                    lstm_step(4 * i + r, r % 2)
                    if r == 0:
                        x_low(2 * i + 2, 1)
                        if w is not None:
                            dve.tensor_reduce(blk_s[:, 2, :], raw, AX.X, ALU.max,
                                              apply_absolute_value=True).then_inc(wq_step, 1)
                            dve.wait_ge(wq_step, 5 * w + 1)
                            dve.tensor_scalar(s16, blk_s[:, 2, :], 1 / 7.0, TINY, ALU.mult, ALU.max).then_inc(wq_step, 1)
                            dve.wait_ge(wq_step, 5 * w + 2)
                            dve.reciprocal(i16, s16).then_inc(wq_step, 1)
                    if r == 1 and w is not None:
                        dve.wait_ge(wq_step, 5 * w + 3)
                        dve.tensor_tensor(w16.rearrange("p (b c) -> p b c", c=WBLK), raw,
                                          i16.unsqueeze(2).broadcast_to([P, 16, WBLK]), ALU.mult).then_inc(wq_step, 1)
                    if r == 2:
                        if not last:
                            x_low(2 * i + 3, 0)
                        if w is not None:
                            dve.wait_ge(wq_step, 5 * w + 4)
                            dve.tensor_tensor(wd.rearrange("p (b c) -> p b c", c=WBLK),
                                              w16.rearrange("p (b c) -> p b c", c=WBLK),
                                              s16.unsqueeze(2).broadcast_to([P, 16, WBLK]), ALU.mult).then_inc(wq_step, 1)
                if w is not None:
                    dve.wait_ge(wt_hi_done, w + 1)
                    dve.scalar_tensor_tensor(out=wt_l[:, ds(2 * w, 2), :],
                                             in0=ps[:, 6, :].rearrange("p (q c) -> p q c", q=2), scalar=WS,
                                             in1=wt_h[:, ds(2 * w, 2), :], op0=ALU.mult,
                                             op1=ALU.subtract).then_inc(wt_lo_done, 1)

            lstm_turn(0, None, False)
            dve.wait_ge(d_ffn, 48)
            with dve.Fori(1, 1 + PIECES // 2) as i:
                lstm_turn(i, i - 1, False)
            with dve.Fori(1 + PIECES // 2, T // 4 - 1) as i:
                lstm_turn(i, None, False)
            lstm_turn(T // 4 - 1, None, True)

            def greatest(n, row, cols):
                dve.tensor_reduce(colmax[:, n:n + 1], maxes[:, row, 0:cols], AX.X, ALU.max).then_inc(m_col, 1)
                dve.wait_ge(m_row, n + 1)
                dve.tensor_reduce(top[:, n:n + 1], ps[0:1, 7, 0:P], AX.X, ALU.max).then_inc(m_top, 1)
                dve.wait_ge(m_all, n + 1)
                return ps[:, 7, 256 + n:257 + n]

            n_step = 0

            def mstep(ins):
                nonlocal n_step
                n_step += 1
                ins.then_inc(m_step, 1)
                dve.wait_ge(m_step, n_step)

            dve.wait_ge(hmax_done, T)
            m = greatest(0, 0, T)
            mstep(dve.tensor_scalar(col(C_SH), m, 1 / QMAX, 2 * TINY, ALU.mult, ALU.max))
            mstep(dve.reciprocal(col(C_IH), col(C_SH)))
            mstep(dve.tensor_scalar(col(C_U), col(C_SH), 0.5 / WS, None, ALU.mult))
            mstep(dve.memset(col(C_R), 0.0))
            assert n_step == 4
            for c in range(8):
                dve.wait_ge(xq_int, c + 1)
                hi, lo = (v[:, :, 8 * c:8 * c + 8, :].rearrange("p k t n -> p t k n") for v in (xh_v, xl_v))
                q = qb[c % 2].rearrange("p (t k n) -> p t k n", k=KD, n=N)
                dve.tensor_copy(hi, q).then_inc(xq_hi, 1)
                dve.wait_ge(xq_hi, c + 1)
                dve.tensor_tensor(lo, q, hi, ALU.subtract).then_inc(xq_lo, 1)

            dve.wait_ge(d_rnn, 64)
            split(rx_h[:, :], rx_l[:, :], rx_raw, WS)
            split(rh_h[:, :], rh_l[:, :], rh_raw, WS)
            split(wr_h[:, :], wr_l[:, :], wr_raw[:, :], WS)
            assert n_prep == PREP1
            dve.wait_ge(d_moe_small, 16 * 8)
            prep(dve.tensor_copy(b2_hi[:, :], b2_raw[:, :]))
            prep(dve.tensor_reduce(nlow2[:, :], ident[0:3 * SLOTS, 2 * SLOTS:3 * SLOTS], AX.X, ALU.add))
            dve.wait_ge(prep_v, n_prep)
            prep(dve.tensor_scalar(nlow2[:, :], nlow2[:, :], -1.0, None, ALU.mult))
            dve.wait_ge(prep_v, n_prep)
            prep(dve.scalar_tensor_tensor(out=b2_x[:, :], in0=b2_hi[:, :], scalar=nlow2[:, 0:1], in1=b2_raw[:, :],
                                          op0=ALU.mult, op1=ALU.add))
            prep(dve.memset(w9[:, :, E:SLOTS], 1 / WS))

            def pair(it):
                return ps[:, 2 * (it % 3):2 * (it % 3) + 2, :].rearrange("p b c -> p (b c)")

            def blk(p):
                return big[:, ds(p * BLOCK, BLOCK)]

            def abs_max(out_, in_):
                return dve.tensor_reduce(out_, in_, AX.X, ALU.max, apply_absolute_value=True)

            with dve.Fori(0, CH) as cc:
                for it in range(IT):
                    dve.wait_ge(pair_free_a, 3 + IT * cc + it + 1)
                    abs_max(maxes[:, 1, ds(IT * cc + it, 1)], blk(IT * cc + it)).then_inc(gate_max, 1)
            dve.wait_ge(gate_max, BLOCKS)
            m = greatest(1, 1, BLOCKS)
            mstep(dve.tensor_scalar(col(C_T1), m, 1 / QMAX, None, ALU.mult))
            mstep(dve.tensor_scalar(col(C_SG), col(C_T1), TINY, None, ALU.max))
            mstep(dve.reciprocal(col(C_IG), col(C_SG)))
            mstep(dve.tensor_scalar(col(C_SGH), col(C_SG), 0.5, None, ALU.mult))
            mstep(dve.tensor_scalar(col(C_SG16), col(C_SG), 1 / 65536.0, None, ALU.mult))
            assert n_step == 9
            with dve.Fori(0, CH) as cc:
                for it in range(IT):
                    p = IT * cc + it
                    dve.wait_ge(pair_done, BLOCKS + p + 1)
                    abs_max(maxes[:, 2, ds(p, 1)], pair(it)).then_inc(pair_free_v, 1)
                    dve.wait_ge(gate_s, p + 1)
                    dve.tensor_tensor(blk(p), qb[it % 2], sq[it % 2], ALU.mult).then_inc(gated, 1)
                    dve.wait_ge(gated, p + 3)
                    abs_max(maxes[:, 3, ds(p, 1)], blk(p)).then_inc(gated_max, 1)
            dve.wait_ge(pair_free_v, 3 + BLOCKS)
            dve.wait_ge(gated_max, BLOCKS)
            m = greatest(2, 2, BLOCKS)
            mstep(dve.tensor_scalar(col(C_T1), m, col(C_U), 1 / QMAX, ALU.mult, ALU.mult))
            mstep(dve.tensor_scalar(col(C_SU), col(C_T1), TINY, None, ALU.max))
            mstep(dve.reciprocal(col(C_ISU), col(C_SU)))
            mstep(dve.tensor_scalar(col(C_FU), col(C_ISU), col(C_U), None, ALU.mult))
            m = greatest(3, 3, BLOCKS)
            mstep(dve.tensor_scalar(col(C_T2), m, col(C_SG16), 1 / QMAX, ALU.mult, ALU.mult))
            mstep(dve.tensor_scalar(col(C_S2), col(C_T2), TINY, None, ALU.max))
            mstep(dve.reciprocal(col(C_T3), col(C_S2)))
            mstep(dve.tensor_scalar(col(C_F2), col(C_T3), col(C_SG16), None, ALU.mult))
            mstep(dve.tensor_scalar(col(C_T4), col(C_S2), col(C_SU), None, ALU.mult))
            assert n_step == 18
            with dve.Fori(0, CH) as cc:
                for it in range(IT):
                    p = IT * cc + it
                    dve.wait_ge(gated_q, p + 1)
                    dve.wait_ge(pair_free_a, 3 + BLOCKS + p + 1)
                    dve.tensor_tensor(blk(p), qb[it % 2], tmp_i[:, (2 + it % 2) * BLOCK:(3 + it % 2) * BLOCK],
                                      ALU.mult).then_inc(prod, 1)
                    dve.wait_ge(prod, p + 3)
                    abs_max(maxes[:, 1, ds(p, 1)], blk(p)).then_inc(prod_max, 1)
            dve.wait_ge(prod_max, BLOCKS)
            m = greatest(4, 1, BLOCKS)
            mstep(dve.tensor_scalar(col(C_T1), m, col(C_T4), 1 / QMAX, ALU.mult, ALU.mult))
            mstep(dve.tensor_scalar(col(C_S3), col(C_T1), TINY, None, ALU.max))
            mstep(dve.reciprocal(col(C_T3), col(C_S3)))
            mstep(dve.tensor_scalar(col(C_F3), col(C_T3), col(C_T4), None, ALU.mult))
            mstep(dve.tensor_scalar(col(C_OUT), col(C_S3), 1 / WS, None, ALU.mult))
            assert n_step == 23

            def o_split(p, it):
                dve.wait_ge(o_int, p + 1)
                hi = big16[:, ds(p * 2 * BLOCK, BLOCK)]
                lo = big16[:, ds(p * 2 * BLOCK + BLOCK, BLOCK)]
                dve.tensor_copy(hi, qb[it % 2]).then_inc(o_hi, 1)
                dve.wait_ge(o_hi, p + 1)
                dve.tensor_tensor(lo, qb[it % 2], hi, ALU.subtract).then_inc(o_lo, 1)

            def down_turn(cc, first, last):
                for j in range(4):
                    n = 4 * cc + j
                    tiles = xn[:, ds(2 * n, 2), :].rearrange("p t c -> p (t c)")
                    dve.wait_ge(down, n + 1)
                    dve.scalar_tensor_tensor(out=tiles, in0=ps[:, j, :], scalar=col(C_OUT), in1=tiles,
                                             op0=ALU.mult, op1=ALU.add).then_inc(x2_new, 1)
                    dve.wait_ge(x2_hi, n + 1)
                    dve.tensor_tensor(x2l[j], tiles, x2h[j], ALU.subtract).then_inc(x2_lo, 1)
                    if not last:
                        for it in NEXT[j]:
                            o_split(IT * cc + IT + it, it)

            for p in range(2 * IT):
                o_split(p, p % IT)
            down_turn(0, True, True)
            with dve.Fori(1, CH - 1) as cc:
                down_turn(cc, False, False)
            down_turn(CH - 1, False, True)

            def rnn_split(t):
                dve.wait_ge(r_tanh, t + 1)
                hi, lo = (v[:, :, ds(t, 1), :].rearrange("p k a n -> p k (a n)") for v in (xh_v, xl_v))
                new = hr[:, :].rearrange("p (k n) -> p k n", k=KD)
                dve.tensor_copy(hi, new).then_inc(r_hi, 1)
                dve.wait_ge(r_hi, t + 1)
                dve.tensor_tensor(lo, new, hi, ALU.subtract).then_inc(r_lo, 1)

            def expert_low(q, e, m):
                dve.wait_ge(e_hi, 2 * q + m + 1)
                at = e * EXP + m * 2048
                dve.scalar_tensor_tensor(out=big16[:, ds(at + 1024, 1024)], in0=stage[:, m, :], scalar=WS,
                                         in1=big16[:, ds(at, 1024)], op0=ALU.mult,
                                         op1=ALU.subtract).then_inc(e_lo, 1)

            for j in range(4):
                rnn_split(j)
            for q in range(EARLY_FILLS):
                for m in range(2):
                    rnn_split(4 + 2 * q + m)
                    expert_low(q, (q + E) % SLOTS, m)

            dve.wait_ge(const_step, CONSTS)
            dve.wait_ge(d_const, 16)
            dve.tensor_copy(carry[:, 0, :], consts[:, K_BASE:K_BASE + E]).then_inc(carried, 1)

            def over_e(v):
                return v.unsqueeze(2).broadcast_to([P, 4, E])

            def superchunk(c, with_rnn):
                k = 0

                def link(ins):
                    nonlocal k
                    k += 1
                    ins.then_inc(route_step, 1)
                    dve.wait_ge(route_step, ROUTE_STEPS * c + k)

                def rnn(r):
                    if with_rnn:
                        rnn_split(SUPER_T * c + SUPER_T + r)

                def hidden(ht):
                    dve.wait_ge(gelu, 4 + 4 * c + ht + 1)
                    dve.tensor_tensor(h1(1, ht), hf[ht % 2], h1(0, ht), ALU.subtract).then_inc(split_lo, 1)

                def weights():
                    dve.wait_ge(route_e, c + 1)
                    link(dve.tensor_reduce(mrow[:, 4:8], ee[:, :, :], AX.X, ALU.add))
                    link(dve.reciprocal(mrow[:, 8:12], mrow[:, 4:8]))
                    link(dve.tensor_scalar(mrow[:, 12:16], mrow[:, 8:12], 1 / WS, None, ALU.mult))
                    link(dve.tensor_tensor(ee[:, :, :], ee[:, :, :], over_e(mrow[:, 12:16]), ALU.mult))
                    link(dve.scalar_tensor_tensor(out=w9[:, :, 0:E], in0=rank[:, :, :], scalar=float(TOP_K), in1=ee[:, :, :],
                                                  op0=ALU.is_lt, op1=ALU.mult))
                    link(dve.tensor_scalar(w9x[:, :, 0:SLOTS], w9[:, :, :], WS * WS, None, ALU.mult))
                    dve.tensor_copy(w9x[:, :, 2 * SLOTS:3 * SLOTS], w9x[:, :, 0:SLOTS]).then_inc(w9_done, 1)
                    dve.scalar_tensor_tensor(out=w9x[:, :, SLOTS:2 * SLOTS], in0=w9[:, :, :], scalar=WS * WS,
                                             in1=w9x[:, :, 0:SLOTS], op0=ALU.mult, op1=ALU.subtract).then_inc(w9_done, 1)
                    dve.wait_ge(d_rows, 16 + 128 * c)
                    dve.wait_ge(empty_made, 3)
                    dve.tensor_copy(rows32[:, :, W_AT:W_AT + SLOTS], w9[:, :, :]).then_inc(row_tail, 1)
                    dve.tensor_tensor(rows32[:, :, DST_AT:DST_AT + E], rank[:, :, :],
                                      over_e(consts[:, ds(K_DST + 4 * c, 4)]), ALU.add).then_inc(row_tail, 1)

                lv = ps[:, 7, 0:4 * E].rearrange("p (t e) -> p t e", e=E)
                dve.wait_ge(route, c + 1)
                link(dve.scalar_tensor_tensor(out=lg[:, :, :], in0=lv, scalar=1 / WS,
                                              in1=rb_all[:, :].unsqueeze(1).broadcast_to([P, 4, E]),
                                              op0=ALU.mult, op1=ALU.add))
                link(dve.tensor_reduce(mrow[:, 0:4], lg[:, :, :], AX.X, ALU.max))
                dve.tensor_tensor(zz[:, :, :], lg[:, :, :], over_e(mrow[:, 0:4]), ALU.subtract).then_inc(route_z, 1)
                mine = lg[:, :, :].unsqueeze(3).broadcast_to([P, 4, E, E])
                other = lg[:, :, :].unsqueeze(2).broadcast_to([P, 4, E, E])
                link(dve.tensor_tensor(cmp_a[:, :, :, :], other, mine, ALU.is_ge))
                link(dve.tensor_tensor(cmp_b[:, :, :, :], other, mine, ALU.is_gt))
                if with_rnn:
                    hidden(0)
                rnn(0)
                for tt in range(4):
                    last = dve.tensor_tensor(cmp_a[:, tt, :, :], cmp_a[:, tt, :, :], before[:, :, :], ALU.mult)
                link(last)
                link(dve.tensor_tensor(cmp_b[:, :, :, :], cmp_b[:, :, :, :], cmp_a[:, :, :, :], ALU.max))
                if with_rnn:
                    hidden(1)
                rnn(1)
                link(dve.tensor_reduce(rank[:, :, :], cmp_b[:, :, :, :], AX.X, ALU.add))
                dve.tensor_scalar(chosen[:, :, :], rank[:, :, :], float(TOP_K), None, ALU.is_lt).then_inc(route_c, 1)
                if not with_rnn:
                    weights()
                if with_rnn:
                    hidden(2)
                rnn(2)
                if with_rnn:
                    hidden(3)
                rnn(3)
                dve.wait_ge(placed_sum, c + 1)
                dve.wait_ge(carried, c + 1)
                link(dve.tensor_tensor(place[:, :, :], ps[:, 7, 64:64 + 4 * E].rearrange("p (t e) -> p t e", e=E),
                                       carry[:, 0, :].unsqueeze(1).broadcast_to([P, 4, E]), ALU.add))
                link(dve.tensor_tensor(carry[:, 1, :], ps[:, 7, 64 + 4 * E:64 + 5 * E], carry[:, 0, :], ALU.add))
                dve.tensor_copy(carry[:, 0, :], carry[:, 1, :]).then_inc(carried, 1)
                link(dve.scalar_tensor_tensor(out=place_j[:, :, 0, :], in0=rank[:, :, :], scalar=0.0, in1=place[:, :, :],
                                              op0=ALU.is_equal, op1=ALU.mult))
                link(dve.scalar_tensor_tensor(out=place_j[:, :, 1, :], in0=rank[:, :, :], scalar=1.0, in1=place[:, :, :],
                                              op0=ALU.is_equal, op1=ALU.mult))
                link(dve.tensor_reduce(place[:, :, 0:TOP_K], place_j[:, :, :, :], AX.X, ALU.add))
                dve.wait_ge(d_rows, 16 + 128 * c)
                dve.tensor_copy(row_j[:, :, :], place[:, :, 0:TOP_K]).then_inc(row_idx, 1)
                if not with_rnn:
                    for ht in range(HT):
                        hidden(ht)
                    unit_table()
                rnn(4)
                if with_rnn:
                    weights()
                rnn(5)
                dve.wait_ge(w9_tr, c + 1)
                dve.tensor_copy(w9t, ps[0:3 * SLOTS, 7, 256:512].bitcast(F16)).then_inc(w9t_done, 1)
                if with_rnn:
                    expert_low(c + EARLY_FILLS, c + EARLY_FILLS - 1, 0)

                def add_shared(b):
                    dve.wait_ge(down1, 2 * c + b + 1)
                    tiles = xn[:, ds(4 * c + 2 * b, 2), :].rearrange("p t c -> p (t c)")
                    dve.scalar_tensor_tensor(out=tiles, in0=ps[:, 4 + b, :], scalar=1 / WS, in1=tiles,
                                             op0=ALU.mult, op1=ALU.add).then_inc(added, 1)

                rnn(6)
                add_shared(0)
                rnn(7)
                if with_rnn:
                    expert_low(c + EARLY_FILLS, c + EARLY_FILLS - 1, 1)
                add_shared(1)
                k += 1
                dve.sem_inc(route_step, 1)
                assert k == ROUTE_STEPS, k

            def unit_table():
                k = 0

                def row(ins):
                    nonlocal k
                    k += 1
                    ins.then_inc(table, 1)
                    dve.wait_ge(table, k)

                cnt, till, lim, over, first, end = (count[:, i, :] for i in range(6))
                unit = consts[:, K_UNIT:K_UNIT + UNITS]
                dve.wait_ge(carried, SUPERS + 1)
                row(dve.tensor_tensor(cnt, carry[:, 0, :], consts[:, K_BASE:K_BASE + E], ALU.subtract))
                row(dve.tensor_scalar(tiles_i[:, :], cnt, 1 / UROWS, (UROWS / 2 - 0.5) / UROWS, ALU.mult, ALU.add))
                row(dve.tensor_copy(first, tiles_i[:, :]))
                row(dve.tensor_scalar(till, first, 1.0, None, ALU.max))
                row(dve.scalar_tensor_tensor(out=lim, in0=till, scalar=float(UROWS), in1=cnt, op0=ALU.mult, op1=ALU.subtract))
                for h in range(HALVES):
                    lane = consts[:, K_LANE + h:K_LANE + h + 1]
                    row(dve.tensor_scalar(over, lim, lane, NOWHERE, ALU.is_le, ALU.mult))
                    dve.scalar_tensor_tensor(out=fill_i[:, h * E:(h + 1) * E], in0=carry[:, 0, :], scalar=lane, in1=over,
                                             op0=ALU.add, op1=ALU.add).then_inc(filled, 1)
                    dve.wait_ge(filled, h + 1)
                square = cmp_a[:, 0, :, :]
                row(dve.tensor_tensor(square, before[:, :, :], till.unsqueeze(1).broadcast_to([P, E, E]), ALU.mult))
                row(dve.tensor_reduce(first, square, AX.X, ALU.add))
                row(dve.tensor_tensor(end, first, till, ALU.add))
                row(dve.tensor_tensor(reached, unit.unsqueeze(2).broadcast_to([P, UNITS, E]),
                                      end.unsqueeze(1).broadcast_to([P, UNITS, E]), ALU.is_ge))
                row(dve.tensor_reduce(unit_f[:, 0, :], reached, AX.X, ALU.add))
                row(dve.tensor_tensor(reached, reached, till.unsqueeze(1).broadcast_to([P, UNITS, E]), ALU.mult))
                row(dve.tensor_reduce(unit_f[:, 1, :], reached, AX.X, ALU.add))
                row(dve.tensor_copy(unit_i[:, 0, :], unit_f[:, 0, :]))
                row(dve.scalar_tensor_tensor(out=unit_f[:, 0, :], in0=unit_f[:, 0, :], scalar=REGION / UROWS, in1=unit,
                                             op0=ALU.mult, op1=ALU.add))
                row(dve.tensor_tensor(unit_i[:, 1, :], unit_f[:, 0, :], unit_f[:, 1, :], ALU.subtract))
                assert k == TABLE_STEPS, k

            dve.wait_ge(x2_out, PAIRS)
            with dve.Fori(0, SUPERS - 1) as c:
                superchunk(c, True)
            superchunk(SUPERS - 1, False)

            def unit_split(i, u):
                for b in range(2):
                    n = 2 * i + b
                    cols = slice(b * 512, (b + 1) * 512)
                    dve.wait_ge(u_gelu, n + 1)
                    if b == 0 and not (isinstance(i, int) and i < 2):
                        dve.wait_ge(u_down, i - 1)
                    hi, lo = h1r[u % 2][:, 0:H][:, cols], h1r[u % 2][:, H:2 * H][:, cols]
                    dve.tensor_copy(hi, hfr[u % 2][:, cols]).then_inc(u_hi, 1)
                    dve.wait_ge(u_hi, n + 1)
                    dve.tensor_tensor(lo, hfr[u % 2][:, cols], hi, ALU.subtract).then_inc(u_lo, 1)

            def unit_result(i, g, u):
                e = dve.value_load(unit_i[0:1, 0, ds(i, 1)], min_val=0, max_val=E)
                dve.wait_ge(u_down, i + 1)
                if not (isinstance(g, int) and g == 0):
                    dve.wait_ge(u_out[u], 16 * HALVES * g)
                for h in range(HALVES):
                    ins = dve.tensor_scalar(yr[u][:, h * D:(h + 1) * D], ps[:, 6 + u % 2, h * D:(h + 1) * D],
                                            xr32[u][:, h, ds(W_AT + e, 1)], None, ALU.mult)
                ins.then_inc(u_y, 1)
                dve.tensor_copy(dst_i[:, HALVES * u:HALVES * (u + 1)],
                                xr32[u][:, :, ds(DST_AT + e, 1)].rearrange("p h a -> p (h a)")).then_inc(u_dst, 1)

            unit_split(0, 0)

            def units(g, last):
                count = LAST if last else RING
                for u in range(count):
                    i = RING * g + u
                    if not (last and u + 1 >= count):
                        unit_split(i + 1, (u + 1) % RING)
                    unit_result(i, g, u)

            units(0, False)
            with dve.Fori(1, TURNS - 1) as g:
                units(g, False)
            units(TURNS - 1, True)

            for s in range(SUPERS):
                dve.wait_ge(d_super[s], 32)
                for j in range(TOP_K):
                    tiles = xn[:, 4 * s:4 * s + 4, :]
                    dve.tensor_tensor(tiles, tiles, pairs[:, s, :, j * D:(j + 1) * D], ALU.add).then_inc(summed, 1)
                    dve.wait_ge(summed, 2 * s + j + 1)


_INS = ['x', 'cond_1024', 'L0_cond_Wx', 'L0_cond_Wh', 'L0_cond_b', 'L0_ffn_w_gate', 'L0_ffn_w_up', 'L0_ffn_w_down',
        'L1_cond_Wx', 'L1_cond_Wh', 'L1_cond_b', 'L1_ffn_router_w', 'L1_ffn_router_b', 'L1_ffn_sw1', 'L1_ffn_sb1',
        'L1_ffn_sw2', 'L1_ffn_sb2', 'L1_ffn_rw1', 'L1_ffn_rb1', 'L1_ffn_rw2', 'L1_ffn_rb2']


def kernel(**inputs):
    import numpy as _np
    import concourse.bacc as _bacc
    from concourse import mybir as _mybir
    from concourse.bass_utils import run_bass_kernel_spmd as _run

    nc = _bacc.Bacc("TRN2", target_bir_lowering=False, num_devices=1)
    arrays, args = {}, {}
    for name in _INS:
        v = _np.ascontiguousarray(inputs[name])
        arrays[f"in_{name}"] = v
        args[name] = nc.dram_tensor(f"in_{name}", v.shape, _mybir.dt.from_np(v.dtype), kind="ExternalInput").ap()
    k = _np.zeros((P, K_COLS), _np.float32)
    lanes = _np.arange(P)
    k[:, K_DST:K_DST + TILES] = TOP_K * ((lanes % N) * T + lanes // N)[:, None] + 2 * TOP_K * _np.arange(TILES)
    k[:, K_LANE:K_LANE + HALVES] = lanes[:, None] + P * _np.arange(HALVES)
    k[:, K_BASE:K_BASE + E] = REGION * _np.arange(E)
    k[:, K_UNIT:] = _np.arange(UNITS)
    arrays["consts"] = k
    args["consts"] = nc.dram_tensor("consts", k.shape, F32, kind="ExternalInput").ap()
    rows = nc.dram_tensor("rows", (E * REGION + DUMMY * UROWS, ROW), I16, kind="Internal").ap()
    pairs = nc.dram_tensor("pairs", (TOP_K * T * N, D), F32, kind="Internal").ap()
    out = nc.dram_tensor("out_0", (N, T, D), F32, kind="ExternalOutput").ap()
    mixed_layers(nc, args, rows, pairs, out)
    r = _run(nc, [arrays], core_ids=[0])
    return r.results[0]["out_0"]
```
